# Optimizing a Trainium2 kernel written in Bass

```python
import numpy as np
import jax
import jax.numpy as jnp

def _softmax(x, axis=-1):
    return jax.nn.softmax(x, axis=axis)

def _gelu(x):
    return jax.nn.gelu(x, approximate=True)

def _silu(x):
    return jax.nn.silu(x)

def _sigmoid(x):
    return jax.nn.sigmoid(x)

def _layernorm(x, axis=-1, eps=1e-05):
    m = jnp.mean(x, axis=axis, keepdims=True)
    v = jnp.var(x, axis=axis, keepdims=True)
    return (x - m) / jnp.sqrt(v + eps)

def _scatter_add(tgt, idx, src, axis=0):
    return tgt.at[idx].add(src)

def _segment_sum(src, seg, n):
    return jax.ops.segment_sum(src, seg, n)
kernel_name = 'mk_prb_d2_jaxref_r8_048350'

def setup_inputs(seed: int=0):
    np.random.seed(seed)
    _w = jnp.asarray

    def _L0_attn_setup():
        import jax, jax.numpy as jnp
        import numpy as np
        HIDDEN = 256
        NUM_HEADS = 16
        HEAD_DIM = 128
        WINDOW_SIZE = 64
        NUM_GLOBAL = 16
        SCALING = HEAD_DIM ** (-0.5)

        def _sliding_mask(q_len: int, kv_len: int) -> jnp.ndarray:
            q_pos = jnp.arange(q_len)[:, None]
            kv_pos = jnp.arange(kv_len)[None, :]
            half_window = WINDOW_SIZE // 2
            local = jnp.abs(q_pos - kv_pos) < half_window
            glob = (q_pos < NUM_GLOBAL) | (kv_pos < NUM_GLOBAL)
            mask = local | glob
            return jnp.where(mask, 0.0, -jnp.inf).astype(jnp.float32)
        key = jax.random.key(seed)
        ks = jax.random.split(key, 5)
        std = HIDDEN ** (-0.5)
        hidden_states = jax.random.normal(ks[0], (1, 512, HIDDEN), dtype=jnp.float32)
        Wq = jax.random.normal(ks[1], (HIDDEN, NUM_HEADS * HEAD_DIM), dtype=jnp.float32) * std
        Wk = jax.random.normal(ks[2], (HIDDEN, NUM_HEADS * HEAD_DIM), dtype=jnp.float32) * std
        Wv = jax.random.normal(ks[3], (HIDDEN, NUM_HEADS * HEAD_DIM), dtype=jnp.float32) * std
        Wo = jax.random.normal(ks[4], (NUM_HEADS * HEAD_DIM, HIDDEN), dtype=jnp.float32) * std
        return {'hidden_states': hidden_states, 'Wq': Wq, 'Wk': Wk, 'Wv': Wv, 'Wo': Wo}
    _L0_attn_in = _L0_attn_setup()

    def _L0_ffn_setup():
        import jax, jax.numpy as jnp
        import numpy as np
        ALPHA = 1.702
        LIMIT = 7.0
        TOP_K = 4
        B, S, H = (1, 128, 256)
        E, D = (16, 256)
        key = jax.random.key(seed)
        ks = jax.random.split(key, 7)
        s = 0.02
        return {'hidden_states': jax.random.normal(ks[0], (B, S, H), dtype=jnp.float32), 'router_weight': jax.random.normal(ks[1], (E, H), dtype=jnp.float32) * s, 'router_bias': jax.random.normal(ks[2], (E,), dtype=jnp.float32) * s, 'gate_up_proj': jax.random.normal(ks[3], (E, H, 2 * D), dtype=jnp.float32) * s, 'gate_up_proj_bias': jax.random.normal(ks[4], (E, 2 * D), dtype=jnp.float32) * s, 'down_proj': jax.random.normal(ks[5], (E, D, H), dtype=jnp.float32) * s, 'down_proj_bias': jax.random.normal(ks[6], (E, H), dtype=jnp.float32) * s}
    _L0_ffn_in = _L0_ffn_setup()

    def _L1_attn_setup():
        import jax, jax.numpy as jnp
        import numpy as np
        D = 256
        B = 8
        T = 256

        def _reference_tuple_inner(x, Wk, Wv, Wr, time_decay):
            shifted = jnp.pad(x[:, :-1], ((0, 0), (1, 0), (0, 0)))
            k = jnp.einsum('btd,ed->bte', shifted, Wk)
            v = jnp.einsum('btd,ed->bte', shifted, Wv)
            r = jnp.einsum('btd,ed->bte', x, Wr)
            w = jnp.exp(-jnp.exp(time_decay))
            ek = jnp.exp(k)
            a = ek * v
            a_t = jnp.moveaxis(a, 1, 0)
            b_t = jnp.moveaxis(ek, 1, 0)

            def step(carry, inp):
                num, den = carry
                at, bt = inp
                num = w * num + at
                den = w * den + bt
                return ((num, den), num / (den + 1e-08))
            init = (jnp.zeros((x.shape[0], D), x.dtype), jnp.zeros((x.shape[0], D), x.dtype))
            _, wkv_t = jax.lax.scan(step, init, (a_t, b_t))
            wkv = jnp.moveaxis(wkv_t, 0, 1)
            return (r * wkv, shifted[:, -1])
        key = jax.random.key(seed)
        k0, k1, k2, k3, k4 = jax.random.split(key, 5)
        s = 1.0 / np.sqrt(D)
        return {'x': jax.random.normal(k0, (B, T, D), jnp.float32), 'Wk': jax.random.normal(k1, (D, D), jnp.float32) * s, 'Wv': jax.random.normal(k2, (D, D), jnp.float32) * s, 'Wr': jax.random.normal(k3, (D, D), jnp.float32) * s, 'time_decay': jax.random.normal(k4, (D,), jnp.float32) * 0.5}
    _L1_attn_in = _L1_attn_setup()

    def _L1_ffn_setup():
        import jax, jax.numpy as jnp
        import numpy as np
        B, S, H = (1, 256, 256)
        E, K, I = (16, 4, 176)
        IS = 352
        CAP = 128
        key = jax.random.key(seed)
        ks = jax.random.split(key, 8)
        sc = 0.02
        return {'hidden_states': jax.random.normal(ks[0], (B, S, H), jnp.float32), 'gate_w': jax.random.normal(ks[1], (E, H), jnp.float32) * sc, 'w_gate': jax.random.normal(ks[2], (E, H, I), jnp.float32) * sc, 'w_up': jax.random.normal(ks[3], (E, H, I), jnp.float32) * sc, 'w_down': jax.random.normal(ks[4], (E, I, H), jnp.float32) * sc, 'sw_gate': jax.random.normal(ks[5], (H, IS), jnp.float32) * sc, 'sw_up': jax.random.normal(ks[6], (H, IS), jnp.float32) * sc, 'sw_down': jax.random.normal(ks[7], (IS, H), jnp.float32) * sc}
    _L1_ffn_in = _L1_ffn_setup()
    _d = {'L0_attn_hidden_states': _L0_attn_in['hidden_states'], 'L0_attn_Wq': _L0_attn_in['Wq'], 'L0_attn_Wk': _L0_attn_in['Wk'], 'L0_attn_Wv': _L0_attn_in['Wv'], 'L0_attn_Wo': _L0_attn_in['Wo'], 'L0_ffn_router_weight': _L0_ffn_in['router_weight'], 'L0_ffn_router_bias': _L0_ffn_in['router_bias'], 'L0_ffn_gate_up_proj': _L0_ffn_in['gate_up_proj'], 'L0_ffn_gate_up_proj_bias': _L0_ffn_in['gate_up_proj_bias'], 'L0_ffn_down_proj': _L0_ffn_in['down_proj'], 'L0_ffn_down_proj_bias': _L0_ffn_in['down_proj_bias'], 'L1_attn_Wk': _L1_attn_in['Wk'], 'L1_attn_Wv': _L1_attn_in['Wv'], 'L1_attn_Wr': _L1_attn_in['Wr'], 'L1_attn_time_decay': _L1_attn_in['time_decay'], 'L1_ffn_gate_w': _L1_ffn_in['gate_w'], 'L1_ffn_w_gate': _L1_ffn_in['w_gate'], 'L1_ffn_w_up': _L1_ffn_in['w_up'], 'L1_ffn_w_down': _L1_ffn_in['w_down'], 'L1_ffn_sw_gate': _L1_ffn_in['sw_gate'], 'L1_ffn_sw_up': _L1_ffn_in['sw_up'], 'L1_ffn_sw_down': _L1_ffn_in['sw_down']}
    _x0 = _d['L0_attn_hidden_states']
    _d['L0_attn_hidden_states'] = jax.random.normal(jax.random.fold_in(jax.random.key(seed), 1), (1, 1024, 256), dtype=_x0.dtype)
    del _x0
    return _d

def reference(L0_attn_hidden_states, L0_attn_Wq, L0_attn_Wk, L0_attn_Wv, L0_attn_Wo, L0_ffn_router_weight, L0_ffn_router_bias, L0_ffn_gate_up_proj, L0_ffn_gate_up_proj_bias, L0_ffn_down_proj, L0_ffn_down_proj_bias, L1_attn_Wk, L1_attn_Wv, L1_attn_Wr, L1_attn_time_decay, L1_ffn_gate_w, L1_ffn_w_gate, L1_ffn_w_up, L1_ffn_w_down, L1_ffn_sw_gate, L1_ffn_sw_up, L1_ffn_sw_down):

    def _L0_attn_ref(hidden_states, Wq, Wk, Wv, Wo):
        import jax, jax.numpy as jnp
        import numpy as np
        HIDDEN = 256
        NUM_HEADS = 16
        HEAD_DIM = 128
        WINDOW_SIZE = 64
        NUM_GLOBAL = 16
        SCALING = HEAD_DIM ** (-0.5)

        def _sliding_mask(q_len: int, kv_len: int) -> jnp.ndarray:
            q_pos = jnp.arange(q_len)[:, None]
            kv_pos = jnp.arange(kv_len)[None, :]
            half_window = WINDOW_SIZE // 2
            local = jnp.abs(q_pos - kv_pos) < half_window
            glob = (q_pos < NUM_GLOBAL) | (kv_pos < NUM_GLOBAL)
            mask = local | glob
            return jnp.where(mask, 0.0, -jnp.inf).astype(jnp.float32)
        bsz, q_len, _ = hidden_states.shape
        q = (hidden_states @ Wq).reshape(bsz, q_len, NUM_HEADS, HEAD_DIM).transpose(0, 2, 1, 3)
        k = (hidden_states @ Wk).reshape(bsz, q_len, NUM_HEADS, HEAD_DIM).transpose(0, 2, 1, 3)
        v = (hidden_states @ Wv).reshape(bsz, q_len, NUM_HEADS, HEAD_DIM).transpose(0, 2, 1, 3)
        mask = _sliding_mask(q_len, q_len)[None, None]
        scores = jnp.einsum('bhqd,bhkd->bhqk', q, k) * SCALING + mask
        attn = jax.nn.softmax(scores.astype(jnp.float32), axis=-1).astype(q.dtype)
        out = jnp.einsum('bhqk,bhkd->bhqd', attn, v)
        out = out.transpose(0, 2, 1, 3).reshape(bsz, q_len, NUM_HEADS * HEAD_DIM)
        return out @ Wo

    def _L0_ffn_ref(hidden_states, router_weight, router_bias, gate_up_proj, gate_up_proj_bias, down_proj, down_proj_bias):
        import jax, jax.numpy as jnp
        import numpy as np
        ALPHA = 1.702
        LIMIT = 7.0
        TOP_K = 4
        B, S, H = (1, 128, 256)
        E, D = (16, 256)
        batch, seq, hdim = hidden_states.shape
        x = hidden_states.reshape(-1, hdim)
        T = x.shape[0]
        logits = x @ router_weight.T + router_bias
        top_val, top_idx = jax.lax.top_k(logits, TOP_K)
        top_val = jax.nn.softmax(top_val, axis=-1)
        router_scores = jnp.zeros_like(logits).at[jnp.arange(T)[:, None], top_idx].set(top_val)
        gate_up = jnp.einsum('th,ehd->etd', x, gate_up_proj) + gate_up_proj_bias[:, None, :]
        gate = gate_up[..., ::2]
        up = gate_up[..., 1::2]
        gate = jnp.minimum(gate, LIMIT)
        up = jnp.clip(up, -LIMIT, LIMIT)
        glu = gate * jax.nn.sigmoid(gate * ALPHA)
        out = jnp.einsum('etd,edh->eth', (up + 1.0) * glu, down_proj) + down_proj_bias[:, None, :]
        out = out * router_scores.T[:, :, None]
        out = out.sum(axis=0)
        return out.reshape(batch, seq, hdim)

    def _L1_attn_ref(x, Wk, Wv, Wr, time_decay):
        import jax, jax.numpy as jnp
        import numpy as np
        D = 256
        B = 8
        T = 256

        def _reference_tuple_inner(x, Wk, Wv, Wr, time_decay):
            shifted = jnp.pad(x[:, :-1], ((0, 0), (1, 0), (0, 0)))
            k = jnp.einsum('btd,ed->bte', shifted, Wk)
            v = jnp.einsum('btd,ed->bte', shifted, Wv)
            r = jnp.einsum('btd,ed->bte', x, Wr)
            w = jnp.exp(-jnp.exp(time_decay))
            ek = jnp.exp(k)
            a = ek * v
            a_t = jnp.moveaxis(a, 1, 0)
            b_t = jnp.moveaxis(ek, 1, 0)

            def step(carry, inp):
                num, den = carry
                at, bt = inp
                num = w * num + at
                den = w * den + bt
                return ((num, den), num / (den + 1e-08))
            init = (jnp.zeros((x.shape[0], D), x.dtype), jnp.zeros((x.shape[0], D), x.dtype))
            _, wkv_t = jax.lax.scan(step, init, (a_t, b_t))
            wkv = jnp.moveaxis(wkv_t, 0, 1)
            return (r * wkv, shifted[:, -1])
        return _reference_tuple_inner(x, Wk, Wv, Wr, time_decay)[0]

    def _L1_ffn_ref(hidden_states, gate_w, w_gate, w_up, w_down, sw_gate, sw_up, sw_down):
        import jax, jax.numpy as jnp
        import numpy as np
        B, S, H = (1, 256, 256)
        E, K, I = (16, 4, 176)
        IS = 352
        CAP = 128
        b, s, h = hidden_states.shape
        x = hidden_states.reshape(-1, h)
        T = x.shape[0]
        scores = jax.nn.softmax(x @ gate_w.T, axis=-1)
        topk_w, topk_i = jax.lax.top_k(scores, K)
        topk_w = topk_w / (topk_w.sum(-1, keepdims=True) + 1e-20)
        flat_i = topk_i.reshape(-1)
        flat_w = topk_w.reshape(-1)
        order = jnp.argsort(flat_i)
        se = flat_i[order]
        counts = jax.ops.segment_sum(jnp.ones_like(flat_i), flat_i, num_segments=E)
        starts = jnp.cumsum(counts) - counts
        rank = jnp.arange(T * K) - starts[se]
        tok = order // K
        slot = jnp.where(rank < CAP, rank, CAP)
        buf = jnp.full((E, CAP + 1), T, dtype=jnp.int32).at[se, slot].set(tok)[:, :CAP]
        wbuf = jnp.zeros((E, CAP + 1), x.dtype).at[se, slot].set(flat_w[order])[:, :CAP]
        xpad = jnp.concatenate([x, jnp.zeros((1, h), x.dtype)], axis=0)
        xg = xpad[buf]
        gact = jax.nn.silu(jnp.einsum('ech,ehi->eci', xg, w_gate))
        mid = gact * jnp.einsum('ech,ehi->eci', xg, w_up)
        eout = jnp.einsum('eci,eih->ech', mid, w_down) * wbuf[..., None]
        y = jnp.zeros((T + 1, h), x.dtype).at[buf.reshape(-1)].add(eout.reshape(-1, h))[:T]
        shared = jax.nn.silu(x @ sw_gate) * (x @ sw_up) @ sw_down
        return (y + shared).reshape(b, s, h)
    x = L0_attn_hidden_states
    xn = _layernorm(x, axis=-1)
    x = x + _L0_attn_ref(xn, L0_attn_Wq, L0_attn_Wk, L0_attn_Wv, L0_attn_Wo) + _L0_ffn_ref(xn, L0_ffn_router_weight, L0_ffn_router_bias, L0_ffn_gate_up_proj, L0_ffn_gate_up_proj_bias, L0_ffn_down_proj, L0_ffn_down_proj_bias)
    xn = _layernorm(x, axis=-1)
    x = x + _L1_attn_ref(xn, L1_attn_Wk, L1_attn_Wv, L1_attn_Wr, L1_attn_time_decay) + _L1_ffn_ref(xn, L1_ffn_gate_w, L1_ffn_w_gate, L1_ffn_w_up, L1_ffn_w_down, L1_ffn_sw_gate, L1_ffn_sw_up, L1_ffn_sw_down)
    return x

_drawn_inputs = setup_inputs


def setup_inputs(seed=0):
    import zlib

    import numpy as np

    out = dict(_drawn_inputs(seed))
    spreads = {}
    factors = {'L0_ffn_router_bias': 8.0,
     'L0_ffn_gate_up_proj_bias': 8.0,
     'L0_ffn_down_proj_bias': 5.317,
     'L1_ffn_gate_w': 8.0,
     'L1_ffn_w_gate': 8.0,
     'L1_ffn_w_up': 8.0,
     'L1_ffn_w_down': 8.0,
     'L1_ffn_sw_gate': 3.936,
     'L1_ffn_sw_up': 3.904,
     'L1_ffn_sw_down': 3.893}
    for name, (base, spread) in spreads.items():
        noise = np.random.default_rng([zlib.crc32(name.encode()), seed]).standard_normal(out[name].shape)
        drawn = base * np.exp(spread * noise) if base else spread * noise
        out[name] = jnp.asarray(drawn.astype(out[name].dtype))
    for name, factor in factors.items():
        out[name] = (out[name] * factor).astype(out[name].dtype)
    return out
```

```python
from contextlib import ExitStack

import concourse.bass as bass
from concourse import mybir

F32 = mybir.dt.float32
F32R = mybir.dt.float32r
BF16 = mybir.dt.bfloat16
U32 = mybir.dt.uint32
ALU = mybir.AluOpType
ACT = mybir.ActivationFunctionType
AX_X = mybir.AxisListType.X

P = 128
T, H = 1024, 256
NT, KC = T // P, H // P
HEADS, HD = 16, 128
PAIRS = HEADS // 2
WINDOW, GLOBALS = 64, 16
HALF = WINDOW // 2
SCALE = HD ** -0.5
WIN = P + WINDOW
KW = WIN + GLOBALS
VT = NT + 1
TP = VT * P
KB = WIN - P + GLOBALS
EXPERTS, FD, TOPK = 16, 256, 4
ALPHA, LIMIT = 1.702, 7.0
EPS = 1e-5
OUTSIDE = 1e30

UNITS = (["q0", "k0", "v0", "v1", "v2", "v3", "sg0", "gate00", "up00", "gate10", "up10", "q1", "k1",
          "down00", "down10", "sg1", "gate01", "up01", "gate11", "up11", "down01", "down11", "wo0", "wo1"])
NU = len(UNITS)
BY_ACT = [u for u in UNITS if u[:2] in ("sg", "up")]
BY_DVE = [u for u in UNITS if u not in BY_ACT]
NA, ND = len(BY_ACT), len(BY_DVE)
V_TILES = [(0, 3), (3, 5), (5, 7), (7, 9)]
NS = 2 * NT
NP = 2 * (NT + 1)
NW = 10

ID = 176
IC = ID // 2
SD = 352
S_CHUNKS = [(0, 128), (128, 256), (256, 352)]
CAP = 128
GW = H + EXPERTS
NONE = 999.0
RING = ([(u, "dve") for u in ("wkT", "wvT", "wrT", "gwT", "xT00", "xT01", "xT10", "xT11", "logits")] +
        [(f"{u}{c}{h}", "act") for c in range(2) for u in "kvr" for h in range(2)] +
        [("pos", "dve")] +
        [(f"{u}{c}{h}", "dve") for c in range(2) for h in range(2) for u in ("sg", "su")] +
        [("slots0", "dve"), ("slots1", "dve")] +
        [(f"{u}2{h}", "dve") for h in range(2) for u in ("sg", "su")])
RNAMES = [u for u, _ in RING]


def after(i, per, n):
    return i * per + (per + n)


def full(i, u):
    return after(i, NU, UNITS.index(u) + 1)


def read_dve(i, u):
    return after(i, ND, BY_DVE.index(u) + 1)


def read_act(i, u):
    return after(i, NA, BY_ACT.index(u) + 1)


def ring_reads(u, reader):
    return sum(r == reader for _, r in RING[:RNAMES.index(u) + 1])


def build(nc, x, wq, wk, wv, wo, rw, rb, gup, gub, dnp, dnb, l1, out):
    with ExitStack() as ctx:
        def sb(name, shape, dt=F32, c=ctx):
            return c.enter_context(nc.sbuf_tensor(name, shape, dt))

        def sem(name):
            return ctx.enter_context(nc.semaphore(name))

        ident = sb("ident", [P, P])
        acc = sb("acc", [P, NT, H])
        iota16 = sb("iota16", [P, EXPERTS])
        top8 = sb("top8", [P, NT, 8])
        topi = sb("topi", [P, NT, 8], U32)
        topif = sb("topif", [P, NT, TOPK])
        topw = sb("topw", [P, NT, TOPK])
        onehot = sb("onehot", [P, NT, EXPERTS])
        stats = sb("stats", [P, NT, 6])
        mv = sb("mv", [P, NT, 2])
        sd = sb("sd", [P, 4, NT])
        lg = sb("lg", [P, NT, EXPERTS])
        scores = sb("scores", [P, EXPERTS, NT])
        rsum = sb("rsum", [P, NT])
        small = sb("small", [P, 8])

        l0 = ctx.enter_context(ExitStack())
        s0 = lambda name, shape, dt=F32: sb(name, shape, dt, l0)
        mask = s0("mask", [P, 3, KW])
        rb_bc = s0("rb_bc", [P, EXPERTS])
        rw_raw = s0("rw_raw", [EXPERTS, H])
        rwT = [s0(f"rwT{n}", [P, KC, EXPERTS], F32R) for n in "hl"]
        gub_raw = s0("gub_raw", [EXPERTS, 2 * FD])
        ebias = s0("ebias", [P, 2, 2, EXPERTS])
        dnb_sb = s0("dnb_sb", [EXPERTS, H])
        xT = [s0(f"xT{n}", [P, KC, TP], F32R) for n in "hl"]
        qT = [s0(f"qT{n}", [P, T], F32R) for n in "hl"]
        kw = [s0(f"kw{n}", [P, NT, KW], F32R) for n in "hl"]
        vp = [s0(f"vp{n}", [P, VT, 2 * HD], F32R) for n in "hl"]
        vb = [s0(f"vb{n}", [P, NT, 2 * HD], F32R) for n in "hl"]
        sm = s0("sm", [P, 2, KW])
        pr = s0("pr", [P, 2, 2 * P])
        nm = s0("nm", [P, 2])
        rs = s0("rs", [P, 2])
        rr = s0("rr", [P, 2])
        gm = s0("gm", [GLOBALS, 1])
        gs = s0("gs", [GLOBALS, 1])
        gr = s0("gr", [GLOBALS, 1])
        pg = s0("pg", [GLOBALS, TP])
        pT = [s0(f"pT{n}", [P, 3, 2 * P], F32R) for n in "hl"]
        oT = [s0(f"oT{n}", [P, 2, T], F32R) for n in "hl"]
        qkv_raw = s0("qkv_raw", [P, 3, KC, 2 * HD])
        wo_raw = s0("wo_raw", [P, 2, H])
        gu_raw = s0("gu_raw", [P, KC, 2 * FD])
        dn_raw = s0("dn_raw", [P, 2, H])
        qkvw = [s0(f"qkvw{n}", [P, 3, KC, 2 * HD], F32R) for n in "hl"]
        wow = [s0(f"wow{n}", [P, 2, H], F32R) for n in "hl"]
        guw = [s0(f"guw{n}", [P, 2, KC, 2, FD], F32R) for n in "hl"]
        dnw = [s0(f"dnw{n}", [P, 2, 2, H], F32R) for n in "hl"]
        ff = s0("ff", [P, 3, T])
        hh = [s0(f"hh{n}", [P, 2, T], F32R) for n in "hl"]
        xn = ff[:, 0:2, :].rearrange("p a (b h) -> p (a b) h", h=H)
        scT = ff[0:EXPERTS, 2, :]

        l0.close()

        gw_raw = sb("gw_raw", [EXPERTS, H])
        gwT = [sb(f"gwT{n}", [P, KC, EXPERTS], F32R) for n in "hl"]
        td = sb("td", [P, KC])
        decay = sb("decay", [P, KC])
        xr = [sb(f"xr{n}", [P, NT, GW], F32R) for n in "hl"]
        x2T = [sb(f"x2T{n}", [P, KC, T + 2], F32R) for n in "hl"]
        kvr_raw = sb("kvr_raw", [P, 3, KC, H])
        kvrT = [sb(f"kvrT{n}", [P, 3, KC, H], F32R) for n in "hl"]
        sgu_raw = sb("sgu_raw", [P, 2, KC, SD])
        sgu = [sb(f"sgu{n}", [P, 2, KC, SD], F32R) for n in "hl"]
        sd_raw = sb("sd_raw", [P, 3, H])
        sdw = [sb(f"sdw{n}", [P, 3, H], F32R) for n in "hl"]
        eg_raw = sb("eg_raw", [P, 2, KC, 2, ID])
        ed_raw = sb("ed_raw", [IC, 2, 2, H])
        egw = [sb(f"egw{n}", [P, 2, KC, 2, ID], F32R) for n in "hl"]
        edw = [sb(f"edw{n}", [IC, 2, 2, H], F32R) for n in "hl"]
        xn2 = sb("xn2", [P, NT, H])
        ek = xn2[:].rearrange("p (c t) h -> p c (t h)", c=KC)
        av = sb("av", [P, KC, T])
        rT = sb("rT", [P, KC, T])
        den = sb("den", [P, KC, T])
        st = sb("st", [P, 2, 512])
        sT = [sb(f"sT{n}", [P, 3, T], F32R) for n in "hl"]
        room = kvr_raw[:].rearrange("p n k d -> p (n k d)")
        tt2, gs2, mid = (room[:, n * ID:(n + 1) * ID] for n in range(3))
        xg = room[:, 3 * ID:3 * ID + GW]
        alls, chosen, w16 = (room[:, 1024 + n * P:1024 + (n + 1) * P].rearrange("p (t e) -> p t e", t=NT)
                             for n in range(3))
        chosen_b = sb("chosen_b", [P, NT, EXPERTS], BF16)
        before = sb("before", [P, P], BF16)
        ones_b = sb("ones_b", [P, P], BF16)
        slot = sb("slot", [P, EXPERTS, NT])
        slotT = sb("slotT", [P, T], BF16)
        sel = sb("sel", [P, EXPERTS, P], BF16)
        iota_c = sb("iota_c", [P, P])
        iota_p = sb("iota_p", [P, 1])
        pmat = sb("pmat", [P, 2, NT, CAP], F32R)
        pmT = sb("pmT", [P, 2, T], F32R)
        wsc = sb("wsc", [P, 1])
        xgT = [sb(f"xgT{n}", [P, KC, CAP], F32R) for n in "hl"]
        midT = [sb(f"midT{n}", [IC, 2, CAP], F32R) for n in "hl"]
        eo = [sb(f"eo{n}", [P, H], F32R) for n in "hl"]

        pm = [ctx.enter_context(nc.psum_tensor("stage", [P, 2, T], F32)),
              ctx.enter_context(nc.psum_tensor("ps_s", [P, 512], F32)),
              ctx.enter_context(nc.psum_tensor("ps_t", [P, 512], F32)),
              ctx.enter_context(nc.psum_tensor("ps_o", [P, T], F32))]
        stage, ps_s, ps_t, ps_o = pm

        y = stage[:].rearrange("p a (b h) -> p (a b) h", h=H)
        ring = [ps_s[:], ps_t[:], ps_o[:, 0:512], ps_o[:, 512:T]]
        ps_g, ps_x, ps_f, ps_b = ring

        def ring_of(u):
            return ring[RNAMES.index(u) % 4]

        x_in = sem("x_in")
        small_in = sem("small_in")
        consts = sem("consts")
        pool_seq = sem("pool_seq")
        zeroed = sem("zeroed")
        vseq = sem("vseq")
        sqrt_done = sem("sqrt_done")
        xn_ready = sem("xn_ready")
        xnT_full = sem("xnT_full")
        xT_hi = sem("xT_hi")
        xT_lo = sem("xT_lo")
        small_T = sem("small_T")
        small_hi = sem("small_hi")
        rwT_ready = sem("rwT_ready")
        logits_full = sem("logits_full")
        top_sub = sem("top_sub")
        top_exp = sem("top_exp")
        scores_ready = sem("scores_ready")
        scT_full = sem("scT_full")
        scT_ready = sem("scT_ready")
        bias_full = sem("bias_full")
        acc_ready = sem("acc_ready")
        stage_full = sem("stage_full")
        stage_read_dve = sem("stage_read_dve")
        stage_read_act = sem("stage_read_act")
        qkv_hi = sem("qkv_hi")
        vb_ready = sem("vb_ready")
        scores_full = sem("scores_full")
        smax_done = sem("smax_done")
        exp_done = sem("exp_done")
        recip_done = sem("recip_done")
        p_norm = sem("p_norm")
        gmin_done = sem("gmin_done")
        grecip_done = sem("grecip_done")
        pg_ready = sem("pg_ready")
        pt_full = sem("pt_full")
        pt_hi = sem("pt_hi")
        pt_lo = sem("pt_lo")
        pv_done = sem("pv_done")
        out_hi = sem("out_hi")
        out_lo = sem("out_lo")
        tanh_done = sem("tanh_done")
        clip_done = sem("clip_done")
        glu_done = sem("glu_done")
        h_ready = sem("h_ready")
        h_hi = sem("h_hi")
        h_lo = sem("h_lo")
        w_hi = sem("w_hi")
        w_lo = sem("w_lo")
        ex_loaded = sem("ex_loaded")
        qkv_loaded = sem("qkv_loaded")
        wo_loaded = sem("wo_loaded")
        out_stored = sem("out_stored")
        held = sem("held")

        l1_loaded = sem("l1_loaded")
        l1_consts = sem("l1_consts")
        tokens_hi = sem("tokens_hi")
        ring_full = sem("ring_full")
        ring_act = sem("ring_act")
        ring_dve = sem("ring_dve")
        zeros2 = sem("zeros2")
        decay_exp = sem("decay_exp")
        decay_ready = sem("decay_ready")
        ring_hi = sem("ring_hi")
        l1_w_hi = sem("l1_w_hi")
        l1_w_lo = sem("l1_w_lo")
        l1_sub = sem("l1_sub")
        l1_exp = sem("l1_exp")
        chosen_ready = sem("chosen_ready")
        slots_ready = sem("slots_ready")
        st_tanh = sem("st_tanh")
        sgs_done = sem("sgs_done")
        smid_done = sem("smid_done")
        sT_hi = sem("sT_hi")
        sT_lo = sem("sT_lo")
        rows_hi = sem("rows_hi")
        rows_lo = sem("rows_lo")
        rw_ready = sem("rw_ready")
        y_done = sem("y_done")
        out_ready = sem("out_ready")
        wraw_loaded = sem("wraw_loaded")
        pm_ready = sem("pm_ready")
        g_full = sem("g_full")
        xg_copied = sem("xg_copied")
        xt_full = sem("xt_full")
        xgt_hi = sem("xgt_hi")
        xgt_lo = sem("xgt_lo")
        sb_full = sem("sb_full")
        pmt_ready = sem("pmt_ready")
        f1_full = sem("f1_full")
        tanh2_done = sem("tanh2_done")
        gs2_done = sem("gs2_done")
        mid_ready = sem("mid_ready")
        mt_full = sem("mt_full")
        mt_hi = sem("mt_hi")
        mt_lo = sem("mt_lo")
        f2_full = sem("f2_full")
        eo_hi = sem("eo_hi")
        eo_lo = sem("eo_lo")
        sc_done = sem("sc_done")
        ew_loaded = [sem(f"ew_loaded{b}") for b in range(2)]
        ew_hi = sem("ew_hi")
        ew_lo = sem("ew_lo")
        wsc_ready = sem("wsc_ready")

        block = ctx.enter_context(nc.Block())

        @block.sync
        def _(sp):
            sp.dma_start(acc[:], x.rearrange("(t p) h -> p t h", p=P)).then_inc(x_in, 16)
            sp.dma_start(rw_raw[:], rw).then_inc(small_in, 16)
            sp.dma_start(gub_raw[:], gub).then_inc(small_in, 16)
            sp.dma_start(dnb_sb[:], dnb).then_inc(small_in, 16)
            sp.dma_start(rb_bc[:], rb.rearrange("(a e) -> a e", a=1).broadcast_to([P, EXPERTS])).then_inc(small_in, 16)
            with sp.Fori(0, PAIRS) as i:
                sp.wait_ge(stage_read_dve, read_dve(i, "v3"))
                for n in range(2):
                    sp.dma_start(vb[n][0:WIN - P, :, :].bitcast(F32), vp[n][0:WIN - P, 1:VT, :].bitcast(F32)).then_inc(vb_ready, 16)
                    for t in range(NT):
                        sp.dma_start(vb[n][WIN - P:KB, t, :].bitcast(F32),
                                     vp[n][HALF:HALF + GLOBALS, 0, :].bitcast(F32)).then_inc(vb_ready, 16)
            sp.wait_ge(stage_read_dve, read_dve(PAIRS - 1, "wo1"))
            for n, w in enumerate((l1["Wk"], l1["Wv"], l1["Wr"])):
                sp.dma_start(kvr_raw[:, n, :, :], w.rearrange("(c p) d -> p c d", p=P)).then_inc(l1_loaded, 16)
            sp.dma_start(gw_raw[:], l1["gate_w"]).then_inc(l1_loaded, 16)
            sp.dma_start(td[:], l1["time_decay"].rearrange("(c p) -> p c", p=P),
                         allow_slow_non_contiguous=True).then_inc(l1_loaded, 16)
            for n, w in enumerate((l1["sw_gate"], l1["sw_up"])):
                sp.dma_start(sgu_raw[:, n, :, :], w.rearrange("(k p) n -> p k n", p=P)).then_inc(l1_loaded, 16)
            sp.dma_start(sd_raw[:, 0:2, :], l1["sw_down"][0:2 * P, :].rearrange("(c p) n -> p c n", p=P))\
                .then_inc(l1_loaded, 16)
            sp.dma_start(sd_raw[0:SD - 2 * P, 2, :], l1["sw_down"][2 * P:SD, :]).then_inc(l1_loaded, 16)

            def load(e, b):
                for n, w in enumerate((l1["w_gate"], l1["w_up"])):
                    sp.dma_start(eg_raw[:, b, :, n, :], w[e].rearrange("(k p) n -> p k n", p=P)).then_inc(ew_loaded[b], 16)
                sp.dma_start(ed_raw[:, b, :, :], l1["w_down"][e].rearrange("(c p) n -> p c n", p=IC)).then_inc(ew_loaded[b], 16)

            with sp.Fori(0, EXPERTS // 2) as i:
                sp.wait_ge(ew_lo, i * 2 + 1)
                load(i * 2, 0)
                load(i * 2 + 1, 1)
            for q in range(2):
                sp.wait_ge(out_ready, q + 1)
                sp.dma_start(out.rearrange("(t p) h -> p t h", p=P)[:, 4 * q:4 * q + 4, :], acc[:, 4 * q:4 * q + 4, :])\
                    .then_inc(out_stored, 16)
            sp.wait_ge(out_stored, 32)

        @block.gpsimd
        def _(pool):
            seq = 0

            def step(ins):
                nonlocal seq
                ins.then_inc(pool_seq, 1)
                seq += 1
                pool.wait_ge(pool_seq, seq)

            step(nc.gpsimd.memset(ident[:], 0.0))
            step(nc.gpsimd.affine_select(out=ident[:], in_=ident[:], compare_op=ALU.not_equal, fill=1.0,
                                         base=0, pattern=[[-1, P]], channel_multiplier=1))
            nc.gpsimd.iota(iota16[:], pattern=[[1, EXPERTS]], base=0, channel_multiplier=0,
                           allow_small_or_imprecise_dtypes=True).then_inc(consts, 1)
            step(nc.gpsimd.memset(mask[:], 0.0))
            for m in range(3):
                win = mask[:, m, 0:WIN]
                step(nc.gpsimd.affine_select(out=win, in_=win, compare_op=ALU.is_ge, fill=OUTSIDE,
                                             base=-1, pattern=[[1, WIN]], channel_multiplier=-1))
                step(nc.gpsimd.affine_select(out=win, in_=win, compare_op=ALU.is_ge, fill=OUTSIDE,
                                             base=WINDOW - 1, pattern=[[-1, WIN]], channel_multiplier=1))
            win = mask[:, 0, 0:WIN]
            step(nc.gpsimd.affine_select(out=win, in_=win, compare_op=ALU.is_ge, fill=OUTSIDE,
                                         base=-HALF - GLOBALS, pattern=[[1, WIN]], channel_multiplier=0))
            win = mask[:, 2, 0:WIN]
            nc.gpsimd.affine_select(out=win, in_=win, compare_op=ALU.is_ge, fill=OUTSIDE,
                                    base=P + HALF - 1, pattern=[[-1, WIN]], channel_multiplier=0).then_inc(consts, 1)

            def load_expert(e):
                pool.dma_start(gu_raw[:], gup[e].rearrange("(k p) n -> p k n", p=P)).then_inc(ex_loaded, 16)
                pool.dma_start(dn_raw[:], dnp[e].rearrange("(c p) n -> p c n", p=P)).then_inc(ex_loaded, 16)

            with pool.Fori(0, PAIRS) as i:
                pool.wait_ge(w_lo, after(i, NW, -7))
                load_expert(i * 2)
                for n, w in enumerate((wq, wk, wv)):
                    pool.dma_start(qkv_raw[:, n, :, :], w.rearrange("(k p) (g n) -> g p k n", p=P, n=2 * HD)[i])\
                        .then_inc(qkv_loaded, 16)
                pool.wait_ge(w_lo, after(i, NW, -3))
                load_expert(i * 2 + 1)
                pool.dma_start(wo_raw[:], wo.rearrange("(g j d) n -> g d j n", j=2, d=HD)[i]).then_inc(wo_loaded, 16)

            pool.wait_ge(stage_read_dve, read_dve(PAIRS - 1, "wo1"))
            step(nc.gpsimd.memset(before[:], 1.0))
            step(nc.gpsimd.affine_select(out=before[:], in_=before[:], compare_op=ALU.is_gt, fill=0.0,
                                         base=0, pattern=[[1, P]], channel_multiplier=-1))
            nc.gpsimd.memset(ones_b[:], 1.0)
            nc.gpsimd.iota(iota_c[:], pattern=[[1, P]], base=0, channel_multiplier=0,
                           allow_small_or_imprecise_dtypes=True)
            nc.gpsimd.iota(iota_p[:], pattern=[[1, 1]], base=0, channel_multiplier=1,
                           allow_small_or_imprecise_dtypes=True)
            step(nc.gpsimd.memset(sel[:], 0.0))
            nc.gpsimd.affine_select(out=sel[:], in_=sel[:], compare_op=ALU.not_equal, fill=1.0, base=0,
                                    pattern=[[-1, EXPERTS], [0, P]], channel_multiplier=1).then_inc(l1_consts, 1)
            pool.sem_inc(ew_lo, 1)

            def weights_lo(i, b):
                pool.wait_ge(ew_hi, after(i, 2, b + 1))
                nc.gpsimd.tensor_tensor(egw[1][:, b], eg_raw[:, b], egw[0][:, b].bitcast(F32), ALU.subtract)
                nc.gpsimd.tensor_tensor(edw[1][:, b], ed_raw[:, b], edw[0][:, b].bitcast(F32), ALU.subtract)\
                    .then_inc(ew_lo, 1)

            with pool.Fori(0, EXPERTS // 2) as i:
                weights_lo(i, 0)
                weights_lo(i, 1)

        def k_windows(t_out, src):
            a = src[:, 0:T]
            mid = bass.AP(a.tensor, a.offset + P - HALF, [list(a.ap[0]), [P, NT - 2], [1, WIN]])
            return [(t_out[:, 1:NT - 1, 0:WIN], mid),
                    (t_out[:, 0, HALF:WIN], src[:, 0:WIN - HALF]),
                    (t_out[:, NT - 1, 0:WIN - HALF], src[:, T - WIN + HALF:T]),
                    (t_out[:, :, WIN:KW], src[:, 0:GLOBALS].unsqueeze(1).broadcast_to([P, NT, GLOBALS]))]

        def stage_of(u):
            return stage[:, UNITS.index(u) % 2, :]

        def expert_pieces(b):
            gr_ = gu_raw[:].rearrange("p k (d s) -> p k s d", s=2)
            return [(guw[0][:, b, k], guw[1][:, b, k], gr_[:, k]) for k in range(KC)] + \
                   [(dnw[0][:, b], dnw[1][:, b], dn_raw[:])]

        qkv_pieces = [(qkvw[0][:, n], qkvw[1][:, n], qkv_raw[:, n]) for n in range(3)]
        wo_piece = (wow[0][:], wow[1][:], wo_raw[:])

        @block.scalar
        def _(act):
            for s_, per in ((qkv_hi, 8), (exp_done, NS), (stage_read_act, NA), (pt_hi, NP), (tanh_done, 4),
                            (h_hi, 4), (out_hi, 2), (w_hi, 4)):
                act.sem_inc(s_, per)
            act.wait_ge(sqrt_done, 1)
            nc.scalar.activation(sd[:, 1], sd[:, 0], ACT.Sqrt).then_inc(sqrt_done, 1)

            for k in range(KC):
                act.wait_ge(xnT_full, k + 1)
                nc.scalar.activation(xT[0][:, k, HALF:HALF + T], stage[:, k, :], ACT.Copy).then_inc(xT_hi, 1)
            act.wait_ge(small_T, 1)
            nc.scalar.activation(rwT[0][:], ps_s[:, 0:KC * EXPERTS].rearrange("p (k e) -> p k e", k=KC),
                                 ACT.Copy).then_inc(small_hi, 1)

            def split_hi(i, n, piece):
                nc.scalar.activation(piece[0], piece[2], ACT.Copy).then_inc(w_hi, 1)

            def even_expert(i, n):
                if n == 0:
                    act.wait_ge(ex_loaded, i * 64 + 96)
                    act.wait_ge(stage_full, full(i, "down10"))
                split_hi(i, n, expert_pieces(0)[n])

            def next_qkv(i, n):
                if n == 0:
                    act.wait_ge(qkv_loaded, i * 48 + 96)
                    act.wait_ge(stage_full, full(i, "k1"))
                split_hi(i, n, qkv_pieces[n])

            for n in range(3):
                even_expert(-1, n)
            for n in range(3):
                next_qkv(-1, n)

            act.wait_ge(top_sub, 1)
            nc.scalar.activation(topw[:], topw[:], ACT.Exp).then_inc(top_exp, 1)

            def body(i, more):
                def qk(j):
                    act.wait_ge(stage_full, full(i, f"q{j}"))
                    act.wait_ge(scores_full, after(i, NS, NT * j))
                    nc.scalar.activation(qT[0][:], stage_of(f"q{j}"), ACT.Copy, scale=-SCALE).then_inc(qkv_hi, 1)
                    act.wait_ge(stage_full, full(i, f"k{j}"))
                    for n, (dst, src) in enumerate(k_windows(kw[0], stage_of(f"k{j}"))):
                        ins = nc.scalar.activation(dst, src, ACT.Copy)
                    ins.then_inc(qkv_hi, 1)

                def values():
                    act.wait_ge(pv_done, after(i, NP, 0))
                    for v, (a, b) in enumerate(V_TILES):
                        act.wait_ge(stage_full, full(i, f"v{v}"))
                        src = stage_of(f"v{v}")[:, 0:(b - a) * 2 * HD].rearrange("p (t n) -> p t n", n=2 * HD)
                        nc.scalar.activation(vp[0][:, a:b, :], src, ACT.Copy).then_inc(qkv_hi, 1)

                def head(j):
                    for s in range(NT + 3):
                        if s == 0:
                            act.wait_ge(gmin_done, after(i, 2, j + 1))
                            act.wait_ge(pt_full, after(i, NP, 9 * j))
                            nc.scalar.activation(pg[:, HALF:HALF + T], stage_of(f"sg{j}")[0:GLOBALS, :], ACT.Exp,
                                                 bias=gm[:, 0:1], scale=-1.0, accum_out=gs[:, 0:1])\
                                .then_inc(stage_read_act, 1)
                        if s < NT:
                            n = NT * j + s
                            act.wait_ge(smax_done, after(i, NS, n + 1))
                            act.wait_ge(pt_full, after(i, NP, 9 * ((n - 2) // NT) + (n - 2) % NT + 1))
                            nc.scalar.activation(pr[:, n % 2, 0:KW], sm[:, n % 2, :], ACT.Exp,
                                                 bias=nm[:, n % 2:n % 2 + 1], scale=-1.0,
                                                 accum_out=rs[:, n % 2:n % 2 + 1]).then_inc(exp_done, 1)
                        for c in range(2):
                            e = 2 * j + c
                            if s == 3 + 4 * c:
                                act.wait_ge(stage_read_dve, read_dve(i, f"gate{c}{j}"))
                                act.wait_ge(h_ready, after(i, 4, e))
                                nc.scalar.activation(ff[:, 1], ff[:, 0], ACT.Tanh, scale=ALPHA / 2)\
                                    .then_inc(tanh_done, 1)
                            if s == 4 + 4 * c:
                                act.wait_ge(stage_full, full(i, f"up{c}{j}"))
                                act.wait_ge(h_lo, after(i, 4, e))
                                nc.scalar.activation(ff[:, 2], stage_of(f"up{c}{j}"), ACT.Identity,
                                                     bias=ub(i, c, j), scale=0.5).then_inc(stage_read_act, 1)
                            if s == 5 + 4 * c:
                                act.wait_ge(h_ready, after(i, 4, e + 1))
                                if c == 0:
                                    act.wait_ge(stage_full, after(i, NU, 0) - 2 if j == 0 else full(i, "down10"))
                                nc.scalar.activation(hh[0][:, c], ff[:, 2], ACT.Copy).then_inc(h_hi, 1)
                        if 1 <= s <= NT + 1:
                            m = 9 * j + s - 1
                            w = 2 * P if s <= NT else VT * GLOBALS
                            act.wait_ge(pt_full, after(i, NP, m + 1))
                            act.wait_ge(pv_done, after(i, NP, m - 2))
                            nc.scalar.activation(pT[0][:, m % 3, 0:w], ps_t[:, 0:w], ACT.Copy)\
                                .then_inc(pt_hi, 1)
                        if j == 0:
                            if s in (0, 1, 3):
                                n = {0: 0, 1: 1, 3: 2}[s]
                                if n == 0:
                                    act.wait_ge(ex_loaded, i * 64 + 64)
                                    act.wait_ge(stage_full, after(i, NU, 0) - 2)
                                split_hi(i, n, expert_pieces(1)[n])
                            if s == 7:
                                act.wait_ge(wo_loaded, i * 16 + 16)
                                act.wait_ge(stage_full, after(i, NU, 0))
                                split_hi(i, 3, wo_piece)
                        elif more:
                            if s in (0, 1, 3):
                                even_expert(i, {0: 0, 1: 1, 3: 2}[s])
                            if s in (7, 9, 10):
                                next_qkv(i, {7: 0, 9: 1, 10: 2}[s])
                    act.wait_ge(pv_done, after(i, NP, 9 * j + 9))
                    if j == 0:
                        act.wait_ge(stage_full, after(i, NU, 0))
                    nc.scalar.activation(oT[0][:, j], ps_o[:], ACT.Copy).then_inc(out_hi, 1)

                def ub(i, c, j):
                    e = i * 2 + j
                    return ebias[:, 1, c, bass.ds(e, 1)]

                qk(0)
                values()
                head(0)
                qk(1)
                head(1)

            with act.Fori(0, PAIRS - 1) as i:
                body(i, True)
            body(PAIRS - 1, False)

            for s_ in (xg_copied, xgt_hi, tanh2_done, mt_hi, eo_hi, ew_hi):
                act.sem_inc(s_, 2)

            def ring_hi_of(u, dst, src):
                act.wait_ge(ring_full, RNAMES.index(u) + 1)
                nc.scalar.activation(dst, src, ACT.Copy).then_inc(ring_hi, 1)

            for n, u in enumerate(("wkT", "wvT", "wrT")):
                ring_hi_of(u, kvrT[0][:, n], ring_of(u).rearrange("p (k e) -> p k e", k=KC))
            ring_hi_of("gwT", gwT[0][:], ring_of("gwT")[:, 0:KC * EXPERTS].rearrange("p (k e) -> p k e", k=KC))
            act.wait_ge(sqrt_done, 3)
            nc.scalar.activation(sd[:, 1], sd[:, 0], ACT.Sqrt).then_inc(sqrt_done, 1)
            act.wait_ge(l1_loaded, 9 * 16)
            nc.scalar.activation(decay[:], td[:], ACT.Exp).then_inc(decay_exp, 1)
            act.wait_ge(decay_exp, 1)
            nc.scalar.activation(decay[:], decay[:], ACT.Exp, scale=-1.0).then_inc(decay_ready, 1)
            for k in range(KC):
                for h in range(2):
                    u = f"xT{k}{h}"
                    ring_hi_of(u, x2T[0][:, k, 1 + h * 512:1 + (h + 1) * 512], ring_of(u))
            for g in range(2):
                nc.scalar.activation(sgu[0][:, g], sgu_raw[:, g], ACT.Copy).then_inc(l1_w_hi, 1)
            for h in range(2):
                nc.scalar.activation(xr[0][:, 4 * h:4 * h + 4, 0:H], xn2[:, 4 * h:4 * h + 4, :], ACT.Copy)\
                    .then_inc(rows_hi, 1)
            act.wait_ge(l1_sub, 1)
            nc.scalar.activation(topw[:], topw[:], ACT.Exp)
            nc.scalar.activation(alls[:], alls[:], ACT.Exp).then_inc(l1_exp, 1)
            for c in range(KC):
                for u, func, dst in (("k", ACT.Exp, ek), ("v", ACT.Copy, av), ("r", ACT.Copy, rT)):
                    for h in range(2):
                        act.wait_ge(ring_full, RNAMES.index(f"{u}{c}{h}") + 1)
                        if u == "k" and c == 0 and h == 0:
                            act.wait_ge(rows_lo, 2)
                        nc.scalar.activation(dst[:, c, h * 512:(h + 1) * 512], ring_of(f"{u}{c}{h}"), func)\
                            .then_inc(ring_act, 1)
            nc.scalar.activation(sdw[0][:, 0:2], sd_raw[:, 0:2], ACT.Copy)
            nc.scalar.activation(sdw[0][0:SD - 2 * P, 2], sd_raw[0:SD - 2 * P, 2], ACT.Copy).then_inc(l1_w_hi, 1)

            def expert_hi(i, b):
                act.wait_ge(ew_loaded[b], i * 48 + 48)
                act.wait_ge(f2_full, after(i, 2, b - 1))
                nc.scalar.activation(egw[0][:, b], eg_raw[:, b], ACT.Copy)
                nc.scalar.activation(edw[0][:, b], ed_raw[:, b], ACT.Copy).then_inc(ew_hi, 1)

            for n in range(7):
                c, h = n // 2, n % 2
                if n < 6:
                    w = S_CHUNKS[c][1] - S_CHUNKS[c][0]
                    act.wait_ge(ring_full, RNAMES.index(f"sg{c}{h}") + 1)
                    if n >= 2:
                        act.wait_ge(sT_lo, n - 1)
                    nc.scalar.activation(st[0:w, n % 2], ring_of(f"sg{c}{h}")[0:w, :], ACT.Tanh, scale=0.5)\
                        .then_inc(st_tanh, 1)
                if n >= 1:
                    c, h = (n - 1) // 2, (n - 1) % 2
                    w = S_CHUNKS[c][1] - S_CHUNKS[c][0]
                    act.wait_ge(smid_done, n)
                    nc.scalar.activation(sT[0][0:w, c, h * 512:(h + 1) * 512], st[0:w, (n - 1) % 2], ACT.Copy)\
                        .then_inc(sT_hi, 1)
                if n == 1:
                    expert_hi(0, 0)

            def step2(i, b, last):
                n = b + 1
                act.wait_ge(g_full, after(i, 2, n))
                act.wait_ge(xt_full, after(i, 2, b))
                act.wait_ge(wsc_ready, after(i, 2, b))
                nc.scalar.activation(xg[:], ps_g[:, 0:GW], ACT.Copy).then_inc(xg_copied, 1)
                act.wait_ge(xt_full, after(i, 2, n))
                act.wait_ge(f1_full, after(i, 2, b))
                nc.scalar.activation(xgT[0][:], ps_x[:, 0:H].rearrange("p (k c) -> p k c", k=KC), ACT.Copy)\
                    .then_inc(xgt_hi, 1)
                if not last:
                    if b == 0:
                        expert_hi(i, 1)
                    else:
                        act.wait_ge(ew_loaded[0], i * 48 + 96)
                        act.wait_ge(f2_full, after(i, 2, 1))
                        nc.scalar.activation(egw[0][:, 0], eg_raw[:, 0], ACT.Copy)
                        nc.scalar.activation(edw[0][:, 0], ed_raw[:, 0], ACT.Copy).then_inc(ew_hi, 1)
                act.wait_ge(f1_full, after(i, 2, n))
                act.wait_ge(gs2_done, after(i, 2, b))
                nc.scalar.activation(tt2[:], ps_f[:, 0:ID], ACT.Tanh, scale=0.5).then_inc(tanh2_done, 1)
                act.wait_ge(mt_full, after(i, 2, n))
                act.wait_ge(f2_full, after(i, 2, b))
                nc.scalar.activation(midT[0][:], ps_x[0:IC, 0:2 * CAP].rearrange("p (c t) -> p c t", c=2), ACT.Copy)\
                    .then_inc(mt_hi, 1)
                act.wait_ge(f2_full, after(i, 2, n))
                act.wait_ge(sc_done, after(i, 2, b))
                nc.scalar.activation(eo[0][:], ps_f[:, 0:H], ACT.Copy).then_inc(eo_hi, 1)

            step2(0, 0, False)
            step2(0, 1, False)
            with act.Fori(1, EXPERTS // 2 - 1) as i:
                step2(i, 0, False)
                step2(i, 1, False)
            step2(EXPERTS // 2 - 1, 0, False)
            step2(EXPERTS // 2 - 1, 1, True)

        @block.tensor
        def _(pe):
            for s_, per in ((stage_full, NU), (scores_full, NS), (pt_full, NP), (pv_done, NP)):
                pe.sem_inc(s_, per)

            def three(out_, a, b, start, stop):
                nc.tensor.matmul(out_, a[0], b[0], start=start, stop=False, skip_group_check=True)
                nc.tensor.matmul(out_, a[0], b[1], start=False, stop=False, skip_group_check=True)
                return nc.tensor.matmul(out_, a[1], b[0], start=False, stop=stop, skip_group_check=True)

            pe.wait_ge(consts, 1)
            for k in range(KC):
                for t in range(NT):
                    if k == 0:
                        pe.wait_ge(xn_ready, t + 1)
                    ins = nc.tensor.transpose(stage[:, k, t * P:(t + 1) * P], xn[:, t, k * P:(k + 1) * P], ident[:])
                ins.then_inc(xnT_full, 1)
            pe.wait_ge(small_in, 64)
            for k in range(KC):
                nc.tensor.transpose(ps_s[:, k * EXPERTS:(k + 1) * EXPERTS], rw_raw[:, k * P:(k + 1) * P],
                                    ident[0:EXPERTS, 0:EXPERTS])
            bias_src = gub_raw[:].rearrange("e (c d s) -> e s c d", s=2, d=P)
            for s in range(2):
                for c in range(2):
                    col = KC * EXPERTS + (2 * s + c) * EXPERTS
                    ins = nc.tensor.transpose(ps_s[:, col:col + EXPERTS], bias_src[:, s, c, :],
                                              ident[0:EXPERTS, 0:EXPERTS])
            ins.then_inc(small_T, 1)
            pe.wait_ge(xT_lo, KC)
            pe.wait_ge(rwT_ready, 1)
            for t in range(NT):
                for k in range(KC):
                    a = [xT[n][:, k, HALF + t * P:HALF + (t + 1) * P] for n in range(2)]
                    ins = three(ps_t[:, t * EXPERTS:(t + 1) * EXPERTS], a, [rwT[n][:, k, :] for n in range(2)],
                                k == 0, k == KC - 1)
            ins.then_inc(logits_full, 1)

            def body(i):
                def stage_free(u):
                    n = UNITS.index(u) - 2
                    last, i_back = UNITS[n], (0 if n >= 0 else 1)
                    if last in BY_ACT:
                        pe.wait_ge(stage_read_act, after(i, NA, BY_ACT.index(last) + 1 - i_back * NA))
                    else:
                        pe.wait_ge(stage_read_dve, after(i, ND, BY_DVE.index(last) + 1 - i_back * ND))

                def project(u, parts, n_half=(0, 1)):
                    o = stage_of(u)
                    if 0 in n_half:
                        stage_free(u)
                    for h in n_half:
                        for k in range(KC):
                            b = [xT[n][:, k, HALF + h * 512:HALF + (h + 1) * 512] for n in range(2)]
                            ins = three(o[:, h * 512:(h + 1) * 512], parts(k), b, k == 0, k == KC - 1)
                    if 1 in n_half:
                        ins.then_inc(stage_full, 1)

                def qk(j):
                    if j == 0:
                        pe.wait_ge(w_lo, after(i, NW, 0))
                    for n, u in enumerate(("q", "k")):
                        project(f"{u}{j}", lambda k: [qkvw[m][:, n, k, j * HD:(j + 1) * HD] for m in range(2)])

                def values():
                    for v, (a, b) in enumerate(V_TILES):
                        u = f"v{v}"
                        stage_free(u)
                        for t in range(a, b):
                            o = stage_of(u)[:, (t - a) * 2 * HD:(t - a + 1) * 2 * HD]
                            for k in range(KC):
                                ins = three(o, [xT[n][:, k, t * P:(t + 1) * P] for n in range(2)],
                                            [qkvw[n][:, 2, k, :] for n in range(2)], k == 0, k == KC - 1)
                        ins.then_inc(stage_full, 1)

                def global_scores(j):
                    u = f"sg{j}"
                    stage_free(u)
                    pe.wait_ge(stage_read_dve, read_dve(i, f"k{j}"))
                    for h in range(2):
                        ins = three(stage_of(u)[:, h * 512:(h + 1) * 512], [qT[n][:, 0:P] for n in range(2)],
                                    [kw[n][:, 4 * h:4 * h + 4, HALF:HALF + P] for n in range(2)], True, True)
                    ins.then_inc(stage_full, 1)

                def expert_piece(j, s):
                    u = ("gate0", "up0", "gate1", "up1")[s // 2]
                    g, c = (0 if u[0] == "g" else 1), int(u[-1])
                    if s == 0:
                        pe.wait_ge(w_lo, after(i, NW, 0 if j == 0 else 3))
                    project(f"{u}{j}", lambda k: [guw[n][:, j, k, g, c * P:(c + 1) * P] for n in range(2)], (s % 2,))

                def down(j):
                    pe.wait_ge(h_lo, after(i, 4, 2 * j + 2))
                    for q in range(2):
                        u = f"down{q}{j}"
                        stage_free(u)
                        for t in range(4):
                            tt = 4 * q + t
                            for c in range(2):
                                ins = three(stage_of(u)[:, t * H:(t + 1) * H],
                                            [hh[n][:, c, tt * P:(tt + 1) * P] for n in range(2)],
                                            [dnw[n][:, j, c, :] for n in range(2)], c == 0, c == 1)
                        ins.then_inc(stage_full, 1)

                def head(j):
                    for s in range(NT + 3):
                        if s < NT:
                            n = NT * j + s
                            pe.wait_ge(smax_done, after(i, NS, n))
                            three(ps_s[:, 0:KW], [qT[m][:, s * P:(s + 1) * P] for m in range(2)],
                                  [kw[m][:, s, :] for m in range(2)], True, True).then_inc(scores_full, 1)
                        if 1 <= s <= NT:
                            n, m = NT * j + s - 1, 9 * j + s - 1
                            pe.wait_ge(p_norm, after(i, NS, n + 1))
                            pe.wait_ge(pt_lo, after(i, NP, m))
                            for b in range(2):
                                ins = nc.tensor.transpose(ps_t[:, b * P:(b + 1) * P],
                                                          pr[:, n % 2, b * P:(b + 1) * P], ident[:])
                            ins.then_inc(pt_full, 1)
                        if s == NT + 1:
                            m = 9 * j + NT
                            pe.wait_ge(pg_ready, after(i, 2, j + 1))
                            pe.wait_ge(pt_lo, after(i, NP, m))
                            pe.sem_inc(held, 1)
                            for t in range(VT):
                                ins = nc.tensor.transpose(ps_t[:, t * GLOBALS:(t + 1) * GLOBALS],
                                                          pg[:, t * P:(t + 1) * P], ident[0:GLOBALS, 0:GLOBALS])
                            ins.then_inc(pt_full, 1)
                        if 2 <= s <= NT + 1:
                            t, m = s - 2, 9 * j + s - 2
                            pe.wait_ge(pt_lo, after(i, NP, m + 1))
                            if t == 0:
                                pe.wait_ge(out_lo, after(i, 2, j))
                                if j == 0:
                                    pe.wait_ge(stage_read_dve, read_dve(i, "v3"))
                                    pe.wait_ge(vb_ready, i * 288 + 288)
                            o = ps_o[:, t * P:(t + 1) * P]
                            hs = slice(j * HD, (j + 1) * HD)
                            three(o, [vp[n][:, t, hs] for n in range(2)], [pT[n][:, m % 3, 0:P] for n in range(2)],
                                  True, False)
                            three(o, [vb[n][0:KB, t, hs] for n in range(2)],
                                  [pT[n][0:KB, m % 3, P:2 * P] for n in range(2)], False, True).then_inc(pv_done, 1)
                        if s == NT + 2:
                            m = 9 * j + NT
                            pe.wait_ge(pt_lo, after(i, NP, m + 1))
                            hs = slice(j * HD, (j + 1) * HD)
                            for t in range(VT):
                                ins = three(ps_o[:, 0:GLOBALS], [vp[n][:, t, hs] for n in range(2)],
                                            [pT[n][:, m % 3, t * GLOBALS:(t + 1) * GLOBALS] for n in range(2)],
                                            t == 0, t == VT - 1)
                            ins.then_inc(pv_done, 1)
                        if s < NT:
                            expert_piece(j, s)

                qk(0)
                values()
                global_scores(0)
                head(0)
                qk(1)
                down(0)
                global_scores(1)
                head(1)
                down(1)
                pe.wait_ge(w_lo, after(i, NW, 4))
                pe.wait_ge(out_lo, after(i, 2, 2))
                for q in range(2):
                    u = f"wo{q}"
                    stage_free(u)
                    for t in range(4):
                        tt = 4 * q + t
                        for j in range(2):
                            ins = three(stage_of(u)[:, t * H:(t + 1) * H],
                                        [oT[n][:, j, tt * P:(tt + 1) * P] for n in range(2)],
                                        [wow[n][:, j, :] for n in range(2)], j == 0, j == 1)
                    ins.then_inc(stage_full, 1)

            pe.wait_ge(scores_ready, 1)
            for t in range(NT):
                ins = nc.tensor.transpose(ps_o[0:EXPERTS, t * P:(t + 1) * P], scores[:, :, t], ident[:])
            ins.then_inc(scT_full, 1)
            pe.wait_ge(scT_ready, 1)
            for t in range(NT):
                ins = nc.tensor.matmul(stage[:, t // 4, (t % 4) * H:(t % 4 + 1) * H], scT[:, t * P:(t + 1) * P],
                                       dnb_sb[:], start=True, stop=True)
            ins.then_inc(bias_full, 1)
            pe.wait_ge(acc_ready, 1)

            with pe.Fori(0, PAIRS) as i:
                body(i)

            for s_, per in ((g_full, 2), (xt_full, 2), (sb_full, 4), (f1_full, 2), (mt_full, 2), (f2_full, 2),
                            (sc_done, 2)):
                pe.sem_inc(s_, per)

            def ring_free(u):
                n = RNAMES.index(u) - 4
                if n >= 0:
                    last, reader = RING[n]
                    pe.wait_ge(ring_act if reader == "act" else ring_dve, ring_reads(last, reader))

            pe.wait_ge(stage_read_dve, read_dve(PAIRS - 1, "wo1"))
            pe.wait_ge(l1_loaded, 9 * 16)
            for n, u in enumerate(("wkT", "wvT", "wrT")):
                for k in range(KC):
                    for c in range(KC):
                        ins = nc.tensor.transpose(ring_of(u)[:, k * H + c * P:k * H + (c + 1) * P],
                                                  kvr_raw[:, n, c, k * P:(k + 1) * P], ident[:])
                ins.then_inc(ring_full, 1)
            for k in range(KC):
                ins = nc.tensor.transpose(ring_of("gwT")[:, k * EXPERTS:(k + 1) * EXPERTS], gw_raw[:, k * P:(k + 1) * P],
                                          ident[0:EXPERTS, 0:EXPERTS])
            ins.then_inc(ring_full, 1)
            for k in range(KC):
                for h in range(2):
                    u = f"xT{k}{h}"
                    ring_free(u)
                    for t in range(4 * h, 4 * h + 4):
                        pe.wait_ge(xn_ready, NT + t + 1)
                        ins = nc.tensor.transpose(ring_of(u)[:, (t % 4) * P:(t % 4 + 1) * P],
                                                  xn2[:, t, k * P:(k + 1) * P], ident[:])
                    ins.then_inc(ring_full, 1)
            ring_free("logits")
            pe.wait_ge(ring_dve, ring_reads("xT11", "dve"))
            for t in range(NT):
                for k in range(KC):
                    ins = three(ring_of("logits")[:, t * EXPERTS:(t + 1) * EXPERTS],
                                [x2T[n][:, k, 1 + t * P:1 + (t + 1) * P] for n in range(2)],
                                [gwT[n][:, k, :] for n in range(2)], k == 0, k == KC - 1)
            ins.then_inc(ring_full, 1)

            def ring_project(u, w, parts, shift, h):
                ring_free(u)
                for k in range(KC):
                    b = [x2T[n][:, k, shift + h * 512:shift + (h + 1) * 512] for n in range(2)]
                    ins = three(ring_of(u)[0:w, :], parts(k), b, k == 0, k == KC - 1)
                ins.then_inc(ring_full, 1)

            pe.wait_ge(zeros2, 1)
            for c in range(KC):
                for n, u in enumerate("kvr"):
                    for h in range(2):
                        ring_project(f"{u}{c}{h}", P, lambda k: [kvrT[m][:, n, k, c * P:(c + 1) * P] for m in range(2)],
                                     1 if u == "r" else 0, h)
            ring_free("pos")
            pe.wait_ge(chosen_ready, 1)
            pe.wait_ge(l1_consts, 1)
            pos = ring_of("pos")[:, 0:NT * EXPERTS].rearrange("p (t e) -> p t e", t=NT)
            nc.tensor.matmul(pos, before[:], chosen_b[:], start=True, stop=False, skip_group_check=True)
            for t in range(NT - 1):
                ins = nc.tensor.matmul(pos[:, t + 1:NT, :], ones_b[:],
                                       chosen_b[:, t:t + 1, :].broadcast_to([P, NT - 1 - t, EXPERTS]),
                                       start=False, stop=t == NT - 2, skip_group_check=True)
            ins.then_inc(ring_full, 1)

            def shared(c, h):
                lo, hi = S_CHUNKS[c]
                for g, u in enumerate(("sg", "su")):
                    ring_project(f"{u}{c}{h}", hi - lo, lambda k: [sgu[m][:, g, k, lo:hi] for m in range(2)], 1, h)

            pe.wait_ge(l1_w_lo, 2)
            for c in range(2):
                for h in range(2):
                    shared(c, h)
            pe.wait_ge(slots_ready, 1)
            for h in range(2):
                u = f"slots{h}"
                ring_free(u)
                for t in range(4 * h, 4 * h + 4):
                    ins = nc.tensor.transpose(ring_of(u)[0:EXPERTS, (t % 4) * P:(t % 4 + 1) * P], slot[:, :, t],
                                              ident[:])
                ins.then_inc(ring_full, 1)
            shared(2, 0)
            shared(2, 1)
            pe.wait_ge(sT_lo, 6)
            pe.wait_ge(l1_w_lo, 3)
            for t in range(NT):
                for c, (lo, hi) in enumerate(S_CHUNKS):
                    three(y[:, t, :], [sT[n][0:hi - lo, c, t * P:(t + 1) * P] for n in range(2)],
                          [sdw[n][0:hi - lo, c, :] for n in range(2)], c == 0 and t % 2 == 0, False)

            def gather(b, half):
                for t in range(4 * half, 4 * half + 4):
                    for n in range(2):
                        ins = nc.tensor.matmul(ps_g[:, 0:GW], pmat[:, b, t, :], xr[n][:, t, :],
                                               start=t == 0 and n == 0, stop=t == NT - 1 and n == 1,
                                               skip_group_check=True)
                return ins

            def scatter(b, half):
                for t in range(4 * half, 4 * half + 4):
                    for n in range(2):
                        ins = nc.tensor.matmul(y[:, t, :], pmT[:, b, t * P:(t + 1) * P], eo[n][:],
                                               start=False, stop=False, skip_group_check=True)
                return ins

            pe.wait_ge(ring_dve, ring_reads(RNAMES[-1], "dve"))
            pe.wait_ge(rows_lo, 3)
            pe.wait_ge(pm_ready, after(0, 2, 1))
            gather(0, 0)
            gather(0, 1).then_inc(g_full, 1)

            def step2(i, b, first, last):
                n = b + 1

                def slots_row(h):
                    pe.wait_ge(pmt_ready, after(i, 4, 2 * b + h))
                    pe.sem_inc(held, 1)
                    nc.tensor.matmul(ps_b, sel[:, bass.ds(i * 2 + b, 1), :].rearrange("p a c -> p (a c)"),
                                     slotT[:, h * 512:(h + 1) * 512], start=True, stop=True).then_inc(sb_full, 1)

                pe.wait_ge(xg_copied, after(i, 2, n))
                pe.wait_ge(mt_lo, after(i, 2, b))
                for k in range(KC):
                    ins = nc.tensor.transpose(ps_x[:, k * P:(k + 1) * P], xg[:, k * P:(k + 1) * P], ident[:])
                ins.then_inc(xt_full, 1)
                slots_row(0)
                pe.wait_ge(eo_lo, after(i, 2, b))
                if not first:
                    pe.wait_ge(pmt_ready, after(i, 4, 2 * b))
                    scatter(1 - b, 0)
                pe.wait_ge(xgt_lo, after(i, 2, n))
                pe.wait_ge(ew_lo, i * 2 + (b + 2))
                for k in range(KC):
                    ins = three(ps_f[:, 0:2 * ID], [xgT[m][:, k, :] for m in range(2)],
                                [egw[m][:, b, k].rearrange("p g n -> p (g n)") for m in range(2)], k == 0, k == KC - 1)
                ins.then_inc(f1_full, 1)
                slots_row(1)
                if not first:
                    scatter(1 - b, 1).then_inc(sc_done, 1)
                else:
                    pe.sem_inc(sc_done, 1)
                pe.wait_ge(mid_ready, after(i, 2, n))
                for c in range(2):
                    ins = nc.tensor.transpose(ps_x[0:IC, c * CAP:(c + 1) * CAP], mid[:, c * IC:(c + 1) * IC], ident[:])
                ins.then_inc(mt_full, 1)
                if not last:
                    pe.wait_ge(pm_ready, after(i, 2, n + 1))
                    gather(1 - b, 0)
                pe.wait_ge(mt_lo, after(i, 2, n))
                for c in range(2):
                    ins = three(ps_f[:, 0:H], [midT[m][:, c, :] for m in range(2)],
                                [edw[m][:, b, c, :] for m in range(2)], c == 0, c == 1)
                ins.then_inc(f2_full, 1)
                if not last:
                    gather(1 - b, 1).then_inc(g_full, 1)

            step2(0, 0, True, False)
            step2(0, 1, False, False)
            with pe.Fori(1, EXPERTS // 2 - 1) as i:
                step2(i, 0, False, False)
                step2(i, 1, False, False)
            step2(EXPERTS // 2 - 1, 0, False, False)
            step2(EXPERTS // 2 - 1, 1, False, True)
            pe.wait_ge(eo_lo, after(EXPERTS // 2 - 1, 2, 2))
            pe.wait_ge(pmt_ready, after(EXPERTS // 2 - 1, 4, 4))
            pe.wait_ge(rw_ready, 2)
            for h in range(2):
                scatter(1, h)
                for t in range(4 * h, 4 * h + 4):
                    for c in range(KC):
                        ins = nc.tensor.matmul(y[:, t, c * P:(c + 1) * P], av[:, c, t * P:(t + 1) * P], ident[:],
                                               start=False, stop=t % 2 == 1 and c == KC - 1, skip_group_check=True)
                ins.then_inc(y_done, 1)

        @block.vector
        def _(dve):
            for s_, per in ((stage_read_dve, ND), (smax_done, NS), (p_norm, NS), (recip_done, NS), (gmin_done, 2),
                            (grecip_done, 2), (pg_ready, 2), (pt_lo, NP), (out_lo, 2), (clip_done, 4),
                            (glu_done, 4), (h_ready, 4), (h_lo, 4), (w_lo, 4)):
                dve.sem_inc(s_, per)
            seq = 0

            def step(ins):
                nonlocal seq
                ins.then_inc(vseq, 1)
                seq += 1
                dve.wait_ge(vseq, seq)

            V = nc.vector
            for n in range(2):
                for ap in (xT[n][:, :, 0:HALF], xT[n][:, :, HALF + T:TP], kw[n][:, 0, 0:HALF],
                           kw[n][:, NT - 1, WIN - HALF:WIN]):
                    V.memset(ap.bitcast(F32), 0.0)
            V.memset(pr[:, :, KW:2 * P], 0.0)
            V.memset(pg[:, 0:HALF], 0.0)
            step(V.memset(pg[:, HALF + T:TP], 0.0))

            def layer_norm(xn, sq):
                for t in range(NT):
                    V.bn_stats(stats[:, t, :], acc[:, t, :])
                step(V.memset(small[:, 0:1], 0.0))
                for t in range(NT):
                    V.bn_aggr(mv[:, t, :], stats[:, t, :])
                step(V.memset(small[:, 0:1], 0.0))
                V.tensor_scalar(sd[:, 0], mv[:, :, 1], EPS, None, ALU.add).then_inc(sqrt_done, 1)
                dve.wait_ge(sqrt_done, sq)
                step(V.reciprocal(sd[:, 2], sd[:, 1]))
                step(V.tensor_tensor(sd[:, 3], sd[:, 0], sd[:, 2], ALU.mult))
                step(V.tensor_tensor(sd[:, 2], sd[:, 3], sd[:, 1], ALU.add))
                step(V.tensor_scalar(sd[:, 3], sd[:, 2], 0.5, None, ALU.mult))
                step(V.reciprocal(sd[:, 2], sd[:, 3]))
                for t in range(NT):
                    V.tensor_scalar(xn[:, t, :], acc[:, t, :], mv[:, t, 0:1], sd[:, 2, t:t + 1],
                                    ALU.subtract, ALU.mult).then_inc(xn_ready, 1)

            dve.wait_ge(x_in, 16)
            layer_norm(xn, 2)
            for k in range(KC):
                dve.wait_ge(xT_hi, k + 1)
                V.tensor_tensor(xT[1][:, k, HALF:HALF + T], stage[:, k, :],
                                xT[0][:, k, HALF:HALF + T].bitcast(F32), ALU.subtract).then_inc(xT_lo, 1)
            dve.wait_ge(small_hi, 1)
            V.tensor_tensor(rwT[1][:], ps_s[:, 0:KC * EXPERTS].rearrange("p (k e) -> p k e", k=KC),
                            rwT[0][:].bitcast(F32), ALU.subtract).then_inc(rwT_ready, 1)
            b0 = KC * EXPERTS
            V.tensor_copy(ebias[:, 0], ps_s[:, b0:b0 + 2 * EXPERTS].rearrange("p (c e) -> p c e", c=2))
            step(V.tensor_scalar(ebias[:, 1], ps_s[:, b0 + 2 * EXPERTS:b0 + 4 * EXPERTS].rearrange(
                "p (c e) -> p c e", c=2), 1.0, 0.5, ALU.add, ALU.mult))

            def split_lo(i, n, piece):
                dve.wait_ge(w_hi, after(i, NW, n + 1))
                V.tensor_tensor(piece[1], piece[2], piece[0].bitcast(F32), ALU.subtract).then_inc(w_lo, 1)

            def next_piece(i, n):
                split_lo(i, 4 + n, (expert_pieces(0) + qkv_pieces)[n])

            for n in range(6):
                next_piece(-1, n)

            dve.wait_ge(consts, 2)
            dve.wait_ge(logits_full, 1)
            step(V.tensor_tensor(lg[:], ps_t[:, 0:NT * EXPERTS].rearrange("p (t e) -> p t e", t=NT),
                                 rb_bc[:].unsqueeze(1).broadcast_to([P, NT, EXPERTS]), ALU.add))
            for t in range(NT):
                V.max(top8[:, t, :], lg[:, t, :])
            step(V.memset(small[:, 0:1], 0.0))
            for t in range(NT):
                V.max_index(topi[:, t, :], top8[:, t, :], lg[:, t, :])
            V.tensor_tensor(topw[:], top8[:, :, 0:TOPK], top8[:, :, 0:1].broadcast_to([P, NT, TOPK]),
                            ALU.subtract).then_inc(top_sub, 1)
            step(V.memset(small[:, 0:1], 0.0))
            step(V.tensor_copy(topif[:], topi[:, :, 0:TOPK]))
            dve.wait_ge(top_exp, 1)
            step(V.tensor_reduce(rsum[:], topw[:], AX_X, ALU.add))
            step(V.reciprocal(rsum[:], rsum[:]))
            step(V.tensor_tensor(topw[:], topw[:], rsum[:].unsqueeze(2).broadcast_to([P, NT, TOPK]), ALU.mult))
            sc_te = scores[:].rearrange("p e t -> p t e")
            for n in range(TOPK):
                dst = sc_te if n == 0 else onehot[:]
                step(V.tensor_tensor(dst, iota16[:].unsqueeze(1).broadcast_to([P, NT, EXPERTS]),
                                     topif[:, :, n:n + 1].broadcast_to([P, NT, EXPERTS]), ALU.is_equal))
                step(V.tensor_tensor(dst, dst, topw[:, :, n:n + 1].broadcast_to([P, NT, EXPERTS]), ALU.mult))
                if n:
                    step(V.tensor_tensor(sc_te, sc_te, onehot[:], ALU.add))
            V.memset(small[:, 0:1], 0.0).then_inc(scores_ready, 1)
            dve.wait_ge(scT_full, 1)
            V.tensor_copy(scT, ps_o[0:EXPERTS, :]).then_inc(scT_ready, 1)
            dve.wait_ge(bias_full, 1)
            V.tensor_tensor(acc[:], acc[:], stage[:].rearrange("p a (b h) -> p (a b) h", h=H), ALU.add)\
                .then_inc(acc_ready, 1)

            def body(i, more):
                def qk(j):
                    dve.wait_ge(qkv_hi, after(i, 8, 1 if j == 0 else 7))
                    V.scalar_tensor_tensor(qT[1][:], stage_of(f"q{j}"), -SCALE, qT[0][:].bitcast(F32),
                                           ALU.mult, ALU.subtract).then_inc(stage_read_dve, 1)
                    dve.wait_ge(qkv_hi, after(i, 8, 2 if j == 0 else 8))
                    pieces = k_windows(kw[0], stage_of(f"k{j}"))
                    lows = k_windows(kw[1], stage_of(f"k{j}"))
                    for (hi, src), (lo, _) in zip(pieces, lows):
                        ins = V.tensor_tensor(lo, src, hi.bitcast(F32), ALU.subtract)
                    ins.then_inc(stage_read_dve, 1)

                def values():
                    for v, (a, b) in enumerate(V_TILES):
                        dve.wait_ge(qkv_hi, after(i, 8, 3 + v))
                        src = stage_of(f"v{v}")[:, 0:(b - a) * 2 * HD].rearrange("p (t n) -> p t n", n=2 * HD)
                        V.tensor_tensor(vp[1][:, a:b, :], src, vp[0][:, a:b, :].bitcast(F32), ALU.subtract)\
                            .then_inc(stage_read_dve, 1)

                def head(j):
                    for s in range(NT + 3):
                        if s == 0:
                            dve.wait_ge(stage_full, full(i, f"sg{j}"))
                            V.tensor_reduce(gm[:, 0:1], stage_of(f"sg{j}")[0:GLOBALS, :], AX_X, ALU.min)\
                                .then_inc(gmin_done, 1)
                        if s < NT:
                            n = NT * j + s
                            dve.wait_ge(scores_full, after(i, NS, n + 1))
                            dve.wait_ge(exp_done, after(i, NS, n - 1))
                            dve.sem_inc(held, 1)
                            V.tensor_tensor_reduce(sm[:, n % 2, :], ps_s[:, 0:KW],
                                                   mask[:, 0 if s == 0 else 2 if s == NT - 1 else 1, :],
                                                   1.0, 3e38, ALU.add, ALU.min, nm[:, n % 2:n % 2 + 1])\
                                .then_inc(smax_done, 1)
                        if 1 <= s <= NT:
                            n = NT * j + s - 1
                            dve.wait_ge(exp_done, after(i, NS, n + 1))
                            V.reciprocal(rr[:, n % 2:n % 2 + 1], rs[:, n % 2:n % 2 + 1]).then_inc(recip_done, 1)
                            dve.wait_ge(recip_done, after(i, NS, n + 1))
                            V.tensor_scalar(pr[:, n % 2, 0:KW], pr[:, n % 2, 0:KW], rr[:, n % 2:n % 2 + 1], None,
                                            ALU.mult).then_inc(p_norm, 1)
                        if s == 1:
                            dve.wait_ge(stage_read_act, read_act(i, f"sg{j}"))
                            V.reciprocal(gr[:, 0:1], gs[:, 0:1]).then_inc(grecip_done, 1)
                            dve.wait_ge(grecip_done, after(i, 2, j + 1))
                            V.tensor_scalar(pg[:, HALF:HALF + T], pg[:, HALF:HALF + T], gr[:, 0:1], None,
                                            ALU.mult).then_inc(pg_ready, 1)
                        for c in range(2):
                            e = 2 * j + c
                            if s == 2 + 4 * c:
                                dve.wait_ge(stage_full, full(i, f"gate{c}{j}"))
                                V.tensor_scalar(ff[:, 0], stage_of(f"gate{c}{j}"),
                                                ebias[:, 0, c, bass.ds(i * 2 + j, 1)], LIMIT, ALU.add, ALU.min)\
                                    .then_inc(stage_read_dve, 1)
                            if s == 4 + 4 * c:
                                dve.wait_ge(tanh_done, after(i, 4, e + 1))
                                V.scalar_tensor_tensor(ff[:, 1], ff[:, 1], 1.0, ff[:, 0], ALU.add, ALU.mult)\
                                    .then_inc(glu_done, 1)
                                dve.wait_ge(stage_read_act, read_act(i, f"up{c}{j}"))
                                V.tensor_scalar(ff[:, 2], ff[:, 2], (LIMIT + 1) / 2, (1 - LIMIT) / 2,
                                                ALU.min, ALU.max).then_inc(clip_done, 1)
                                dve.wait_ge(glu_done, after(i, 4, e + 1))
                                dve.wait_ge(clip_done, after(i, 4, e + 1))
                                V.tensor_tensor(ff[:, 2], ff[:, 2], ff[:, 1], ALU.mult).then_inc(h_ready, 1)
                            if s == 5 + 4 * c:
                                dve.wait_ge(h_hi, after(i, 4, e + 1))
                                V.tensor_tensor(hh[1][:, c], ff[:, 2], hh[0][:, c].bitcast(F32), ALU.subtract)\
                                    .then_inc(h_lo, 1)
                        if 1 <= s <= NT + 1:
                            m = 9 * j + s - 1
                            w = 2 * P if s <= NT else VT * GLOBALS
                            dve.wait_ge(pt_hi, after(i, NP, m + 1))
                            V.tensor_tensor(pT[1][:, m % 3, 0:w], ps_t[:, 0:w],
                                            pT[0][:, m % 3, 0:w].bitcast(F32), ALU.subtract).then_inc(pt_lo, 1)
                        if j == 0:
                            if s in (0, 1, 3):
                                n = {0: 0, 1: 1, 3: 2}[s]
                                split_lo(i, n, expert_pieces(1)[n])
                            if s == 7:
                                split_lo(i, 3, wo_piece)
                        elif more and s in (0, 1, 3, 7, 9, 10):
                            next_piece(i, {0: 0, 1: 1, 3: 2, 7: 3, 9: 4, 10: 5}[s])
                    dve.wait_ge(out_hi, after(i, 2, j + 1))
                    V.tensor_tensor(oT[1][:, j], ps_o[:], oT[0][:, j].bitcast(F32), ALU.subtract).then_inc(out_lo, 1)

                def down(j):
                    for q in range(2):
                        dve.wait_ge(stage_full, full(i, f"down{q}{j}"))
                        dve.wait_ge(stage_read_dve, (after(i, ND, 0) if j == 0 else read_dve(i, "down10")))
                        for t in range(4):
                            tt = 4 * q + t
                            ins = V.scalar_tensor_tensor(acc[:, tt, :], stage_of(f"down{q}{j}")[:, t * H:(t + 1) * H],
                                                         scores[:, bass.ds(i * 2 + j, 1), tt], acc[:, tt, :],
                                                         ALU.mult, ALU.add)
                        ins.then_inc(stage_read_dve, 1)

                qk(0)
                values()
                head(0)
                qk(1)
                down(0)
                head(1)
                down(1)
                dve.wait_ge(stage_read_dve, read_dve(i, "down11"))
                for q in range(2):
                    dve.wait_ge(stage_full, full(i, f"wo{q}"))
                    V.tensor_tensor(acc[:, 4 * q:4 * q + 4, :], acc[:, 4 * q:4 * q + 4, :],
                                    stage_of(f"wo{q}").rearrange("p (t h) -> p t h", h=H), ALU.add)\
                        .then_inc(stage_read_dve, 1)

            with dve.Fori(0, PAIRS - 1) as i:
                body(i, True)
            body(PAIRS - 1, False)


            for s_, per in ((pm_ready, 2), (xgt_lo, 2), (pmt_ready, 4), (gs2_done, 2), (mid_ready, 2), (mt_lo, 2),
                            (eo_lo, 2), (wsc_ready, 2)):
                dve.sem_inc(s_, per)
            dve.wait_ge(stage_read_dve, read_dve(PAIRS - 1, "wo1"))
            layer_norm(xn2, 4)
            V.memset(x2T[0][:, :, 0:1].bitcast(F32), 0.0)
            V.memset(slotT[:], 0.0)
            V.memset(x2T[1][:, :, 0:1].bitcast(F32), 0.0).then_inc(zeros2, 1)

            def ring_lo(u, dst, src, hi):
                dve.wait_ge(ring_hi, [v for v, r in RING if r == "dve"].index(u) + 1)
                V.tensor_tensor(dst, src, hi.bitcast(F32), ALU.subtract).then_inc(ring_dve, 1)

            for n, u in enumerate(("wkT", "wvT", "wrT")):
                ring_lo(u, kvrT[1][:, n], ring_of(u).rearrange("p (k e) -> p k e", k=KC), kvrT[0][:, n])
            ring_lo("gwT", gwT[1][:], ring_of("gwT")[:, 0:KC * EXPERTS].rearrange("p (k e) -> p k e", k=KC), gwT[0][:])
            for k in range(KC):
                for h in range(2):
                    cols = slice(1 + h * 512, 1 + (h + 1) * 512)
                    ring_lo(f"xT{k}{h}", x2T[1][:, k, cols], ring_of(f"xT{k}{h}"), x2T[0][:, k, cols])

            dve.wait_ge(ring_full, RNAMES.index("logits") + 1)
            V.tensor_copy(lg[:], ring_of("logits")[:, 0:NT * EXPERTS].rearrange("p (t e) -> p t e", t=NT))\
                .then_inc(ring_dve, 1)
            dve.wait_ge(ring_dve, ring_reads("logits", "dve"))
            for t in range(NT):
                V.max(top8[:, t, :], lg[:, t, :])
            step(V.memset(small[:, 0:1], 0.0))
            V.tensor_tensor(topw[:], top8[:, :, 0:TOPK], top8[:, :, 0:1].broadcast_to([P, NT, TOPK]), ALU.subtract)
            V.tensor_tensor(alls[:], lg[:], top8[:, :, 0:1].broadcast_to([P, NT, EXPERTS]),
                            ALU.subtract).then_inc(l1_sub, 1)
            for t in range(NT):
                V.max_index(topi[:, t, :], top8[:, t, :], lg[:, t, :])
            for h in range(2):
                dve.wait_ge(rows_hi, h + 1)
                V.tensor_tensor(xr[1][:, 4 * h:4 * h + 4, 0:H], xn2[:, 4 * h:4 * h + 4, :],
                                xr[0][:, 4 * h:4 * h + 4, 0:H].bitcast(F32), ALU.subtract).then_inc(rows_lo, 1)
            dve.wait_ge(rows_lo, 2)
            step(V.tensor_copy(topif[:], topi[:, :, 0:TOPK]))
            dve.wait_ge(l1_exp, 1)
            step(V.tensor_reduce(rsum[:], alls[:], AX_X, ALU.add))
            step(V.reciprocal(rsum[:], rsum[:]))
            step(V.tensor_tensor(topw[:], topw[:], rsum[:].unsqueeze(2).broadcast_to([P, NT, TOPK]), ALU.mult))
            step(V.tensor_reduce(rsum[:], topw[:], AX_X, ALU.add))
            step(V.tensor_scalar(rsum[:], rsum[:], 1e-20, None, ALU.add))
            step(V.reciprocal(rsum[:], rsum[:]))
            step(V.tensor_tensor(topw[:], topw[:], rsum[:].unsqueeze(2).broadcast_to([P, NT, TOPK]), ALU.mult))
            for n in range(TOPK):
                one, weighted = (chosen, w16) if n == 0 else (onehot, alls)
                step(V.tensor_tensor(one[:], iota16[:].unsqueeze(1).broadcast_to([P, NT, EXPERTS]),
                                     topif[:, :, n:n + 1].broadcast_to([P, NT, EXPERTS]), ALU.is_equal))
                step(V.tensor_tensor(weighted[:], one[:], topw[:, :, n:n + 1].broadcast_to([P, NT, EXPERTS]), ALU.mult))
                if n:
                    V.tensor_tensor(chosen[:], chosen[:], onehot[:], ALU.add)
                    step(V.tensor_tensor(w16[:], w16[:], alls[:], ALU.add))
            V.tensor_copy(chosen_b[:], chosen[:]).then_inc(chosen_ready, 1)
            step(V.tensor_copy(xr[0][:, :, H:GW], w16[:]))
            V.tensor_tensor(xr[1][:, :, H:GW], w16[:], xr[0][:, :, H:GW].bitcast(F32), ALU.subtract)\
                .then_inc(rows_lo, 1)
            for g in range(2):
                dve.wait_ge(l1_w_hi, g + 1)
                V.tensor_tensor(sgu[1][:, g], sgu_raw[:, g], sgu[0][:, g].bitcast(F32), ALU.subtract).then_inc(l1_w_lo, 1)
            dve.wait_ge(ring_full, RNAMES.index("pos") + 1)
            slot_te = slot[:].rearrange("p e t -> p t e")
            V.scalar_tensor_tensor(slot_te, ring_of("pos")[:, 0:NT * EXPERTS].rearrange("p (t e) -> p t e", t=NT),
                                   -NONE, chosen[:], ALU.add, ALU.mult).then_inc(ring_dve, 1)
            dve.wait_ge(ring_dve, ring_reads("pos", "dve"))
            V.tensor_scalar(slot[:], slot[:], NONE, None, ALU.add).then_inc(slots_ready, 1)

            def shared_lo(n):
                c, h = n // 2, n % 2
                w = S_CHUNKS[c][1] - S_CHUNKS[c][0]
                dve.wait_ge(sT_hi, n + 1)
                hi = sT[0][0:w, c, h * 512:(h + 1) * 512]
                V.tensor_tensor(sT[1][0:w, c, h * 512:(h + 1) * 512], st[0:w, n % 2], hi.bitcast(F32), ALU.subtract)\
                    .then_inc(sT_lo, 1)

            def shared_unit(n):
                c, h = n // 2, n % 2
                w = S_CHUNKS[c][1] - S_CHUNKS[c][0]
                dve.wait_ge(st_tanh, n + 1)
                V.scalar_tensor_tensor(st[0:w, n % 2], st[0:w, n % 2], 1.0, ring_of(f"sg{c}{h}")[0:w, :],
                                       ALU.add, ALU.mult).then_inc(ring_dve, 1)
                dve.wait_ge(ring_dve, ring_reads(f"sg{c}{h}", "dve"))
                dve.wait_ge(ring_full, RNAMES.index(f"su{c}{h}") + 1)
                V.scalar_tensor_tensor(st[0:w, n % 2], st[0:w, n % 2], 0.5, ring_of(f"su{c}{h}")[0:w, :],
                                       ALU.mult, ALU.mult).then_inc(ring_dve, 1)
                dve.wait_ge(ring_dve, ring_reads(f"su{c}{h}", "dve"))
                V.memset(small[:, 1:2], 0.0).then_inc(smid_done, 1)

            for n in range(4):
                shared_unit(n)
                if n:
                    shared_lo(n - 1)
            dve.wait_ge(l1_w_hi, 3)
            V.tensor_tensor(sdw[1][:, 0:2], sd_raw[:, 0:2], sdw[0][:, 0:2].bitcast(F32), ALU.subtract)
            V.tensor_tensor(sdw[1][0:SD - 2 * P, 2], sd_raw[0:SD - 2 * P, 2], sdw[0][0:SD - 2 * P, 2].bitcast(F32),
                            ALU.subtract).then_inc(l1_w_lo, 1)
            dve.wait_ge(zeros2, 1)
            for h in range(2):
                dve.wait_ge(ring_full, RNAMES.index(f"slots{h}") + 1)
                V.tensor_copy(slotT[0:EXPERTS, h * 512:(h + 1) * 512], ring_of(f"slots{h}")[0:EXPERTS, :])\
                    .then_inc(ring_dve, 1)
            shared_lo(3)

            def slot_matrix(e, b):
                row = slot[:, e, :] if isinstance(e, int) else slot[:, bass.ds(e, 1), :].rearrange("p a t -> p (a t)")
                V.tensor_tensor(pmat[:, b], iota_c[:].unsqueeze(1).broadcast_to([P, NT, CAP]),
                                row.unsqueeze(2).broadcast_to([P, NT, CAP]), ALU.is_equal).then_inc(pm_ready, 1)

            dve.wait_ge(slots_ready, 1)
            slot_matrix(0, 0)
            for n in (4, 5):
                shared_unit(n)
                if n == 5:
                    shared_lo(4)
            shared_lo(5)

            dve.wait_ge(ring_act, ring_reads("r11", "act"))
            dve.wait_ge(decay_ready, 1)
            for c in range(KC):
                w = decay[:, c:c + 1].broadcast_to([P, T])
                V.tensor_tensor_scan(den[:, c], w, ek[:, c], 0.0, ALU.mult, ALU.add)
                step(V.tensor_tensor(av[:, c], av[:, c], ek[:, c], ALU.mult))
                step(V.tensor_tensor_scan(ek[:, c], w, av[:, c], 0.0, ALU.mult, ALU.add))
                step(V.tensor_scalar(den[:, c], den[:, c], 1e-8, None, ALU.add))
                step(V.reciprocal(den[:, c], den[:, c]))
                step(V.tensor_tensor(ek[:, c], ek[:, c], rT[:, c], ALU.mult))
                V.tensor_tensor(av[:, c], ek[:, c], den[:, c], ALU.mult).then_inc(rw_ready, 1)

            def step2(i, b, last):
                n = b + 1
                dve.wait_ge(xg_copied, after(i, 2, n))
                V.tensor_scalar(wsc[:], xg[:, bass.ds(i * 2 + (H + b), 1)], 0.5, None, ALU.mult).then_inc(wsc_ready, 1)
                dve.wait_ge(xgt_hi, after(i, 2, n))
                V.tensor_tensor(xgT[1][:], ps_x[:, 0:H].rearrange("p (k c) -> p k c", k=KC), xgT[0][:].bitcast(F32),
                                ALU.subtract).then_inc(xgt_lo, 1)
                if not last:
                    dve.wait_ge(g_full, after(i, 2, b))
                    slot_matrix(i * 2 + (b + 1), 1 - b)

                def transposed(h):
                    dve.wait_ge(sb_full, after(i, 4, 2 * b + h + 1))
                    dve.wait_ge(sc_done, after(i, 2, b - 1))
                    V.tensor_scalar(pmT[:, b, h * 512:(h + 1) * 512], ps_b, iota_p[:, 0:1], None, ALU.is_equal)\
                        .then_inc(pmt_ready, 1)

                transposed(0)
                dve.wait_ge(tanh2_done, after(i, 2, n))
                V.scalar_tensor_tensor(gs2[:], tt2[:], 1.0, ps_f[:, 0:ID], ALU.add, ALU.mult).then_inc(gs2_done, 1)
                dve.wait_ge(gs2_done, after(i, 2, n))
                dve.wait_ge(wsc_ready, after(i, 2, n))
                dve.wait_ge(mt_full, after(i, 2, b))
                V.scalar_tensor_tensor(mid[:], gs2[:], wsc[:, 0:1], ps_f[:, ID:2 * ID], ALU.mult, ALU.mult)\
                    .then_inc(mid_ready, 1)
                transposed(1)
                dve.wait_ge(mt_hi, after(i, 2, n))
                V.tensor_tensor(midT[1][:], ps_x[0:IC, 0:2 * CAP].rearrange("p (c t) -> p c t", c=2),
                                midT[0][:].bitcast(F32), ALU.subtract).then_inc(mt_lo, 1)
                dve.wait_ge(eo_hi, after(i, 2, n))
                V.tensor_tensor(eo[1][:], ps_f[:, 0:H], eo[0][:].bitcast(F32), ALU.subtract).then_inc(eo_lo, 1)

            with dve.Fori(0, EXPERTS // 2 - 1) as i:
                step2(i, 0, False)
                step2(i, 1, False)
            step2(EXPERTS // 2 - 1, 0, False)
            step2(EXPERTS // 2 - 1, 1, True)
            for q in range(2):
                dve.wait_ge(y_done, q + 1)
                V.tensor_tensor(acc[:, 4 * q:4 * q + 4, :], acc[:, 4 * q:4 * q + 4, :], y[:, 4 * q:4 * q + 4, :],
                                ALU.add).then_inc(out_ready, 1)


_INS = ['L0_attn_hidden_states', 'L0_attn_Wq', 'L0_attn_Wk', 'L0_attn_Wv', 'L0_attn_Wo', 'L0_ffn_router_weight',
        'L0_ffn_router_bias', 'L0_ffn_gate_up_proj', 'L0_ffn_gate_up_proj_bias', 'L0_ffn_down_proj',
        'L0_ffn_down_proj_bias']
_L1 = ['L1_attn_Wk', 'L1_attn_Wv', 'L1_attn_Wr', 'L1_attn_time_decay', 'L1_ffn_gate_w', 'L1_ffn_w_gate',
       'L1_ffn_w_up', 'L1_ffn_w_down', 'L1_ffn_sw_gate', 'L1_ffn_sw_up', 'L1_ffn_sw_down']


def kernel(**inputs):
    import numpy as np
    import concourse.bacc as bacc
    from concourse.bass_utils import run_bass_kernel_spmd as run

    nc = bacc.Bacc("TRN2", target_bir_lowering=False, num_devices=1)
    arrays, aps = {}, {}
    for name in _INS + _L1:
        a = np.ascontiguousarray(inputs[name])
        arrays[f"in_{name}"] = a
        aps[name] = nc.dram_tensor(f"in_{name}", a.shape, mybir.dt.from_np(a.dtype), kind="ExternalInput").ap()
    out = nc.dram_tensor("out_x", (1, T, H), F32, kind="ExternalOutput").ap()
    build(nc, aps[_INS[0]][0], *[aps[n] for n in _INS[1:]], {n.split('_', 2)[2]: aps[n] for n in _L1}, out[0])
    r = run(nc, [arrays], core_ids=[0])
    return r.results[0]["out_x"]
```

```python
from contextlib import ExitStack

import concourse.bass as bass
from concourse import mybir

F32 = mybir.dt.float32
F32R = mybir.dt.float32r
BF16 = mybir.dt.bfloat16
U32 = mybir.dt.uint32
ALU = mybir.AluOpType
ACT = mybir.ActivationFunctionType
AX_X = mybir.AxisListType.X

P = 128
T, H = 1024, 256
NT, KC = T // P, H // P
HEADS, HD = 16, 128
PAIRS = HEADS // 2
WINDOW, GLOBALS = 64, 16
HALF = WINDOW // 2
SCALE = HD ** -0.5
WIN = P + WINDOW
KW = WIN + GLOBALS
VT = NT + 1
TP = VT * P
KB = WIN - P + GLOBALS
EXPERTS, FD, TOPK = 16, 256, 4
ALPHA, LIMIT = 1.702, 7.0
EPS = 1e-5
OUTSIDE = 1e30

UNITS = (["sg0", "gate00", "up00", "gate10", "up10", "q1", "k1", "down00", "down10",
          "sg1", "gate01", "up01", "gate11", "up11", "q0", "k0", "v0", "v1", "v2", "v3", "down01", "down11",
          "wo0", "wo1"])
NEXT = 6
LATE = 4
NU = len(UNITS)
BY_ACT = [u for u in UNITS if u[:2] in ("sg", "up")]
BY_DVE = [u for u in UNITS if u not in BY_ACT]
NA, ND = len(BY_ACT), len(BY_DVE)
V_TILES = [(0, 3), (3, 5), (5, 7), (7, 9)]
NS = 2 * NT
NP = NS + 1
GR = HALF + GLOBALS
NW = 10

ID = 176
IC = ID // 2
SD = 352
S_CHUNKS = [(0, 128), (128, 256), (256, 352)]
CAP = 128
GW = H + EXPERTS
NONE = 999.0
RING = ([(u, "dve") for u in ("wkT", "wvT", "wrT", "gwT", "xT00", "xT01", "xT10", "xT11", "logits")] +
        [(f"{u}{c}{h}", "act") for c in range(2) for u in "kvr" for h in range(2)] +
        [("pos", "dve")] +
        [(f"{u}{c}{h}", "dve") for c in range(2) for h in range(2) for u in ("sg", "su")] +
        [("slots0", "dve"), ("slots1", "dve")] +
        [(f"{u}2{h}", "dve") for h in range(2) for u in ("sg", "su")])
RNAMES = [u for u, _ in RING]


def after(i, per, n):
    return i * per + (per + n)


def full(i, u):
    return after(i, NU, UNITS.index(u) + 1)


def read_dve(i, u):
    return after(i, ND, BY_DVE.index(u) + 1)


def read_act(i, u):
    return after(i, NA, BY_ACT.index(u) + 1)


def ring_reads(u, reader):
    return sum(r == reader for _, r in RING[:RNAMES.index(u) + 1])


def build(nc, x, wq, wk, wv, wo, rw, rb, gup, gub, dnp, dnb, l1, out):
    with ExitStack() as ctx:
        def sb(name, shape, dt=F32, c=ctx):
            return c.enter_context(nc.sbuf_tensor(name, shape, dt))

        def sem(name):
            return ctx.enter_context(nc.semaphore(name))

        ident = sb("ident", [P, P])
        acc = sb("acc", [P, NT, H])
        iota16 = sb("iota16", [P, EXPERTS])
        top8 = sb("top8", [P, NT, 8])
        topi = sb("topi", [P, NT, 8], U32)
        topif = sb("topif", [P, NT, TOPK])
        topw = sb("topw", [P, NT, TOPK])
        onehot = sb("onehot", [P, NT, EXPERTS])
        stats = sb("stats", [P, NT, 6])
        mv = sb("mv", [P, NT, 2])
        sd = sb("sd", [P, 4, NT])
        lg = sb("lg", [P, NT, EXPERTS])
        scores = sb("scores", [P, EXPERTS, NT])
        rsum = sb("rsum", [P, NT])
        small = sb("small", [P, 8])

        l0 = ctx.enter_context(ExitStack())
        s0 = lambda name, shape, dt=F32: sb(name, shape, dt, l0)
        mask = s0("mask", [P, 3, KW])
        rb_bc = s0("rb_bc", [P, EXPERTS])
        rw_raw = s0("rw_raw", [EXPERTS, H])
        rwT = [s0(f"rwT{n}", [P, KC, EXPERTS], F32R) for n in "hl"]
        gub_raw = s0("gub_raw", [EXPERTS, 2 * FD])
        ebias = s0("ebias", [P, 2, 2, EXPERTS])
        dnb_sb = s0("dnb_sb", [EXPERTS, H])
        xT = [s0(f"xT{n}", [P, KC, TP], F32R) for n in "hl"]
        qT = [s0(f"qT{n}", [P, HALF + T], F32R) for n in "hl"]
        kw = [s0(f"kw{n}", [P, NT, KW], F32R) for n in "hl"]
        vp = [s0(f"vp{n}", [P, VT, 2 * HD], F32R) for n in "hl"]
        vb = [s0(f"vb{n}", [P, NT, 2 * HD], F32R) for n in "hl"]
        sm = s0("sm", [P, 2, KW])
        pr = s0("pr", [P, 2, 2 * P])
        nm = s0("nm", [P, 2])
        rs = s0("rs", [P, 2])
        rr = s0("rr", [P, 2])
        gm = s0("gm", [GR, 1])
        gs = s0("gs", [GR, 1])
        gr = s0("gr", [GR, 1])
        pg = s0("pg", [GR, TP])
        pgT = s0("pgT", [P, VT, 2, GR], F32R)
        og = s0("og", [2 * GR, 2 * HD])
        og_sum = s0("og_sum", [2 * GR, 2, GLOBALS])
        pT = [s0(f"pT{n}", [P, 2, 2 * P], F32R) for n in "hl"]
        oT = [s0(f"oT{n}", [P, 2, T], F32R) for n in "hl"]
        qkv_raw = s0("qkv_raw", [P, 3, KC, 2 * HD])
        wo_raw = s0("wo_raw", [P, 2, H])
        gu_raw = s0("gu_raw", [P, KC, 2 * FD])
        dn_raw = s0("dn_raw", [P, 2, H])
        qkvw = [s0(f"qkvw{n}", [P, 3, KC, 2 * HD], F32R) for n in "hl"]
        wow = [s0(f"wow{n}", [P, 2, H], F32R) for n in "hl"]
        guw = [s0(f"guw{n}", [P, 2, KC, 2, FD], F32R) for n in "hl"]
        dnw = [s0(f"dnw{n}", [P, 2, 2, H], F32R) for n in "hl"]
        ff = s0("ff", [P, 3, T])
        hh = [s0(f"hh{n}", [P, 2, T], F32R) for n in "hl"]
        xn = ff[:, 0:2, :].rearrange("p a (b h) -> p (a b) h", h=H)
        scT = ff[0:EXPERTS, 2, :]

        l0.close()

        gw_raw = sb("gw_raw", [EXPERTS, H])
        gwT = [sb(f"gwT{n}", [P, KC, EXPERTS], F32R) for n in "hl"]
        td = sb("td", [P, KC])
        decay = sb("decay", [P, KC])
        xr = [sb(f"xr{n}", [P, NT, GW], F32R) for n in "hl"]
        x2T = [sb(f"x2T{n}", [P, KC, T + 2], F32R) for n in "hl"]
        kvr_raw = sb("kvr_raw", [P, 3, KC, H])
        kvrT = [sb(f"kvrT{n}", [P, 3, KC, H], F32R) for n in "hl"]
        sgu_raw = sb("sgu_raw", [P, 2, KC, SD])
        sgu = [sb(f"sgu{n}", [P, 2, KC, SD], F32R) for n in "hl"]
        sd_raw = sb("sd_raw", [P, 3, H])
        sdw = [sb(f"sdw{n}", [P, 3, H], F32R) for n in "hl"]
        eg_raw = sb("eg_raw", [P, 2, KC, 2, ID])
        ed_raw = sb("ed_raw", [IC, 2, 2, H])
        egw = [sb(f"egw{n}", [P, 2, KC, 2, ID], F32R) for n in "hl"]
        edw = [sb(f"edw{n}", [IC, 2, 2, H], F32R) for n in "hl"]
        xn2 = sb("xn2", [P, NT, H])
        ek = xn2[:].rearrange("p (c t) h -> p c (t h)", c=KC)
        av = sb("av", [P, KC, T])
        rT = sb("rT", [P, KC, T])
        den = sb("den", [P, KC, T])
        st = sb("st", [P, 2, 512])
        sT = [sb(f"sT{n}", [P, 3, T], F32R) for n in "hl"]
        room = kvr_raw[:].rearrange("p n k d -> p (n k d)")
        tt2, gs2, mid = (room[:, n * ID:(n + 1) * ID] for n in range(3))
        xg = room[:, 3 * ID:3 * ID + GW]
        alls, chosen, w16 = (room[:, 1024 + n * P:1024 + (n + 1) * P].rearrange("p (t e) -> p t e", t=NT)
                             for n in range(3))
        chosen_b = sb("chosen_b", [P, NT, EXPERTS], BF16)
        before = sb("before", [P, P], BF16)
        ones_b = sb("ones_b", [P, P], BF16)
        slot = sb("slot", [P, EXPERTS, NT])
        slotT = sb("slotT", [P, T], BF16)
        sel = sb("sel", [P, EXPERTS, P], BF16)
        iota_c = sb("iota_c", [P, P])
        iota_p = sb("iota_p", [P, 1])
        pmat = sb("pmat", [P, 2, NT, CAP], F32R)
        pmT = sb("pmT", [P, 2, T], F32R)
        wsc = sb("wsc", [P, 1])
        xgT = [sb(f"xgT{n}", [P, KC, CAP], F32R) for n in "hl"]
        midT = [sb(f"midT{n}", [IC, 2, CAP], F32R) for n in "hl"]
        eo = [sb(f"eo{n}", [P, H], F32R) for n in "hl"]

        pm = [ctx.enter_context(nc.psum_tensor("stage", [P, 2, T], F32)),
              ctx.enter_context(nc.psum_tensor("ps_s", [P, 512], F32)),
              ctx.enter_context(nc.psum_tensor("ps_t", [P, 512], F32)),
              ctx.enter_context(nc.psum_tensor("ps_o", [P, T], F32))]
        stage, ps_s, ps_t, ps_o = pm

        y = stage[:].rearrange("p a (b h) -> p (a b) h", h=H)
        ring = [ps_s[:], ps_t[:], ps_o[:, 0:512], ps_o[:, 512:T]]
        ps_g, ps_x, ps_f, ps_b = ring

        def ring_of(u):
            return ring[RNAMES.index(u) % 4]

        x_in = sem("x_in")
        small_in = sem("small_in")
        consts = sem("consts")
        pool_seq = sem("pool_seq")
        zeroed = sem("zeroed")
        vseq = sem("vseq")
        sqrt_done = sem("sqrt_done")
        xn_ready = sem("xn_ready")
        xnT_full = sem("xnT_full")
        xT_hi = sem("xT_hi")
        xT_lo = sem("xT_lo")
        small_T = sem("small_T")
        small_hi = sem("small_hi")
        rwT_ready = sem("rwT_ready")
        logits_full = sem("logits_full")
        top_sub = sem("top_sub")
        top_exp = sem("top_exp")
        scores_ready = sem("scores_ready")
        scT_full = sem("scT_full")
        scT_ready = sem("scT_ready")
        bias_full = sem("bias_full")
        acc_ready = sem("acc_ready")
        stage_full = sem("stage_full")
        stage_read_dve = sem("stage_read_dve")
        stage_read_act = sem("stage_read_act")
        qkv_hi = sem("qkv_hi")
        vb_ready = sem("vb_ready")
        scores_full = sem("scores_full")
        smax_done = sem("smax_done")
        exp_done = sem("exp_done")
        recip_done = sem("recip_done")
        p_norm = sem("p_norm")
        gmin_done = sem("gmin_done")
        grecip_done = sem("grecip_done")
        pg_ready = sem("pg_ready")
        pt_full = sem("pt_full")
        pt_hi = sem("pt_hi")
        pt_lo = sem("pt_lo")
        pv_done = sem("pv_done")
        og_copied = sem("og_copied")
        gcols_full = sem("gcols_full")
        out_hi = sem("out_hi")
        out_lo = sem("out_lo")
        tanh_done = sem("tanh_done")
        clip_done = sem("clip_done")
        glu_done = sem("glu_done")
        h_ready = sem("h_ready")
        h_hi = sem("h_hi")
        h0_lo = sem("h0_lo")
        h1_lo = sem("h1_lo")
        w_hi = sem("w_hi")
        w_lo = sem("w_lo")
        ex_loaded = sem("ex_loaded")
        qkv_loaded = sem("qkv_loaded")
        wo_loaded = sem("wo_loaded")
        out_stored = sem("out_stored")
        held = sem("held")

        l1_loaded = sem("l1_loaded")
        l1_consts = sem("l1_consts")
        tokens_hi = sem("tokens_hi")
        ring_full = sem("ring_full")
        ring_act = sem("ring_act")
        ring_dve = sem("ring_dve")
        zeros2 = sem("zeros2")
        decay_exp = sem("decay_exp")
        decay_ready = sem("decay_ready")
        ring_hi = sem("ring_hi")
        l1_w_hi = sem("l1_w_hi")
        l1_w_lo = sem("l1_w_lo")
        l1_sub = sem("l1_sub")
        l1_exp = sem("l1_exp")
        chosen_ready = sem("chosen_ready")
        slots_ready = sem("slots_ready")
        st_tanh = sem("st_tanh")
        sgs_done = sem("sgs_done")
        smid_done = sem("smid_done")
        sT_hi = sem("sT_hi")
        sT_lo = sem("sT_lo")
        rows_hi = sem("rows_hi")
        rows_lo = sem("rows_lo")
        rden_done = sem("rden_done")
        rw_ready = sem("rw_ready")
        y_done = sem("y_done")
        out_ready = sem("out_ready")
        wraw_loaded = sem("wraw_loaded")
        pm_ready = sem("pm_ready")
        g_full = sem("g_full")
        xg_copied = sem("xg_copied")
        xt_full = sem("xt_full")
        xgt_hi = sem("xgt_hi")
        xgt_lo = sem("xgt_lo")
        sb_full = sem("sb_full")
        pmt_ready = sem("pmt_ready")
        f1_full = sem("f1_full")
        tanh2_done = sem("tanh2_done")
        gs2_done = sem("gs2_done")
        mid_ready = sem("mid_ready")
        mt_full = sem("mt_full")
        mt_hi = sem("mt_hi")
        mt_lo = sem("mt_lo")
        f2_full = sem("f2_full")
        eo_hi = sem("eo_hi")
        eo_lo = sem("eo_lo")
        sc_done = sem("sc_done")
        ew_loaded = [sem(f"ew_loaded{b}") for b in range(2)]
        ew_hi = sem("ew_hi")
        ew_lo = sem("ew_lo")
        wsc_ready = sem("wsc_ready")

        block = ctx.enter_context(nc.Block())

        def k_windows(t_out, src):
            a = src[:, 0:T]
            mid = bass.AP(a.tensor, a.offset + P - HALF, [list(a.ap[0]), [P, NT - 2], [1, WIN]])
            return [(t_out[:, 1:NT - 1, 0:WIN], mid),
                    (t_out[:, 0, HALF:WIN], src[:, 0:WIN - HALF]),
                    (t_out[:, NT - 1, 0:WIN - HALF], src[:, T - WIN + HALF:T]),
                    (t_out[:, :, WIN:KW], src[:, 0:GLOBALS].unsqueeze(1).broadcast_to([P, NT, GLOBALS]))]

        def stage_of(u):
            return stage[:, UNITS.index(u) % 2, :]

        def expert_pieces(b):
            gr_ = gu_raw[:].rearrange("p k (d s) -> p k s d", s=2)
            return [(guw[0][:, b, k], guw[1][:, b, k], gr_[:, k]) for k in range(KC)] + \
                   [(dnw[0][:, b], dnw[1][:, b], dn_raw[:])]

        qkv_pieces = [(qkvw[0][:, n], qkvw[1][:, n], qkv_raw[:, n]) for n in range(3)]
        wo_piece = (wow[0][:], wow[1][:], wo_raw[:])

        @block.sync
        def _(sp):
            sp.dma_start(acc[:], x.rearrange("(t p) h -> p t h", p=P)).then_inc(x_in, 16)
            sp.dma_start(rw_raw[:], rw).then_inc(small_in, 16)
            sp.dma_start(gub_raw[:], gub).then_inc(small_in, 16)
            sp.dma_start(dnb_sb[:], dnb).then_inc(small_in, 16)
            sp.dma_start(rb_bc[:], rb.rearrange("(a e) -> a e", a=1).broadcast_to([P, EXPERTS])).then_inc(small_in, 16)
            with sp.Fori(0, PAIRS) as i:
                sp.wait_ge(stage_read_dve, read_dve(i - 1, "v3"))
                for n in range(2):
                    sp.dma_start(vb[n][0:WIN - P, :, :].bitcast(F32), vp[n][0:WIN - P, 1:VT, :].bitcast(F32))\
                        .then_inc(vb_ready, 16)
                    sp.dma_start(vb[n][WIN - P:KB, :, :].bitcast(F32),
                                 vp[n][HALF:HALF + GLOBALS, 0:1, :].bitcast(F32).broadcast_to([GLOBALS, NT, 2 * HD]))\
                        .then_inc(vb_ready, 16)
            sp.wait_ge(stage_read_dve, read_dve(PAIRS - 1, "wo1"))
            for n, w in enumerate((l1["Wk"], l1["Wv"], l1["Wr"])):
                sp.dma_start(kvr_raw[:, n, :, :], w.rearrange("(c p) d -> p c d", p=P)).then_inc(l1_loaded, 16)
            sp.dma_start(gw_raw[:], l1["gate_w"]).then_inc(l1_loaded, 16)
            sp.dma_start(td[:], l1["time_decay"].rearrange("(c p) -> p c", p=P),
                         allow_slow_non_contiguous=True).then_inc(l1_loaded, 16)
            for n, w in enumerate((l1["sw_gate"], l1["sw_up"])):
                sp.dma_start(sgu_raw[:, n, :, :], w.rearrange("(k p) n -> p k n", p=P)).then_inc(l1_loaded, 16)
            sp.dma_start(sd_raw[:, 0:2, :], l1["sw_down"][0:2 * P, :].rearrange("(c p) n -> p c n", p=P))\
                .then_inc(l1_loaded, 16)
            sp.dma_start(sd_raw[0:SD - 2 * P, 2, :], l1["sw_down"][2 * P:SD, :]).then_inc(l1_loaded, 16)

            def load(e, b):
                for n, w in enumerate((l1["w_gate"], l1["w_up"])):
                    sp.dma_start(eg_raw[:, b, :, n, :], w[e].rearrange("(k p) n -> p k n", p=P)).then_inc(ew_loaded[b], 16)
                sp.dma_start(ed_raw[:, b, :, :], l1["w_down"][e].rearrange("(c p) n -> p c n", p=IC)).then_inc(ew_loaded[b], 16)

            with sp.Fori(0, EXPERTS // 2) as i:
                sp.wait_ge(ew_lo, i * 2 + 1)
                load(i * 2, 0)
                load(i * 2 + 1, 1)
            for q in range(2):
                sp.wait_ge(out_ready, q + 1)
                sp.dma_start(out.rearrange("(t p) h -> p t h", p=P)[:, 4 * q:4 * q + 4, :], acc[:, 4 * q:4 * q + 4, :])\
                    .then_inc(out_stored, 16)
            sp.wait_ge(out_stored, 32)

        @block.gpsimd
        def _(pool):
            seq = 0

            def step(ins):
                nonlocal seq
                ins.then_inc(pool_seq, 1)
                seq += 1
                pool.wait_ge(pool_seq, seq)

            step(nc.gpsimd.memset(ident[:], 0.0))
            step(nc.gpsimd.affine_select(out=ident[:], in_=ident[:], compare_op=ALU.not_equal, fill=1.0,
                                         base=0, pattern=[[-1, P]], channel_multiplier=1))
            nc.gpsimd.iota(iota16[:], pattern=[[1, EXPERTS]], base=0, channel_multiplier=0,
                           allow_small_or_imprecise_dtypes=True).then_inc(consts, 1)
            step(nc.gpsimd.memset(og_sum[:], 0.0))
            for n in range(2):
                step(nc.gpsimd.affine_select(out=og_sum[:], in_=og_sum[:], compare_op=ALU.not_equal, fill=1.0,
                                             base=-GR * n, pattern=[[-HALF, 2], [-1, GLOBALS]],
                                             channel_multiplier=1))
            step(nc.gpsimd.memset(mask[:], 0.0))
            for m in range(3):
                win = mask[:, m, 0:WIN]
                step(nc.gpsimd.affine_select(out=win, in_=win, compare_op=ALU.is_ge, fill=OUTSIDE,
                                             base=-1, pattern=[[1, WIN]], channel_multiplier=-1))
                step(nc.gpsimd.affine_select(out=win, in_=win, compare_op=ALU.is_ge, fill=OUTSIDE,
                                             base=WINDOW - 1, pattern=[[-1, WIN]], channel_multiplier=1))
            win = mask[:, 0, 0:WIN]
            step(nc.gpsimd.affine_select(out=win, in_=win, compare_op=ALU.is_ge, fill=OUTSIDE,
                                         base=-HALF - GLOBALS, pattern=[[1, WIN]], channel_multiplier=0))
            win = mask[:, 2, 0:WIN]
            nc.gpsimd.affine_select(out=win, in_=win, compare_op=ALU.is_ge, fill=OUTSIDE,
                                    base=P + HALF - 1, pattern=[[-1, WIN]], channel_multiplier=0).then_inc(consts, 1)

            def load_expert(e):
                pool.dma_start(gu_raw[:], gup[e].rearrange("(k p) n -> p k n", p=P)).then_inc(ex_loaded, 16)
                pool.dma_start(dn_raw[:], dnp[e].rearrange("(c p) n -> p c n", p=P)).then_inc(ex_loaded, 16)

            def load_qkv(g):
                for n, w in enumerate((wq, wk, wv)):
                    pool.dma_start(qkv_raw[:, n, :, :], w.rearrange("(k p) (g n) -> g p k n", p=P, n=2 * HD)[g])\
                        .then_inc(qkv_loaded, 16)

            def load_wo(g):
                pool.dma_start(wo_raw[:], wo.rearrange("(g j d) n -> g d j n", j=2, d=HD)[g]).then_inc(wo_loaded, 16)

            def lows(i, n0, pieces):
                for n, piece in enumerate(pieces):
                    pool.wait_ge(w_hi, after(i, NW, n0 + n + 1))
                    nc.gpsimd.tensor_tensor(piece[1], piece[2], piece[0].bitcast(F32), ALU.subtract).then_inc(w_lo, 1)
                pool.wait_ge(w_lo, after(i, NW, n0 + len(pieces)))

            for s_, per in ((w_lo, 4), (h0_lo, 2)):
                pool.sem_inc(s_, per)
            load_qkv(0)
            load_expert(0)
            load_wo(0)
            lows(-1, 4, qkv_pieces)
            load_qkv(1)
            lows(-1, 7, expert_pieces(0))
            load_expert(1)

            def hidden_lo(i, j):
                pool.wait_ge(h_hi, after(i, 4, 2 * j + 1))
                nc.gpsimd.tensor_tensor(hh[1][:, 0], ff[:, 2], hh[0][:, 0].bitcast(F32), ALU.subtract)\
                    .then_inc(h0_lo, 1)

            def body(i, left):
                lows(i, 0, expert_pieces(1))
                if left:
                    load_expert(i * 2 + 2)
                hidden_lo(i, 0)
                lows(i, 3, [wo_piece])
                if left:
                    load_wo(i + 1)
                    lows(i, 4, qkv_pieces)
                hidden_lo(i, 1)
                if left > 1:
                    load_qkv(i + 2)
                if left:
                    lows(i, 7, expert_pieces(0))
                    load_expert(i * 2 + 3)

            with pool.Fori(0, PAIRS - 2) as i:
                body(i, 2)
            body(PAIRS - 2, 1)
            body(PAIRS - 1, 0)

            pool.wait_ge(stage_read_dve, read_dve(PAIRS - 1, "wo1"))
            step(nc.gpsimd.memset(before[:], 1.0))
            step(nc.gpsimd.affine_select(out=before[:], in_=before[:], compare_op=ALU.is_gt, fill=0.0,
                                         base=0, pattern=[[1, P]], channel_multiplier=-1))
            nc.gpsimd.memset(ones_b[:], 1.0)
            nc.gpsimd.iota(iota_c[:], pattern=[[1, P]], base=0, channel_multiplier=0,
                           allow_small_or_imprecise_dtypes=True)
            nc.gpsimd.iota(iota_p[:], pattern=[[1, 1]], base=0, channel_multiplier=1,
                           allow_small_or_imprecise_dtypes=True)
            step(nc.gpsimd.memset(sel[:], 0.0))
            nc.gpsimd.affine_select(out=sel[:], in_=sel[:], compare_op=ALU.not_equal, fill=1.0, base=0,
                                    pattern=[[-1, EXPERTS], [0, P]], channel_multiplier=1).then_inc(l1_consts, 1)
            pool.sem_inc(ew_lo, 1)

            def weights_lo(i, b):
                pool.wait_ge(ew_hi, after(i, 2, b + 1))
                nc.gpsimd.tensor_tensor(egw[1][:, b], eg_raw[:, b], egw[0][:, b].bitcast(F32), ALU.subtract)
                nc.gpsimd.tensor_tensor(edw[1][:, b], ed_raw[:, b], edw[0][:, b].bitcast(F32), ALU.subtract)\
                    .then_inc(ew_lo, 1)

            with pool.Fori(0, EXPERTS // 2) as i:
                weights_lo(i, 0)
                weights_lo(i, 1)

        @block.scalar
        def _(act):
            for s_, per in ((qkv_hi, 8 - NEXT), (exp_done, NS), (stage_read_act, NA), (pt_hi, NP), (tanh_done, 4),
                            (h_hi, 4), (out_hi, 3), (w_hi, 4)):
                act.sem_inc(s_, per)
            act.wait_ge(sqrt_done, 1)
            nc.scalar.activation(sd[:, 1], sd[:, 0], ACT.Sqrt).then_inc(sqrt_done, 1)

            for k in range(KC):
                act.wait_ge(xnT_full, k + 1)
                nc.scalar.activation(xT[0][:, k, HALF:HALF + T], stage[:, k, :], ACT.Copy).then_inc(xT_hi, 1)
            act.wait_ge(small_T, 1)
            nc.scalar.activation(rwT[0][:], ps_s[:, 0:KC * EXPERTS].rearrange("p (k e) -> p k e", k=KC),
                                 ACT.Copy).then_inc(small_hi, 1)

            def split_hi(i, n, piece):
                nc.scalar.activation(piece[0], piece[2], ACT.Copy).then_inc(w_hi, 1)

            def even_expert(i, n):
                if n == 0:
                    act.wait_ge(ex_loaded, i * 64 + 96)
                    act.wait_ge(stage_full, full(i, "down10"))
                split_hi(i, n, expert_pieces(0)[n])

            def next_qkv(i, n):
                if n == 0:
                    act.wait_ge(qkv_loaded, i * 48 + 96)
                    act.wait_ge(stage_full, full(i, "k1"))
                split_hi(i, n, qkv_pieces[n])

            def q_hi(i, j):
                act.wait_ge(stage_full, full(i, f"q{j}"))
                act.wait_ge(scores_full, after(i, NS, NT * (2 - j)))
                nc.scalar.activation(qT[0][:, HALF:HALF + T], stage_of(f"q{j}"), ACT.Copy, scale=-SCALE)\
                    .then_inc(qkv_hi, 1)

            def k_hi(i, j):
                act.wait_ge(stage_full, full(i, f"k{j}"))
                for dst, src in k_windows(kw[0], stage_of(f"k{j}")):
                    ins = nc.scalar.activation(dst, src, ACT.Copy)
                ins.then_inc(qkv_hi, 1)

            def v_hi(i, v):
                a, b = V_TILES[v]
                act.wait_ge(stage_full, full(i, f"v{v}"))
                if v == 0:
                    act.wait_ge(pv_done, after(i, NP, NP))
                src = stage_of(f"v{v}")[:, 0:(b - a) * 2 * HD].rearrange("p (t n) -> p t n", n=2 * HD)
                nc.scalar.activation(vp[0][:, a:b, :], src, ACT.Copy).then_inc(qkv_hi, 1)

            for n in range(3):
                next_qkv(-1, n)
            act.wait_ge(zeroed, 1)
            q_hi(-1, 0)
            k_hi(-1, 0)
            for v in range(4):
                v_hi(-1, v)
            for n in range(3):
                even_expert(-1, n)

            act.wait_ge(top_sub, 1)
            nc.scalar.activation(topw[:], topw[:], ACT.Exp).then_inc(top_exp, 1)

            def body(i, more):
                def up_bias(c, j):
                    return ebias[:, 1, c, bass.ds(i * 2 + j, 1)]

                def exps(j, s):
                    n = NT * j + s
                    act.wait_ge(smax_done, after(i, NS, n + 1))
                    act.wait_ge(pt_full, after(i, NP, n - 1))
                    nc.scalar.activation(pr[:, n % 2, 0:KW], sm[:, n % 2, :], ACT.Exp, bias=nm[:, n % 2:n % 2 + 1],
                                         scale=-1.0, accum_out=rs[:, n % 2:n % 2 + 1]).then_inc(exp_done, 1)

                def global_exps(j):
                    rows = slice(HALF * j, HALF * j + GLOBALS)
                    act.wait_ge(gmin_done, after(i, 2, j + 1))
                    act.wait_ge(pt_full, after(i, NP, 0))
                    nc.scalar.activation(pg[rows, HALF:HALF + T], stage_of(f"sg{j}")[rows, :], ACT.Exp,
                                         bias=gm[rows, 0:1], scale=-1.0, accum_out=gs[rows, 0:1])\
                        .then_inc(stage_read_act, 1)

                def tanh(j, c):
                    act.wait_ge(stage_read_dve, read_dve(i, f"gate{c}{j}"))
                    act.wait_ge(h_ready, after(i, 4, 2 * j + c))
                    nc.scalar.activation(ff[:, 1], ff[:, 0], ACT.Tanh, scale=ALPHA / 2).then_inc(tanh_done, 1)

                def up(j, c):
                    act.wait_ge(stage_full, full(i, f"up{c}{j}"))
                    act.wait_ge(*((h0_lo, after(i, 2, j + 1)) if c else (h1_lo, after(i, 2, j))))
                    nc.scalar.activation(ff[:, 2], stage_of(f"up{c}{j}"), ACT.Identity,
                                         bias=up_bias(c, j), scale=0.5).then_inc(stage_read_act, 1)

                def hidden_hi(j, c):
                    act.wait_ge(h_ready, after(i, 4, 2 * j + c + 1))
                    if c == 0:
                        act.wait_ge(stage_full, full(i - 1, "down11") if j == 0 else full(i, "down10"))
                    nc.scalar.activation(hh[0][:, c], ff[:, 2], ACT.Copy).then_inc(h_hi, 1)

                def probs_hi(n):
                    act.wait_ge(pt_full, after(i, NP, n + 1))
                    act.wait_ge(pv_done, after(i, NP, n - 1))
                    nc.scalar.activation(pT[0][:, n % 2, :], ps_t[:, 0:2 * P], ACT.Copy).then_inc(pt_hi, 1)

                def head(j):
                    for s in range(NT):
                        exps(j, s)
                        if s == 1:
                            global_exps(j)
                        for c in range(2):
                            if s == 3 + 4 * c:
                                tanh(j, c)
                            if s == 4 + 4 * c:
                                up(j, c)
                            if s == 6 + 4 * c:
                                hidden_hi(j, c)
                        if s:
                            probs_hi(NT * j + s - 1)
                        if j == 0:
                            if s < 3:
                                if s == 0:
                                    act.wait_ge(ex_loaded, i * 64 + 64)
                                    act.wait_ge(stage_full, full(i - 1, "down11"))
                                split_hi(i, s, expert_pieces(1)[s])
                            if s == 5:
                                act.wait_ge(wo_loaded, i * 16 + 16)
                                act.wait_ge(stage_full, after(i, NU, 0))
                                split_hi(i, 3, wo_piece)
                        elif more:
                            if s < 3:
                                next_qkv(i, s)
                            elif s in (4, 5, 6):
                                even_expert(i, s - 4)
                    up(j, 1)
                    probs_hi(NT * j + NT - 1)
                    if j == 0 or more:
                        q_hi(i, 1 - j)
                    hidden_hi(j, 1)
                    if j == 0 or more:
                        k_hi(i, 1 - j)
                    if j == 1:
                        act.wait_ge(pt_full, after(i, NP, NP))
                        nc.scalar.activation(pgT[:, :, 0, :], ps_t[:, 0:VT * GR].rearrange("p (t g) -> p t g", t=VT),
                                             ACT.Copy).then_inc(pt_hi, 1)
                    act.wait_ge(pv_done, after(i, NP, NT * (j + 1)))
                    if j == 0:
                        act.wait_ge(stage_full, after(i, NU, 0))
                    nc.scalar.activation(oT[0][:, j, GLOBALS:T], ps_o[:, GLOBALS:T], ACT.Copy).then_inc(out_hi, 1)

                def global_outputs():
                    act.wait_ge(pv_done, after(i, NP, NP))
                    nc.scalar.activation(og[:], ps_s[0:2 * GR, 0:2 * HD], ACT.Copy).then_inc(og_copied, 1)
                    if more:
                        v_hi(i, 0)
                        v_hi(i, 1)
                    act.wait_ge(gcols_full, i + 1)
                    nc.scalar.activation(oT[0][:, :, 0:GLOBALS],
                                         ps_t[:, 0:2 * GLOBALS].rearrange("p (j c) -> p j c", j=2), ACT.Copy)\
                        .then_inc(out_hi, 1)
                    if more:
                        v_hi(i, 2)
                        v_hi(i, 3)

                head(0)
                head(1)
                global_outputs()

            with act.Fori(0, PAIRS - 1) as i:
                body(i, True)
            body(PAIRS - 1, False)

            for s_ in (tanh2_done, mt_hi, eo_hi, ew_hi):
                act.sem_inc(s_, 2)

            def ring_hi_of(u, dst, src):
                act.wait_ge(ring_full, RNAMES.index(u) + 1)
                nc.scalar.activation(dst, src, ACT.Copy).then_inc(ring_hi, 1)

            for n, u in enumerate(("wkT", "wvT", "wrT")):
                ring_hi_of(u, kvrT[0][:, n], ring_of(u).rearrange("p (k e) -> p k e", k=KC))
            ring_hi_of("gwT", gwT[0][:], ring_of("gwT")[:, 0:KC * EXPERTS].rearrange("p (k e) -> p k e", k=KC))
            act.wait_ge(sqrt_done, 3)
            nc.scalar.activation(sd[:, 1], sd[:, 0], ACT.Sqrt).then_inc(sqrt_done, 1)
            act.wait_ge(l1_loaded, 9 * 16)
            nc.scalar.activation(decay[:], td[:], ACT.Exp).then_inc(decay_exp, 1)
            act.wait_ge(decay_exp, 1)
            nc.scalar.activation(decay[:], decay[:], ACT.Exp, scale=-1.0).then_inc(decay_ready, 1)
            for k in range(KC):
                for h in range(2):
                    u = f"xT{k}{h}"
                    ring_hi_of(u, x2T[0][:, k, 1 + h * 512:1 + (h + 1) * 512], ring_of(u))
            for g in range(2):
                nc.scalar.activation(sgu[0][:, g], sgu_raw[:, g], ACT.Copy).then_inc(l1_w_hi, 1)
            for h in range(2):
                nc.scalar.activation(xr[0][:, 4 * h:4 * h + 4, 0:H], xn2[:, 4 * h:4 * h + 4, :], ACT.Copy)\
                    .then_inc(rows_hi, 1)
            act.wait_ge(l1_sub, 1)
            nc.scalar.activation(topw[:], topw[:], ACT.Exp)
            nc.scalar.activation(alls[:], alls[:], ACT.Exp).then_inc(l1_exp, 1)
            for c in range(KC):
                for u, func, dst in (("k", ACT.Exp, ek), ("v", ACT.Copy, av), ("r", ACT.Copy, rT)):
                    for h in range(2):
                        act.wait_ge(ring_full, RNAMES.index(f"{u}{c}{h}") + 1)
                        if u == "k" and c == 0 and h == 0:
                            act.wait_ge(rows_lo, 2)
                        nc.scalar.activation(dst[:, c, h * 512:(h + 1) * 512], ring_of(f"{u}{c}{h}"), func)\
                            .then_inc(ring_act, 1)
            nc.scalar.activation(sdw[0][:, 0:2], sd_raw[:, 0:2], ACT.Copy)
            nc.scalar.activation(sdw[0][0:SD - 2 * P, 2], sd_raw[0:SD - 2 * P, 2], ACT.Copy).then_inc(l1_w_hi, 1)

            def expert_hi(i, b):
                act.wait_ge(ew_loaded[b], i * 48 + 48)
                act.wait_ge(f2_full, after(i, 2, b - 1))
                nc.scalar.activation(egw[0][:, b], eg_raw[:, b], ACT.Copy)
                nc.scalar.activation(edw[0][:, b], ed_raw[:, b], ACT.Copy).then_inc(ew_hi, 1)

            for n in range(7):
                c, h = n // 2, n % 2
                if n < 6:
                    w = S_CHUNKS[c][1] - S_CHUNKS[c][0]
                    act.wait_ge(ring_full, RNAMES.index(f"sg{c}{h}") + 1)
                    if n >= 2:
                        act.wait_ge(sT_lo, n - 1)
                    nc.scalar.activation(st[0:w, n % 2], ring_of(f"sg{c}{h}")[0:w, :], ACT.Tanh, scale=0.5)\
                        .then_inc(st_tanh, 1)
                if n >= 1:
                    c, h = (n - 1) // 2, (n - 1) % 2
                    w = S_CHUNKS[c][1] - S_CHUNKS[c][0]
                    act.wait_ge(smid_done, n)
                    nc.scalar.activation(sT[0][0:w, c, h * 512:(h + 1) * 512], st[0:w, (n - 1) % 2], ACT.Copy)\
                        .then_inc(sT_hi, 1)
                if n == 1:
                    expert_hi(0, 0)

            def rows_copy(count):
                act.wait_ge(g_full, count)
                nc.scalar.activation(xg[:], ps_g[:, 0:GW], ACT.Copy).then_inc(xg_copied, 1)

            def rows_hi_parts(count):
                act.wait_ge(xt_full, count)
                nc.scalar.activation(xgT[0][:], ps_f[:, 0:H].rearrange("p (k c) -> p k c", k=KC), ACT.Copy)\
                    .then_inc(xgt_hi, 1)

            rows_copy(1)
            rows_hi_parts(1)

            def step2(i, b, last):
                n = b + 1
                act.wait_ge(f1_full, after(i, 2, n))
                act.wait_ge(gs2_done, after(i, 2, b))
                nc.scalar.activation(tt2[:], ps_f[:, 0:ID], ACT.Tanh, scale=0.5).then_inc(tanh2_done, 1)
                if not last:
                    if b == 0:
                        expert_hi(i, 1)
                    else:
                        act.wait_ge(ew_loaded[0], i * 48 + 96)
                        act.wait_ge(f2_full, after(i, 2, 1))
                        nc.scalar.activation(egw[0][:, 0], eg_raw[:, 0], ACT.Copy)
                        nc.scalar.activation(edw[0][:, 0], ed_raw[:, 0], ACT.Copy).then_inc(ew_hi, 1)
                    act.wait_ge(wsc_ready, i * 2 + n)
                    rows_copy(i * 2 + (n + 1))
                act.wait_ge(mt_full, after(i, 2, n))
                act.wait_ge(f2_full, after(i, 2, b))
                nc.scalar.activation(midT[0][:], ps_x[0:IC, 0:2 * CAP].rearrange("p (c t) -> p c t", c=2),
                                     ACT.Copy).then_inc(mt_hi, 1)
                if not last:
                    rows_hi_parts(i * 2 + (n + 1))
                act.wait_ge(f2_full, after(i, 2, n))
                act.wait_ge(sc_done, after(i, 2, n))
                nc.scalar.activation(eo[0][:], ps_g[:, 0:H], ACT.Copy).then_inc(eo_hi, 1)

            step2(0, 0, False)
            step2(0, 1, False)
            with act.Fori(1, EXPERTS // 2 - 1) as i:
                step2(i, 0, False)
                step2(i, 1, False)
            step2(EXPERTS // 2 - 1, 0, False)
            step2(EXPERTS // 2 - 1, 1, True)

        @block.tensor
        def _(pe):
            for s_, per in ((stage_full, NU - NEXT - LATE), (scores_full, NS), (pt_full, NP), (pv_done, NP)):
                pe.sem_inc(s_, per)

            def three(out_, a, b, start, stop):
                nc.tensor.matmul(out_, a[0], b[0], start=start, stop=False, skip_group_check=True)
                nc.tensor.matmul(out_, a[0], b[1], start=False, stop=False, skip_group_check=True)
                return nc.tensor.matmul(out_, a[1], b[0], start=False, stop=stop, skip_group_check=True)

            pe.wait_ge(consts, 1)
            for k in range(KC):
                for t in range(NT):
                    if k == 0:
                        pe.wait_ge(xn_ready, t + 1)
                    ins = nc.tensor.transpose(stage[:, k, t * P:(t + 1) * P], xn[:, t, k * P:(k + 1) * P], ident[:])
                ins.then_inc(xnT_full, 1)
            pe.wait_ge(small_in, 64)
            for k in range(KC):
                nc.tensor.transpose(ps_s[:, k * EXPERTS:(k + 1) * EXPERTS], rw_raw[:, k * P:(k + 1) * P],
                                    ident[0:EXPERTS, 0:EXPERTS])
            bias_src = gub_raw[:].rearrange("e (c d s) -> e s c d", s=2, d=P)
            for s in range(2):
                for c in range(2):
                    col = KC * EXPERTS + (2 * s + c) * EXPERTS
                    ins = nc.tensor.transpose(ps_s[:, col:col + EXPERTS], bias_src[:, s, c, :],
                                              ident[0:EXPERTS, 0:EXPERTS])
            ins.then_inc(small_T, 1)
            pe.wait_ge(xT_lo, KC)
            pe.wait_ge(rwT_ready, 1)
            for t in range(NT):
                for k in range(KC):
                    a = [xT[n][:, k, HALF + t * P:HALF + (t + 1) * P] for n in range(2)]
                    ins = three(ps_t[:, t * EXPERTS:(t + 1) * EXPERTS], a, [rwT[n][:, k, :] for n in range(2)],
                                k == 0, k == KC - 1)
            ins.then_inc(logits_full, 1)

            def stage_free(i, u):
                n = UNITS.index(u) - 2
                last, i_ = UNITS[n], (i if n >= 0 else i - 1)
                pe.wait_ge(*((stage_read_act, read_act(i_, last)) if last in BY_ACT
                             else (stage_read_dve, read_dve(i_, last))))

            def project(i, u, parts, n_half=(0, 1), absent=0):
                o = stage_of(u)
                if 0 in n_half:
                    stage_free(i, u)
                for h in n_half:
                    for k in range(KC):
                        b = [xT[n][:, k, HALF + h * 512:HALF + (h + 1) * 512] for n in range(2)]
                        ins = three(o[:, h * 512:(h + 1) * 512], parts(k), b, k == 0, k == KC - 1)
                if 1 in n_half:
                    ins.then_inc(stage_full, 1 + absent)

            def project_qk(i, n, j):
                project(i, f"{'qk'[n]}{j}", lambda k: [qkvw[m][:, n, k, j * HD:(j + 1) * HD] for m in range(2)])

            def project_v(i, v):
                a, b = V_TILES[v]
                u = f"v{v}"
                stage_free(i, u)
                for t in range(a, b):
                    o = stage_of(u)[:, (t - a) * 2 * HD:(t - a + 1) * 2 * HD]
                    for k in range(KC):
                        ins = three(o, [xT[n][:, k, t * P:(t + 1) * P] for n in range(2)],
                                    [qkvw[n][:, 2, k, :] for n in range(2)], k == 0, k == KC - 1)
                ins.then_inc(stage_full, 3 if v == 3 and isinstance(i, int) else 1)

            pe.wait_ge(w_lo, after(-1, NW, 7))
            for n in range(2):
                project_qk(-1, n, 0)
            for v in range(4):
                project_v(-1, v)

            pe.wait_ge(scores_ready, 1)
            for t in range(NT):
                ins = nc.tensor.transpose(ps_o[0:EXPERTS, t * P:(t + 1) * P], scores[:, :, t], ident[:])
            ins.then_inc(scT_full, 1)
            pe.wait_ge(scT_ready, 1)
            pe.wait_ge(stage_read_dve, read_dve(-1, "v3"))
            for t in range(NT):
                ins = nc.tensor.matmul(stage[:, t // 4, (t % 4) * H:(t % 4 + 1) * H], scT[:, t * P:(t + 1) * P],
                                       dnb_sb[:], start=True, stop=True)
                if t % 4 == 3:
                    ins.then_inc(stage_full, 1)

            def body(i, more):
                def scores_of(j, s):
                    n = NT * j + s
                    pe.wait_ge(smax_done, after(i, NS, n))
                    three(ps_s[:, 0:KW], [qT[m][:, HALF + s * P:HALF + (s + 1) * P] for m in range(2)],
                          [kw[m][:, s, :] for m in range(2)], True, True).then_inc(scores_full, 1)

                def global_scores(j):
                    u = f"sg{j}"
                    stage_free(i, u)
                    for h in range(2):
                        ins = three(stage_of(u)[:, h * 512:(h + 1) * 512],
                                    [qT[n][:, HALF * (1 - j):HALF * (1 - j) + P] for n in range(2)],
                                    [kw[n][:, 4 * h:4 * h + 4, HALF:HALF + P] for n in range(2)], True, True)
                    ins.then_inc(stage_full, 1)

                def expert_piece(j, s):
                    u = ("gate0", "up0", "gate1", "up1")[s // 2]
                    g, c = (0 if u[0] == "g" else 1), int(u[-1])
                    if s == 0:
                        pe.wait_ge(w_lo, after(i, NW, 0 if j == 0 else 3))
                    project(i, f"{u}{j}", lambda k: [guw[n][:, j, k, g, c * P:(c + 1) * P] for n in range(2)],
                            (s % 2,), NEXT if j == 1 and s == NT - 1 and not more else 0)

                def down(j):
                    pe.wait_ge(h0_lo, after(i, 2, j + 1))
                    pe.wait_ge(h1_lo, after(i, 2, j + 1))
                    for q in range(2):
                        u = f"down{q}{j}"
                        stage_free(i, u)
                        for t in range(4):
                            tt = 4 * q + t
                            for c in range(2):
                                ins = three(stage_of(u)[:, t * H:(t + 1) * H],
                                            [hh[n][:, c, tt * P:(tt + 1) * P] for n in range(2)],
                                            [dnw[n][:, j, c, :] for n in range(2)], c == 0, c == 1)
                        ins.then_inc(stage_full, 1)

                def transposed(n):
                    pe.wait_ge(p_norm, after(i, NS, n + 1))
                    pe.wait_ge(pt_lo, after(i, NP, n))
                    for b in range(2):
                        ins = nc.tensor.transpose(ps_t[:, b * P:(b + 1) * P], pr[:, n % 2, b * P:(b + 1) * P],
                                                  ident[:])
                    ins.then_inc(pt_full, 1)

                def weighted_values(j, t):
                    n = NT * j + t
                    hs = slice(j * HD, (j + 1) * HD)
                    pe.wait_ge(pt_lo, after(i, NP, n + 1))
                    if t == 0:
                        pe.wait_ge(out_lo, after(i, 3, j))
                        if j == 0:
                            pe.wait_ge(vb_ready, i * 64 + 64)
                    o = ps_o[:, t * P:(t + 1) * P]
                    three(o, [vp[m][:, t, hs] for m in range(2)], [pT[m][:, n % 2, 0:P] for m in range(2)],
                          True, False)
                    three(o, [vb[m][0:KB, t, hs] for m in range(2)],
                          [pT[m][0:KB, n % 2, P:2 * P] for m in range(2)], False, True).then_inc(pv_done, 1)

                def head(j):
                    pe.wait_ge(stage_read_dve, read_dve(i, "k1") if j else read_dve(i - 1, "k0"))
                    for s in range(NT):
                        scores_of(j, s)
                        if s == 0:
                            global_scores(j)
                        expert_piece(j, s)
                        if s >= 1:
                            transposed(NT * j + s - 1)
                        if s >= 2:
                            weighted_values(j, s - 2)
                    if j == 1 and more:
                        pe.wait_ge(w_lo, after(i, NW, 7))
                    if j == 0 or more:
                        project_qk(i, 0, 1 - j)
                    transposed(NT * j + NT - 1)
                    weighted_values(j, NT - 2)
                    if j == 0 or more:
                        project_qk(i, 1, 1 - j)
                    if j == 1:
                        pe.wait_ge(pt_lo, after(i, NP, NS))
                        pe.wait_ge(pg_ready, after(i, 2, 2))
                        pe.sem_inc(held, 1)
                        for t in range(VT):
                            ins = nc.tensor.transpose(ps_t[:, t * GR:(t + 1) * GR], pg[:, t * P:(t + 1) * P],
                                                      ident[0:GR, 0:GR])
                        ins.then_inc(pt_full, 1)
                    weighted_values(j, NT - 1)

                def global_values():
                    pe.wait_ge(pt_lo, after(i, NP, NP))
                    for t in range(VT):
                        for n in range(2):
                            ins = nc.tensor.matmul(ps_s[0:2 * GR, 0:2 * HD],
                                                   pgT[:, t].rearrange("p n g -> p (n g)"), vp[n][:, t, :],
                                                   start=t == 0 and n == 0, stop=t == VT - 1 and n == 1,
                                                   skip_group_check=True)
                    ins.then_inc(pv_done, 1)

                def global_columns():
                    pe.wait_ge(og_copied, i + 1)
                    for j in range(2):
                        ins = nc.tensor.matmul(ps_t[:, j * GLOBALS:(j + 1) * GLOBALS], og[:, j * HD:(j + 1) * HD],
                                               og_sum[:, j, :], start=True, stop=True)
                    ins.then_inc(gcols_full, 1)

                head(0)
                down(0)
                head(1)
                if more:
                    project_v(i, 0)
                global_values()
                if more:
                    project_v(i, 1)
                global_columns()
                if more:
                    project_v(i, 2)
                    project_v(i, 3)
                down(1)
                pe.wait_ge(w_lo, after(i, NW, 4))
                pe.wait_ge(out_lo, after(i, 3, 3))
                for q in range(2):
                    u = f"wo{q}"
                    stage_free(i, u)
                    for t in range(4):
                        tt = 4 * q + t
                        for j in range(2):
                            ins = three(stage_of(u)[:, t * H:(t + 1) * H],
                                        [oT[n][:, j, tt * P:(tt + 1) * P] for n in range(2)],
                                        [wow[n][:, j, :] for n in range(2)], j == 0, j == 1)
                    ins.then_inc(stage_full, 1)

            with pe.Fori(0, PAIRS - 1) as i:
                body(i, True)
            body(PAIRS - 1, False)

            for s_, per in ((sb_full, 4), (f1_full, 2), (mt_full, 2), (f2_full, 2), (sc_done, 2)):
                pe.sem_inc(s_, per)

            def ring_free(u):
                n = RNAMES.index(u) - 4
                if n >= 0:
                    last, reader = RING[n]
                    pe.wait_ge(ring_act if reader == "act" else ring_dve, ring_reads(last, reader))

            pe.wait_ge(stage_read_dve, read_dve(PAIRS - 1, "wo1"))
            pe.wait_ge(l1_loaded, 9 * 16)
            for n, u in enumerate(("wkT", "wvT", "wrT")):
                for k in range(KC):
                    for c in range(KC):
                        ins = nc.tensor.transpose(ring_of(u)[:, k * H + c * P:k * H + (c + 1) * P],
                                                  kvr_raw[:, n, c, k * P:(k + 1) * P], ident[:])
                ins.then_inc(ring_full, 1)
            for k in range(KC):
                ins = nc.tensor.transpose(ring_of("gwT")[:, k * EXPERTS:(k + 1) * EXPERTS], gw_raw[:, k * P:(k + 1) * P],
                                          ident[0:EXPERTS, 0:EXPERTS])
            ins.then_inc(ring_full, 1)
            for k in range(KC):
                for h in range(2):
                    u = f"xT{k}{h}"
                    ring_free(u)
                    for t in range(4 * h, 4 * h + 4):
                        pe.wait_ge(xn_ready, NT + t + 1)
                        ins = nc.tensor.transpose(ring_of(u)[:, (t % 4) * P:(t % 4 + 1) * P],
                                                  xn2[:, t, k * P:(k + 1) * P], ident[:])
                    ins.then_inc(ring_full, 1)
            ring_free("logits")
            pe.wait_ge(ring_dve, ring_reads("xT11", "dve"))
            for t in range(NT):
                for k in range(KC):
                    ins = three(ring_of("logits")[:, t * EXPERTS:(t + 1) * EXPERTS],
                                [x2T[n][:, k, 1 + t * P:1 + (t + 1) * P] for n in range(2)],
                                [gwT[n][:, k, :] for n in range(2)], k == 0, k == KC - 1)
            ins.then_inc(ring_full, 1)

            def ring_project(u, w, parts, shift, h):
                ring_free(u)
                for k in range(KC):
                    b = [x2T[n][:, k, shift + h * 512:shift + (h + 1) * 512] for n in range(2)]
                    ins = three(ring_of(u)[0:w, :], parts(k), b, k == 0, k == KC - 1)
                ins.then_inc(ring_full, 1)

            pe.wait_ge(zeros2, 1)
            for c in range(KC):
                for n, u in enumerate("kvr"):
                    for h in range(2):
                        ring_project(f"{u}{c}{h}", P, lambda k: [kvrT[m][:, n, k, c * P:(c + 1) * P] for m in range(2)],
                                     1 if u == "r" else 0, h)
            ring_free("pos")
            pe.wait_ge(chosen_ready, 1)
            pe.wait_ge(l1_consts, 1)
            pos = ring_of("pos")[:, 0:NT * EXPERTS].rearrange("p (t e) -> p t e", t=NT)
            nc.tensor.matmul(pos, before[:], chosen_b[:], start=True, stop=False, skip_group_check=True)
            for t in range(NT - 1):
                ins = nc.tensor.matmul(pos[:, t + 1:NT, :], ones_b[:],
                                       chosen_b[:, t:t + 1, :].broadcast_to([P, NT - 1 - t, EXPERTS]),
                                       start=False, stop=t == NT - 2, skip_group_check=True)
            ins.then_inc(ring_full, 1)

            def shared(c, h):
                lo, hi = S_CHUNKS[c]
                for g, u in enumerate(("sg", "su")):
                    ring_project(f"{u}{c}{h}", hi - lo, lambda k: [sgu[m][:, g, k, lo:hi] for m in range(2)], 1, h)

            pe.wait_ge(l1_w_lo, 2)
            for c in range(2):
                for h in range(2):
                    shared(c, h)
            pe.wait_ge(slots_ready, 1)
            for h in range(2):
                u = f"slots{h}"
                ring_free(u)
                for t in range(4 * h, 4 * h + 4):
                    ins = nc.tensor.transpose(ring_of(u)[0:EXPERTS, (t % 4) * P:(t % 4 + 1) * P], slot[:, :, t],
                                              ident[:])
                ins.then_inc(ring_full, 1)
            shared(2, 0)
            shared(2, 1)
            pe.wait_ge(sT_lo, 6)
            pe.wait_ge(l1_w_lo, 3)
            for t in range(NT):
                for c, (lo, hi) in enumerate(S_CHUNKS):
                    three(y[:, t, :], [sT[n][0:hi - lo, c, t * P:(t + 1) * P] for n in range(2)],
                          [sdw[n][0:hi - lo, c, :] for n in range(2)], c == 0 and t % 2 == 0, False)

            def gather(b, half):
                for t in range(4 * half, 4 * half + 4):
                    for n in range(2):
                        ins = nc.tensor.matmul(ps_g[:, 0:GW], pmat[:, b, t, :], xr[n][:, t, :],
                                               start=t == 0 and n == 0, stop=t == NT - 1 and n == 1,
                                               skip_group_check=True)
                return ins

            def scatter(b, half):
                for t in range(4 * half, 4 * half + 4):
                    for n in range(2):
                        ins = nc.tensor.matmul(y[:, t, :], pmT[:, b, t * P:(t + 1) * P], eo[n][:],
                                               start=False, stop=False, skip_group_check=True)
                return ins

            pe.wait_ge(ring_dve, ring_reads(RNAMES[-1], "dve"))
            pe.wait_ge(rows_lo, 3)

            def rows_transposed():
                for k in range(KC):
                    ins = nc.tensor.transpose(ps_f[:, k * P:(k + 1) * P], xg[:, k * P:(k + 1) * P], ident[:])
                return ins

            pe.wait_ge(pm_ready, 1)
            gather(0, 0)
            gather(0, 1).then_inc(g_full, 1)
            pe.wait_ge(xg_copied, 1)
            rows_transposed().then_inc(xt_full, 1)

            def step2(i, b, first, last):
                n = b + 1

                def slots_row(h):
                    pe.wait_ge(pmt_ready, after(i, 4, 2 * b + h))
                    pe.sem_inc(held, 1)
                    nc.tensor.matmul(ps_b, sel[:, bass.ds(i * 2 + b, 1), :].rearrange("p a c -> p (a c)"),
                                     slotT[:, h * 512:(h + 1) * 512], start=True, stop=True).then_inc(sb_full, 1)

                pe.wait_ge(xgt_lo, i * 2 + n)
                pe.wait_ge(ew_lo, i * 2 + (b + 2))
                for k in range(KC):
                    ins = three(ps_f[:, 0:2 * ID], [xgT[m][:, k, :] for m in range(2)],
                                [egw[m][:, b, k].rearrange("p g n -> p (g n)") for m in range(2)], k == 0, k == KC - 1)
                ins.then_inc(f1_full, 1)
                slots_row(0)
                pe.wait_ge(eo_lo, after(i, 2, b))
                if not last:
                    pe.wait_ge(pm_ready, i * 2 + (n + 1))
                    gather(1 - b, 0)
                    gather(1 - b, 1).then_inc(g_full, 1)
                if not first:
                    pe.wait_ge(pmt_ready, after(i, 4, 2 * b))
                    scatter(1 - b, 0)
                pe.wait_ge(mid_ready, after(i, 2, n))
                for c in range(2):
                    ins = nc.tensor.transpose(ps_x[0:IC, c * CAP:(c + 1) * CAP], mid[:, c * IC:(c + 1) * IC], ident[:])
                ins.then_inc(mt_full, 1)
                if not last:
                    pe.wait_ge(xg_copied, i * 2 + (n + 1))
                    rows_transposed().then_inc(xt_full, 1)
                slots_row(1)
                if not first:
                    scatter(1 - b, 1).then_inc(sc_done, 1)
                else:
                    pe.sem_inc(sc_done, 1)
                pe.wait_ge(mt_lo, after(i, 2, n))
                for c in range(2):
                    ins = three(ps_g[:, 0:H], [midT[m][:, c, :] for m in range(2)],
                                [edw[m][:, b, c, :] for m in range(2)], c == 0, c == 1)
                ins.then_inc(f2_full, 1)

            step2(0, 0, True, False)
            step2(0, 1, False, False)
            with pe.Fori(1, EXPERTS // 2 - 1) as i:
                step2(i, 0, False, False)
                step2(i, 1, False, False)
            step2(EXPERTS // 2 - 1, 0, False, False)
            step2(EXPERTS // 2 - 1, 1, False, True)
            pe.wait_ge(eo_lo, after(EXPERTS // 2 - 1, 2, 2))
            pe.wait_ge(pmt_ready, after(EXPERTS // 2 - 1, 4, 4))
            pe.wait_ge(rw_ready, EXPERTS)
            for h in range(2):
                scatter(1, h)
                for t in range(4 * h, 4 * h + 4):
                    for c in range(KC):
                        ins = nc.tensor.matmul(y[:, t, c * P:(c + 1) * P], av[:, c, t * P:(t + 1) * P], ident[:],
                                               start=False, stop=t % 2 == 1 and c == KC - 1, skip_group_check=True)
                ins.then_inc(y_done, 1)

        @block.vector
        def _(dve):
            for s_, per in ((stage_read_dve, ND - NEXT - LATE), (smax_done, NS), (p_norm, NS), (recip_done, NS),
                            (gmin_done, 2), (grecip_done, 2), (pg_ready, 2), (pt_lo, NP), (out_lo, 3), (clip_done, 4),
                            (glu_done, 4), (h_ready, 4), (h1_lo, 2)):
                dve.sem_inc(s_, per)
            seq = 0

            def step(ins):
                nonlocal seq
                ins.then_inc(vseq, 1)
                seq += 1
                dve.wait_ge(vseq, seq)

            V = nc.vector
            for n in range(2):
                for ap in (xT[n][:, :, 0:HALF], xT[n][:, :, HALF + T:TP], kw[n][:, 0, 0:HALF],
                           kw[n][:, NT - 1, WIN - HALF:WIN]):
                    V.memset(ap.bitcast(F32), 0.0)
                V.memset(qT[n][:, 0:HALF].bitcast(F32), 0.0)
            V.memset(pr[:, :, KW:2 * P], 0.0)
            step(V.memset(pg[:], 0.0))
            dve.sem_inc(zeroed, 1)

            def layer_norm(xn, sq):
                for t in range(NT):
                    V.bn_stats(stats[:, t, :], acc[:, t, :])
                step(V.memset(small[:, 0:1], 0.0))
                for t in range(NT):
                    V.bn_aggr(mv[:, t, :], stats[:, t, :])
                step(V.memset(small[:, 0:1], 0.0))
                V.tensor_scalar(sd[:, 0], mv[:, :, 1], EPS, None, ALU.add).then_inc(sqrt_done, 1)
                dve.wait_ge(sqrt_done, sq)
                step(V.reciprocal(sd[:, 2], sd[:, 1]))
                step(V.tensor_tensor(sd[:, 3], sd[:, 0], sd[:, 2], ALU.mult))
                step(V.tensor_tensor(sd[:, 2], sd[:, 3], sd[:, 1], ALU.add))
                step(V.tensor_scalar(sd[:, 3], sd[:, 2], 0.5, None, ALU.mult))
                step(V.reciprocal(sd[:, 2], sd[:, 3]))
                for t in range(NT):
                    V.tensor_scalar(xn[:, t, :], acc[:, t, :], mv[:, t, 0:1], sd[:, 2, t:t + 1],
                                    ALU.subtract, ALU.mult).then_inc(xn_ready, 1)

            dve.wait_ge(x_in, 16)
            layer_norm(xn, 2)
            for k in range(KC):
                dve.wait_ge(xT_hi, k + 1)
                V.tensor_tensor(xT[1][:, k, HALF:HALF + T], stage[:, k, :],
                                xT[0][:, k, HALF:HALF + T].bitcast(F32), ALU.subtract).then_inc(xT_lo, 1)
            dve.wait_ge(small_hi, 1)
            V.tensor_tensor(rwT[1][:], ps_s[:, 0:KC * EXPERTS].rearrange("p (k e) -> p k e", k=KC),
                            rwT[0][:].bitcast(F32), ALU.subtract).then_inc(rwT_ready, 1)
            b0 = KC * EXPERTS
            V.tensor_copy(ebias[:, 0], ps_s[:, b0:b0 + 2 * EXPERTS].rearrange("p (c e) -> p c e", c=2))
            step(V.tensor_scalar(ebias[:, 1], ps_s[:, b0 + 2 * EXPERTS:b0 + 4 * EXPERTS].rearrange(
                "p (c e) -> p c e", c=2), 1.0, 0.5, ALU.add, ALU.mult))

            def q_lo(i, j):
                dve.wait_ge(qkv_hi, after(i, 8, 3 - 2 * j))
                V.scalar_tensor_tensor(qT[1][:, HALF:HALF + T], stage_of(f"q{j}"), -SCALE,
                                       qT[0][:, HALF:HALF + T].bitcast(F32), ALU.mult, ALU.subtract)\
                    .then_inc(stage_read_dve, 1)

            def k_lo(i, j):
                dve.wait_ge(qkv_hi, after(i, 8, 4 - 2 * j))
                for (hi, src), (lo, _) in zip(k_windows(kw[0], stage_of(f"k{j}")), k_windows(kw[1], stage_of(f"k{j}"))):
                    ins = V.tensor_tensor(lo, src, hi.bitcast(F32), ALU.subtract)
                ins.then_inc(stage_read_dve, 1)

            def v_lo(i, v):
                a, b = V_TILES[v]
                dve.wait_ge(qkv_hi, after(i, 8, 5 + v))
                src = stage_of(f"v{v}")[:, 0:(b - a) * 2 * HD].rearrange("p (t n) -> p t n", n=2 * HD)
                V.tensor_tensor(vp[1][:, a:b, :], src, vp[0][:, a:b, :].bitcast(F32), ALU.subtract)\
                    .then_inc(stage_read_dve, 3 if v == 3 and isinstance(i, int) else 1)

            q_lo(-1, 0)
            k_lo(-1, 0)
            for v in range(4):
                v_lo(-1, v)

            dve.wait_ge(consts, 2)
            dve.wait_ge(logits_full, 1)
            step(V.tensor_tensor(lg[:], ps_t[:, 0:NT * EXPERTS].rearrange("p (t e) -> p t e", t=NT),
                                 rb_bc[:].unsqueeze(1).broadcast_to([P, NT, EXPERTS]), ALU.add))
            for t in range(NT):
                V.max(top8[:, t, :], lg[:, t, :])
            step(V.memset(small[:, 0:1], 0.0))
            for t in range(NT):
                V.max_index(topi[:, t, :], top8[:, t, :], lg[:, t, :])
            V.tensor_tensor(topw[:], top8[:, :, 0:TOPK], top8[:, :, 0:1].broadcast_to([P, NT, TOPK]),
                            ALU.subtract).then_inc(top_sub, 1)
            step(V.memset(small[:, 0:1], 0.0))
            step(V.tensor_copy(topif[:], topi[:, :, 0:TOPK]))
            dve.wait_ge(top_exp, 1)
            step(V.tensor_reduce(rsum[:], topw[:], AX_X, ALU.add))
            step(V.reciprocal(rsum[:], rsum[:]))
            step(V.tensor_tensor(topw[:], topw[:], rsum[:].unsqueeze(2).broadcast_to([P, NT, TOPK]), ALU.mult))
            sc_te = scores[:].rearrange("p e t -> p t e")
            for n in range(TOPK):
                dst = sc_te if n == 0 else onehot[:]
                step(V.tensor_tensor(dst, iota16[:].unsqueeze(1).broadcast_to([P, NT, EXPERTS]),
                                     topif[:, :, n:n + 1].broadcast_to([P, NT, EXPERTS]), ALU.is_equal))
                step(V.tensor_tensor(dst, dst, topw[:, :, n:n + 1].broadcast_to([P, NT, EXPERTS]), ALU.mult))
                if n:
                    step(V.tensor_tensor(sc_te, sc_te, onehot[:], ALU.add))
            V.memset(small[:, 0:1], 0.0).then_inc(scores_ready, 1)
            dve.wait_ge(scT_full, 1)
            V.tensor_copy(scT, ps_o[0:EXPERTS, :]).then_inc(scT_ready, 1)
            for q in range(2):
                dve.wait_ge(stage_full, full(-1, f"wo{q}"))
                V.tensor_tensor(acc[:, 4 * q:4 * q + 4, :], acc[:, 4 * q:4 * q + 4, :],
                                stage_of(f"wo{q}").rearrange("p (t h) -> p t h", h=H), ALU.add)\
                    .then_inc(stage_read_dve, 1)

            def body(i, more):
                def smax(j, s):
                    n = NT * j + s
                    dve.wait_ge(scores_full, after(i, NS, n + 1))
                    dve.wait_ge(exp_done, after(i, NS, n - 1))
                    dve.sem_inc(held, 1)
                    V.tensor_tensor_reduce(sm[:, n % 2, :], ps_s[:, 0:KW],
                                           mask[:, 0 if s == 0 else 2 if s == NT - 1 else 1, :],
                                           1.0, 3e38, ALU.add, ALU.min, nm[:, n % 2:n % 2 + 1]).then_inc(smax_done, 1)

                def normalise(n):
                    dve.wait_ge(exp_done, after(i, NS, n + 1))
                    V.reciprocal(rr[:, n % 2:n % 2 + 1], rs[:, n % 2:n % 2 + 1]).then_inc(recip_done, 1)
                    dve.wait_ge(recip_done, after(i, NS, n + 1))
                    V.tensor_scalar(pr[:, n % 2, 0:KW], pr[:, n % 2, 0:KW], rr[:, n % 2:n % 2 + 1], None,
                                    ALU.mult).then_inc(p_norm, 1)

                def probs_lo(n):
                    dve.wait_ge(pt_hi, after(i, NP, n + 1))
                    V.tensor_tensor(pT[1][:, n % 2, :], ps_t[:, 0:2 * P], pT[0][:, n % 2, :].bitcast(F32),
                                    ALU.subtract).then_inc(pt_lo, 1)

                def global_min(j):
                    rows = slice(HALF * j, HALF * j + GLOBALS)
                    dve.wait_ge(stage_full, full(i, f"sg{j}"))
                    V.tensor_reduce(gm[rows, 0:1], stage_of(f"sg{j}")[rows, :], AX_X, ALU.min).then_inc(gmin_done, 1)

                def global_normalise(j):
                    rows = slice(HALF * j, HALF * j + GLOBALS)
                    dve.wait_ge(stage_read_act, read_act(i, f"sg{j}"))
                    V.reciprocal(gr[rows, 0:1], gs[rows, 0:1]).then_inc(grecip_done, 1)
                    dve.wait_ge(grecip_done, after(i, 2, j + 1))
                    V.tensor_scalar(pg[rows, HALF:HALF + T], pg[rows, HALF:HALF + T], gr[rows, 0:1], None,
                                    ALU.mult).then_inc(pg_ready, 1)

                def gate(j, c):
                    dve.wait_ge(stage_full, full(i, f"gate{c}{j}"))
                    V.tensor_scalar(ff[:, 0], stage_of(f"gate{c}{j}"), ebias[:, 0, c, bass.ds(i * 2 + j, 1)], LIMIT,
                                    ALU.add, ALU.min)\
                        .then_inc(stage_read_dve, 1 + NEXT if j == 1 and c == 1 and not more else 1)

                def glu(j, c):
                    dve.wait_ge(tanh_done, after(i, 4, 2 * j + c + 1))
                    V.scalar_tensor_tensor(ff[:, 1], ff[:, 1], 1.0, ff[:, 0], ALU.add, ALU.mult).then_inc(glu_done, 1)

                def clip(j, c):
                    dve.wait_ge(stage_read_act, read_act(i, f"up{c}{j}"))
                    V.tensor_scalar(ff[:, 2], ff[:, 2], (LIMIT + 1) / 2, (1 - LIMIT) / 2, ALU.min, ALU.max)\
                        .then_inc(clip_done, 1)

                def hidden(j, c):
                    dve.wait_ge(glu_done, after(i, 4, 2 * j + c + 1))
                    dve.wait_ge(clip_done, after(i, 4, 2 * j + c + 1))
                    V.tensor_tensor(ff[:, 2], ff[:, 2], ff[:, 1], ALU.mult).then_inc(h_ready, 1)

                def hidden_lo(j):
                    dve.wait_ge(h_hi, after(i, 4, 2 * j + 2))
                    V.tensor_tensor(hh[1][:, 1], ff[:, 2], hh[0][:, 1].bitcast(F32), ALU.subtract).then_inc(h1_lo, 1)

                def head(j):
                    for s in range(NT):
                        smax(j, s)
                        if s == 2:
                            gate(j, 0)
                        if s == 4:
                            glu(j, 0)
                        if s == 5:
                            clip(j, 0)
                        if s == 6:
                            hidden(j, 0)
                        normalise(NT * j + s)
                        if s == 0:
                            global_min(j)
                        if s:
                            probs_lo(NT * j + s - 1)
                        if s == 3:
                            global_normalise(j)
                        if s == 6:
                            gate(j, 1)
                    glu(j, 1)
                    clip(j, 1)
                    probs_lo(NT * j + NT - 1)
                    hidden(j, 1)
                    if j == 0 or more:
                        q_lo(i, 1 - j)
                    hidden_lo(j)
                    if j == 0 or more:
                        k_lo(i, 1 - j)
                    if j == 1:
                        dve.wait_ge(pt_hi, after(i, NP, NP))
                        V.tensor_tensor(pgT[:, :, 1, :], ps_t[:, 0:VT * GR].rearrange("p (t g) -> p t g", t=VT),
                                        pgT[:, :, 0, :].bitcast(F32), ALU.subtract).then_inc(pt_lo, 1)
                    dve.wait_ge(out_hi, after(i, 3, j + 1))
                    V.tensor_tensor(oT[1][:, j, GLOBALS:T], ps_o[:, GLOBALS:T], oT[0][:, j, GLOBALS:T].bitcast(F32),
                                    ALU.subtract).then_inc(out_lo, 1)

                def down(j):
                    for q in range(2):
                        dve.wait_ge(stage_full, full(i, f"down{q}{j}"))
                        dve.wait_ge(stage_read_dve, after(i, ND, 0) if j == 0 else read_dve(i, "down10"))
                        for t in range(4):
                            tt = 4 * q + t
                            ins = V.scalar_tensor_tensor(acc[:, tt, :], stage_of(f"down{q}{j}")[:, t * H:(t + 1) * H],
                                                         scores[:, bass.ds(i * 2 + j, 1), tt], acc[:, tt, :],
                                                         ALU.mult, ALU.add)
                        ins.then_inc(stage_read_dve, 1)

                head(0)
                down(0)
                head(1)
                if more:
                    v_lo(i, 0)
                    v_lo(i, 1)
                dve.wait_ge(out_hi, after(i, 3, 3))
                V.tensor_tensor(oT[1][:, :, 0:GLOBALS], ps_t[:, 0:2 * GLOBALS].rearrange("p (j c) -> p j c", j=2),
                                oT[0][:, :, 0:GLOBALS].bitcast(F32), ALU.subtract).then_inc(out_lo, 1)
                if more:
                    v_lo(i, 2)
                    v_lo(i, 3)
                down(1)
                dve.wait_ge(stage_read_dve, read_dve(i, "down11"))
                for q in range(2):
                    dve.wait_ge(stage_full, full(i, f"wo{q}"))
                    V.tensor_tensor(acc[:, 4 * q:4 * q + 4, :], acc[:, 4 * q:4 * q + 4, :],
                                    stage_of(f"wo{q}").rearrange("p (t h) -> p t h", h=H), ALU.add)\
                        .then_inc(stage_read_dve, 1)

            with dve.Fori(0, PAIRS - 1) as i:
                body(i, True)
            body(PAIRS - 1, False)

            for s_, per in ((pmt_ready, 4), (gs2_done, 2), (mid_ready, 2), (mt_lo, 2), (eo_lo, 2)):
                dve.sem_inc(s_, per)
            dve.wait_ge(stage_read_dve, read_dve(PAIRS - 1, "wo1"))
            layer_norm(xn2, 4)
            V.memset(x2T[0][:, :, 0:1].bitcast(F32), 0.0)
            V.memset(slotT[:], 0.0)
            V.memset(x2T[1][:, :, 0:1].bitcast(F32), 0.0).then_inc(zeros2, 1)

            def ring_lo(u, dst, src, hi):
                dve.wait_ge(ring_hi, [v for v, r in RING if r == "dve"].index(u) + 1)
                V.tensor_tensor(dst, src, hi.bitcast(F32), ALU.subtract).then_inc(ring_dve, 1)

            for n, u in enumerate(("wkT", "wvT", "wrT")):
                ring_lo(u, kvrT[1][:, n], ring_of(u).rearrange("p (k e) -> p k e", k=KC), kvrT[0][:, n])
            ring_lo("gwT", gwT[1][:], ring_of("gwT")[:, 0:KC * EXPERTS].rearrange("p (k e) -> p k e", k=KC), gwT[0][:])
            for k in range(KC):
                for h in range(2):
                    cols = slice(1 + h * 512, 1 + (h + 1) * 512)
                    ring_lo(f"xT{k}{h}", x2T[1][:, k, cols], ring_of(f"xT{k}{h}"), x2T[0][:, k, cols])

            for h in range(2):
                dve.wait_ge(rows_hi, h + 1)
                V.tensor_tensor(xr[1][:, 4 * h:4 * h + 4, 0:H], xn2[:, 4 * h:4 * h + 4, :],
                                xr[0][:, 4 * h:4 * h + 4, 0:H].bitcast(F32), ALU.subtract).then_inc(rows_lo, 1)
            for g in range(2):
                dve.wait_ge(l1_w_hi, g + 1)
                V.tensor_tensor(sgu[1][:, g], sgu_raw[:, g], sgu[0][:, g].bitcast(F32), ALU.subtract).then_inc(l1_w_lo, 1)
            dve.wait_ge(ring_full, RNAMES.index("logits") + 1)
            V.tensor_copy(lg[:], ring_of("logits")[:, 0:NT * EXPERTS].rearrange("p (t e) -> p t e", t=NT))\
                .then_inc(ring_dve, 1)
            dve.wait_ge(ring_dve, ring_reads("logits", "dve"))
            for t in range(NT):
                V.max(top8[:, t, :], lg[:, t, :])
            step(V.memset(small[:, 0:1], 0.0))
            V.tensor_tensor(topw[:], top8[:, :, 0:TOPK], top8[:, :, 0:1].broadcast_to([P, NT, TOPK]), ALU.subtract)
            V.tensor_tensor(alls[:], lg[:], top8[:, :, 0:1].broadcast_to([P, NT, EXPERTS]),
                            ALU.subtract).then_inc(l1_sub, 1)
            for t in range(NT):
                V.max_index(topi[:, t, :], top8[:, t, :], lg[:, t, :])
            step(V.memset(small[:, 0:1], 0.0))
            step(V.tensor_copy(topif[:], topi[:, :, 0:TOPK]))
            dve.wait_ge(l1_exp, 1)
            step(V.tensor_reduce(rsum[:], alls[:], AX_X, ALU.add))
            step(V.reciprocal(rsum[:], rsum[:]))
            step(V.tensor_tensor(topw[:], topw[:], rsum[:].unsqueeze(2).broadcast_to([P, NT, TOPK]), ALU.mult))
            step(V.tensor_reduce(rsum[:], topw[:], AX_X, ALU.add))
            step(V.tensor_scalar(rsum[:], rsum[:], 1e-20, None, ALU.add))
            step(V.reciprocal(rsum[:], rsum[:]))
            step(V.tensor_tensor(topw[:], topw[:], rsum[:].unsqueeze(2).broadcast_to([P, NT, TOPK]), ALU.mult))
            for n in range(TOPK):
                one, weighted = (chosen, w16) if n == 0 else (onehot, alls)
                step(V.tensor_tensor(one[:], iota16[:].unsqueeze(1).broadcast_to([P, NT, EXPERTS]),
                                     topif[:, :, n:n + 1].broadcast_to([P, NT, EXPERTS]), ALU.is_equal))
                step(V.tensor_tensor(weighted[:], one[:], topw[:, :, n:n + 1].broadcast_to([P, NT, EXPERTS]), ALU.mult))
                if n:
                    V.tensor_tensor(chosen[:], chosen[:], onehot[:], ALU.add)
                    step(V.tensor_tensor(w16[:], w16[:], alls[:], ALU.add))
            V.tensor_copy(chosen_b[:], chosen[:]).then_inc(chosen_ready, 1)
            step(V.tensor_copy(xr[0][:, :, H:GW], w16[:]))
            V.tensor_tensor(xr[1][:, :, H:GW], w16[:], xr[0][:, :, H:GW].bitcast(F32), ALU.subtract)\
                .then_inc(rows_lo, 1)
            def recurrence(c):
                dve.wait_ge(ring_act, ring_reads(f"r{c}1", "act"))
                w = decay[:, c:c + 1].broadcast_to([P, T])
                V.tensor_tensor_scan(den[:, c], w, ek[:, c], 0.0, ALU.mult, ALU.add)
                step(V.tensor_tensor(av[:, c], av[:, c], ek[:, c], ALU.mult))
                step(V.tensor_tensor_scan(ek[:, c], w, av[:, c], 0.0, ALU.mult, ALU.add))
                V.tensor_scalar(den[:, c], den[:, c], 1e-8, None, ALU.add)
                step(V.tensor_tensor(ek[:, c], ek[:, c], rT[:, c], ALU.mult))

            dve.wait_ge(decay_ready, 1)
            recurrence(0)
            dve.wait_ge(ring_full, RNAMES.index("pos") + 1)
            slot_te = slot[:].rearrange("p e t -> p t e")
            V.scalar_tensor_tensor(slot_te, ring_of("pos")[:, 0:NT * EXPERTS].rearrange("p (t e) -> p t e", t=NT),
                                   -NONE, chosen[:], ALU.add, ALU.mult).then_inc(ring_dve, 1)
            dve.wait_ge(ring_dve, ring_reads("pos", "dve"))
            V.tensor_scalar(slot[:], slot[:], NONE, None, ALU.add).then_inc(slots_ready, 1)

            def shared_lo(n):
                c, h = n // 2, n % 2
                w = S_CHUNKS[c][1] - S_CHUNKS[c][0]
                dve.wait_ge(sT_hi, n + 1)
                hi = sT[0][0:w, c, h * 512:(h + 1) * 512]
                V.tensor_tensor(sT[1][0:w, c, h * 512:(h + 1) * 512], st[0:w, n % 2], hi.bitcast(F32), ALU.subtract)\
                    .then_inc(sT_lo, 1)

            def shared_unit(n):
                c, h = n // 2, n % 2
                w = S_CHUNKS[c][1] - S_CHUNKS[c][0]
                dve.wait_ge(st_tanh, n + 1)
                V.scalar_tensor_tensor(st[0:w, n % 2], st[0:w, n % 2], 1.0, ring_of(f"sg{c}{h}")[0:w, :],
                                       ALU.add, ALU.mult).then_inc(ring_dve, 1)
                dve.wait_ge(ring_dve, ring_reads(f"sg{c}{h}", "dve"))
                dve.wait_ge(ring_full, RNAMES.index(f"su{c}{h}") + 1)
                V.scalar_tensor_tensor(st[0:w, n % 2], st[0:w, n % 2], 0.5, ring_of(f"su{c}{h}")[0:w, :],
                                       ALU.mult, ALU.mult).then_inc(ring_dve, 1)
                dve.wait_ge(ring_dve, ring_reads(f"su{c}{h}", "dve"))
                V.memset(small[:, 1:2], 0.0).then_inc(smid_done, 1)

            for n in range(4):
                shared_unit(n)
                if n:
                    shared_lo(n - 1)
            dve.wait_ge(l1_w_hi, 3)
            V.tensor_tensor(sdw[1][:, 0:2], sd_raw[:, 0:2], sdw[0][:, 0:2].bitcast(F32), ALU.subtract)
            V.tensor_tensor(sdw[1][0:SD - 2 * P, 2], sd_raw[0:SD - 2 * P, 2], sdw[0][0:SD - 2 * P, 2].bitcast(F32),
                            ALU.subtract).then_inc(l1_w_lo, 1)
            dve.wait_ge(zeros2, 1)
            for h in range(2):
                dve.wait_ge(ring_full, RNAMES.index(f"slots{h}") + 1)
                V.tensor_copy(slotT[0:EXPERTS, h * 512:(h + 1) * 512], ring_of(f"slots{h}")[0:EXPERTS, :])\
                    .then_inc(ring_dve, 1)
            shared_lo(3)

            def slot_matrix(e, b):
                row = slot[:, e, :] if isinstance(e, int) else slot[:, bass.ds(e, 1), :].rearrange("p a t -> p (a t)")
                V.tensor_tensor(pmat[:, b], iota_c[:].unsqueeze(1).broadcast_to([P, NT, CAP]),
                                row.unsqueeze(2).broadcast_to([P, NT, CAP]), ALU.is_equal).then_inc(pm_ready, 1)

            dve.wait_ge(slots_ready, 1)
            slot_matrix(0, 0)
            for n in (4, 5):
                shared_unit(n)
                if n == 5:
                    shared_lo(4)
            shared_lo(5)

            recurrence(1)
            slot_matrix(1, 1)

            def slot_weights(col, count):
                dve.wait_ge(xg_copied, count)
                V.tensor_scalar(wsc[:], xg[:, col], 0.5, None, ALU.mult).then_inc(wsc_ready, 1)

            def rows_lo_parts(count):
                dve.wait_ge(xgt_hi, count)
                V.tensor_tensor(xgT[1][:], ps_f[:, 0:H].rearrange("p (k c) -> p k c", k=KC),
                                xgT[0][:].bitcast(F32), ALU.subtract).then_inc(xgt_lo, 1)

            slot_weights(slice(H, H + 1), 1)
            rows_lo_parts(1)

            def step2(i, b, more, last):
                n = b + 1

                def transposed(h):
                    dve.wait_ge(sb_full, after(i, 4, 2 * b + h + 1))
                    dve.wait_ge(sc_done, after(i, 2, b))
                    V.tensor_scalar(pmT[:, b, h * 512:(h + 1) * 512], ps_b, iota_p[:, 0:1], None, ALU.is_equal)\
                        .then_inc(pmt_ready, 1)

                transposed(0)
                dve.wait_ge(tanh2_done, after(i, 2, n))
                V.scalar_tensor_tensor(gs2[:], tt2[:], 1.0, ps_f[:, 0:ID], ALU.add, ALU.mult).then_inc(gs2_done, 1)
                dve.wait_ge(gs2_done, after(i, 2, n))
                dve.wait_ge(wsc_ready, i * 2 + n)
                dve.wait_ge(mt_full, after(i, 2, b))
                V.scalar_tensor_tensor(mid[:], gs2[:], wsc[:, 0:1], ps_f[:, ID:2 * ID], ALU.mult, ALU.mult)\
                    .then_inc(mid_ready, 1)
                if more:
                    dve.wait_ge(g_full, i * 2 + n)
                    slot_matrix(i * 2 + (b + 2), b)
                if not last:
                    dve.wait_ge(mid_ready, after(i, 2, n))
                    slot_weights(bass.ds(i * 2 + (H + b + 1), 1), i * 2 + (n + 1))
                dve.wait_ge(mt_hi, after(i, 2, n))
                V.tensor_tensor(midT[1][:], ps_x[0:IC, 0:2 * CAP].rearrange("p (c t) -> p c t", c=2),
                                midT[0][:].bitcast(F32), ALU.subtract).then_inc(mt_lo, 1)
                if not last:
                    rows_lo_parts(i * 2 + (n + 1))
                transposed(1)
                cols = bass.ds(i * P, P)
                V.reciprocal(den[:, b, cols], den[:, b, cols]).then_inc(rden_done, 1)
                dve.wait_ge(rden_done, i * 2 + n)
                V.tensor_tensor(av[:, b, cols], ek[:, b, cols], den[:, b, cols], ALU.mult).then_inc(rw_ready, 1)
                dve.wait_ge(eo_hi, after(i, 2, n))
                V.tensor_tensor(eo[1][:], ps_g[:, 0:H], eo[0][:].bitcast(F32), ALU.subtract).then_inc(eo_lo, 1)

            with dve.Fori(0, EXPERTS // 2 - 1) as i:
                step2(i, 0, True, False)
                step2(i, 1, True, False)
            step2(EXPERTS // 2 - 1, 0, False, False)
            step2(EXPERTS // 2 - 1, 1, False, True)
            for q in range(2):
                dve.wait_ge(y_done, q + 1)
                V.tensor_tensor(acc[:, 4 * q:4 * q + 4, :], acc[:, 4 * q:4 * q + 4, :], y[:, 4 * q:4 * q + 4, :],
                                ALU.add).then_inc(out_ready, 1)


_INS = ['L0_attn_hidden_states', 'L0_attn_Wq', 'L0_attn_Wk', 'L0_attn_Wv', 'L0_attn_Wo', 'L0_ffn_router_weight',
        'L0_ffn_router_bias', 'L0_ffn_gate_up_proj', 'L0_ffn_gate_up_proj_bias', 'L0_ffn_down_proj',
        'L0_ffn_down_proj_bias']
_L1 = ['L1_attn_Wk', 'L1_attn_Wv', 'L1_attn_Wr', 'L1_attn_time_decay', 'L1_ffn_gate_w', 'L1_ffn_w_gate',
       'L1_ffn_w_up', 'L1_ffn_w_down', 'L1_ffn_sw_gate', 'L1_ffn_sw_up', 'L1_ffn_sw_down']


def kernel(**inputs):
    import numpy as np
    import concourse.bacc as bacc
    from concourse.bass_utils import run_bass_kernel_spmd as run

    nc = bacc.Bacc("TRN2", target_bir_lowering=False, num_devices=1)
    arrays, aps = {}, {}
    for name in _INS + _L1:
        a = np.ascontiguousarray(inputs[name])
        arrays[f"in_{name}"] = a
        aps[name] = nc.dram_tensor(f"in_{name}", a.shape, mybir.dt.from_np(a.dtype), kind="ExternalInput").ap()
    out = nc.dram_tensor("out_x", (1, T, H), F32, kind="ExternalOutput").ap()
    build(nc, aps[_INS[0]][0], *[aps[n] for n in _INS[1:]], {n.split('_', 2)[2]: aps[n] for n in _L1}, out[0])
    r = run(nc, [arrays], core_ids=[0])
    return r.results[0]["out_x"]
```

```python
from contextlib import ExitStack

import concourse.bass as bass
from concourse import mybir

F32 = mybir.dt.float32
F32R = mybir.dt.float32r
BF16 = mybir.dt.bfloat16
U32 = mybir.dt.uint32
ALU = mybir.AluOpType
ACT = mybir.ActivationFunctionType
AX_X = mybir.AxisListType.X

P = 128
T, H = 1024, 256
NT, KC = T // P, H // P
HEADS, HD = 16, 128
PAIRS = HEADS // 2
WINDOW, GLOBALS = 64, 16
HALF = WINDOW // 2
SCALE = HD ** -0.5
WIN = P + WINDOW
KW = WIN + GLOBALS
VT = NT + 1
TP = VT * P
KB = WIN - P + GLOBALS
EXPERTS, FD, TOPK = 16, 256, 4
ALPHA, LIMIT = 1.702, 7.0
EPS = 1e-5
OUTSIDE = 1e30

UNITS = (["sg0", "gate00", "up00", "gate10", "up10", "q1", "k1", "down00", "down10",
          "sg1", "gate01", "up01", "gate11", "up11", "q0", "k0", "v0", "v1", "v2", "v3", "down01", "down11",
          "wo0", "wo1"])
NEXT = 6
LATE = 4
NU = len(UNITS)
BY_ACT = [u for u in UNITS if u[:2] in ("sg", "up")]
BY_DVE = [u for u in UNITS if u not in BY_ACT]
NA, ND = len(BY_ACT), len(BY_DVE)
V_TILES = [(0, 3), (3, 5), (5, 7), (7, 9)]
NS = 2 * NT
NP = NS + 1
GR = HALF + GLOBALS
NW = 10

ID = 176
IC = ID // 2
SD = 352
S_CHUNKS = [(0, 128), (128, 256), (256, 352)]
CAP = 128
GW = H + EXPERTS
NONE = 999.0
RING = ([(u, "dve") for u in ("wkT", "wvT", "wrT", "gwT", "xT00", "xT10", "xT01", "xT11")] +
        [(u, "act") for u in ("lgT0", "lgT1", "k00", "k01")] + [("logits", "dve")] +
        [(f"{u}{c}{h}", "act") for c in range(2) for u in "kvr" for h in range(2) if (u, c) != ("k", 0)] +
        [("pos", "dve")] +
        [(f"{u}{c}{h}", "dve") for c in range(2) for h in range(2) for u in ("sg", "su")] +
        [("slots0", "dve"), ("slots1", "dve")] +
        [(f"{u}2{h}", "dve") for h in range(2) for u in ("sg", "su")])
RNAMES = [u for u, _ in RING]


def after(i, per, n):
    return i * per + (per + n)


def half(h):
    return slice(h * T // 2, (h + 1) * T // 2)


def full(i, u):
    return after(i, NU, UNITS.index(u) + 1)


def read_dve(i, u):
    return after(i, ND, BY_DVE.index(u) + 1)


def read_act(i, u):
    return after(i, NA, BY_ACT.index(u) + 1)


def ring_reads(u, reader):
    return sum(r == reader for _, r in RING[:RNAMES.index(u) + 1])


def build(nc, x, wq, wk, wv, wo, rw, rb, gup, gub, dnp, dnb, l1, out):
    with ExitStack() as ctx:
        def sb(name, shape, dt=F32, c=ctx):
            return c.enter_context(nc.sbuf_tensor(name, shape, dt))

        def sem(name):
            return ctx.enter_context(nc.semaphore(name))

        ident = sb("ident", [P, P])
        acc = sb("acc", [P, NT, H])
        iota16 = sb("iota16", [P, EXPERTS])
        top8 = sb("top8", [P, NT, 8])
        topi = sb("topi", [P, NT, 8], U32)
        topif = sb("topif", [P, NT, TOPK])
        topw = sb("topw", [P, NT, TOPK])
        onehot = sb("onehot", [P, NT, EXPERTS])
        stats = sb("stats", [P, NT, 6])
        mv = sb("mv", [P, NT, 2])
        sd = sb("sd", [P, 4, NT])
        lg = sb("lg", [P, NT, EXPERTS])
        scores = sb("scores", [P, EXPERTS, NT])
        rsum = sb("rsum", [P, NT])
        small = sb("small", [P, 8])

        qkv_raw = sb("qkv_raw", [P, 3, KC, 2 * HD])
        kvr_raw = qkv_raw
        gw_raw = sb("gw_raw", [EXPERTS, H])
        td = sb("td", [P, KC])
        warm = sb("warm", [P, 1])

        l0 = ctx.enter_context(ExitStack())
        s0 = lambda name, shape, dt=F32: sb(name, shape, dt, l0)
        mask = s0("mask", [P, 3, KW])
        rb_bc = s0("rb_bc", [P, EXPERTS])
        rw_raw = s0("rw_raw", [EXPERTS, H])
        rwT = [s0(f"rwT{n}", [P, KC, EXPERTS], F32R) for n in "hl"]
        gub_raw = s0("gub_raw", [EXPERTS, 2 * FD])
        ebias = s0("ebias", [P, 2, 2, EXPERTS])
        dnb_sb = s0("dnb_sb", [EXPERTS, H])
        xT = [s0(f"xT{n}", [P, KC, TP], F32R) for n in "hl"]
        qT = [s0(f"qT{n}", [P, HALF + T], F32R) for n in "hl"]
        kw = [s0(f"kw{n}", [P, NT, KW], F32R) for n in "hl"]
        vp = [s0(f"vp{n}", [P, VT, 2 * HD], F32R) for n in "hl"]
        vb = [s0(f"vb{n}", [P, NT, 2 * HD], F32R) for n in "hl"]
        sm = s0("sm", [P, 2, KW])
        pr = s0("pr", [P, 2, 2 * P])
        nm = s0("nm", [P, 2])
        rs = s0("rs", [P, 2])
        rr = s0("rr", [P, 2])
        gm = s0("gm", [GR, 1])
        gs = s0("gs", [GR, 1])
        gr = s0("gr", [GR, 1])
        pg = s0("pg", [GR, TP])
        pgT = s0("pgT", [P, VT, 2, GR], F32R)
        og = s0("og", [2 * GR, 2 * HD])
        og_sum = s0("og_sum", [2 * GR, 2, GLOBALS])
        pT = [s0(f"pT{n}", [P, 2, 2 * P], F32R) for n in "hl"]
        oT = [s0(f"oT{n}", [P, 2, T], F32R) for n in "hl"]
        wo_raw = s0("wo_raw", [P, 2, H])
        gu_raw = s0("gu_raw", [P, KC, 2 * FD])
        dn_raw = s0("dn_raw", [P, 2, H])
        qkvw = [s0(f"qkvw{n}", [P, 3, KC, 2 * HD], F32R) for n in "hl"]
        wow = [s0(f"wow{n}", [P, 2, H], F32R) for n in "hl"]
        guw = [s0(f"guw{n}", [P, 2, KC, 2, FD], F32R) for n in "hl"]
        dnw = [s0(f"dnw{n}", [P, 2, 2, H], F32R) for n in "hl"]
        ff = s0("ff", [P, 3, T])
        hh = [s0(f"hh{n}", [P, 2, T], F32R) for n in "hl"]
        xn = ff[:, 0:2, :].rearrange("p a (b h) -> p (a b) h", h=H)
        scT = ff[0:EXPERTS, 2, :]

        l0.close()

        gwT = [sb(f"gwT{n}", [P, KC, EXPERTS], F32R) for n in "hl"]
        decay = sb("decay", [P, KC])
        xr = [sb(f"xr{n}", [P, NT, GW], F32R) for n in "hl"]
        x2T = [sb(f"x2T{n}", [P, KC, T + 2], F32R) for n in "hl"]
        kvrT = [sb(f"kvrT{n}", [P, 3, KC, H], F32R) for n in "hl"]
        sgu_raw = sb("sgu_raw", [P, 2, KC, SD])
        sgu = [sb(f"sgu{n}", [P, 2, KC, SD], F32R) for n in "hl"]
        sd_raw = sb("sd_raw", [P, 3, H])
        sdw = [sb(f"sdw{n}", [P, 3, H], F32R) for n in "hl"]
        eg_raw = sb("eg_raw", [P, 2, KC, 2, ID])
        ed_raw = sb("ed_raw", [IC, 2, 2, H])
        egw = [sb(f"egw{n}", [P, 2, KC, 2, ID], F32R) for n in "hl"]
        edw = [sb(f"edw{n}", [IC, 2, 2, H], F32R) for n in "hl"]
        xn2 = sb("xn2", [P, NT, H])
        ek = xn2[:].rearrange("p (c t) h -> p c (t h)", c=KC)
        av = sb("av", [P, KC, T])
        rT = sb("rT", [P, KC, T])
        den = sb("den", [P, KC, T])
        st = sb("st", [P, 2, 512])
        lgT2 = st[0:EXPERTS].rearrange("p a t -> p (a t)")
        sT = [sb(f"sT{n}", [P, 3, T], F32R) for n in "hl"]
        room = kvr_raw[:].rearrange("p n k d -> p (n k d)")
        tt2, gs2, mid = (room[:, n * ID:(n + 1) * ID] for n in range(3))
        xg = room[:, 3 * ID:3 * ID + GW]
        alls, chosen, w16 = (room[:, 1024 + n * P:1024 + (n + 1) * P].rearrange("p (t e) -> p t e", t=NT)
                             for n in range(3))
        chosen_b = sb("chosen_b", [P, NT, EXPERTS], BF16)
        before = sb("before", [P, P], BF16)
        ones_b = sb("ones_b", [P, P], BF16)
        slot = sb("slot", [P, EXPERTS, NT])
        slotT = sb("slotT", [P, T], BF16)
        sel = sb("sel", [P, EXPERTS, P], BF16)
        iota_c = sb("iota_c", [P, P])
        iota_p = sb("iota_p", [P, 1])
        pmat = sb("pmat", [P, 2, NT, CAP], F32R)
        pmT = sb("pmT", [P, 2, T], F32R)
        wsc = sb("wsc", [P, 1])
        xgT = [sb(f"xgT{n}", [P, KC, CAP], F32R) for n in "hl"]
        midT = [sb(f"midT{n}", [IC, 2, CAP], F32R) for n in "hl"]
        eo = [sb(f"eo{n}", [P, H], F32R) for n in "hl"]

        pm = [ctx.enter_context(nc.psum_tensor("stage", [P, 2, T], F32)),
              ctx.enter_context(nc.psum_tensor("ps_s", [P, 512], F32)),
              ctx.enter_context(nc.psum_tensor("ps_t", [P, 512], F32)),
              ctx.enter_context(nc.psum_tensor("ps_o", [P, T], F32))]
        stage, ps_s, ps_t, ps_o = pm

        y = stage[:].rearrange("p a (b h) -> p (a b) h", h=H)
        ring = [ps_s[:], ps_t[:], ps_o[:, 0:512], ps_o[:, 512:T]]
        ps_g, ps_x, ps_f, ps_b = ring

        def ring_of(u):
            return ring[RNAMES.index(u) % 4]

        x_in = [sem(f"x_in{q}") for q in range(2)]
        small_in = sem("small_in")
        consts = sem("consts")
        pool_seq = sem("pool_seq")
        zeroed = sem("zeroed")
        vseq = sem("vseq")
        sqrt_done = sem("sqrt_done")
        xn_ready = sem("xn_ready")
        xnT_full = sem("xnT_full")
        xT_hi = sem("xT_hi")
        xT_lo = sem("xT_lo")
        small_T = sem("small_T")
        small_hi = sem("small_hi")
        rwT_ready = sem("rwT_ready")
        lgT_full = sem("lgT_full")
        lgT_copied = sem("lgT_copied")
        logits_full = sem("logits_full")
        top_sub = sem("top_sub")
        top_exp = sem("top_exp")
        scores_ready = sem("scores_ready")
        scT_full = sem("scT_full")
        scT_ready = sem("scT_ready")
        bias_full = sem("bias_full")
        bias_added = sem("bias_added")
        stage_full = sem("stage_full")
        stage_read_dve = sem("stage_read_dve")
        stage_read_act = sem("stage_read_act")
        qkv_hi = sem("qkv_hi")
        vb_ready = sem("vb_ready")
        scores_full = sem("scores_full")
        smax_done = sem("smax_done")
        exp_done = sem("exp_done")
        recip_done = sem("recip_done")
        p_norm = sem("p_norm")
        gmin_done = sem("gmin_done")
        grecip_done = sem("grecip_done")
        pg_ready = sem("pg_ready")
        pt_full = sem("pt_full")
        pt_hi = sem("pt_hi")
        pt_lo = sem("pt_lo")
        pv_done = sem("pv_done")
        og_copied = sem("og_copied")
        gcols_full = sem("gcols_full")
        out_hi = sem("out_hi")
        out_lo = sem("out_lo")
        tanh_done = sem("tanh_done")
        clip_done = sem("clip_done")
        glu_done = sem("glu_done")
        h_ready = sem("h_ready")
        h_hi = sem("h_hi")
        h0_lo = sem("h0_lo")
        h1_lo = sem("h1_lo")
        w_hi = sem("w_hi")
        w_lo = sem("w_lo")
        ex_loaded = sem("ex_loaded")
        qkv_loaded = sem("qkv_loaded")
        wo_loaded = sem("wo_loaded")
        out_stored = sem("out_stored")
        held = sem("held")

        l1_early = sem("l1_early")
        l1_loaded = sem("l1_loaded")
        l1_consts = sem("l1_consts")
        ring_full = sem("ring_full")
        ring_act = sem("ring_act")
        ring_dve = sem("ring_dve")
        zeros2 = sem("zeros2")
        decay_exp = sem("decay_exp")
        decay_ready = sem("decay_ready")
        ring_hi = sem("ring_hi")
        l1_w_hi = sem("l1_w_hi")
        l1_w_lo = sem("l1_w_lo")
        l1_sub = sem("l1_sub")
        l1_exp = sem("l1_exp")
        chosen_ready = sem("chosen_ready")
        slots_ready = sem("slots_ready")
        st_tanh = sem("st_tanh")
        smid_done = sem("smid_done")
        sT_hi = sem("sT_hi")
        sT_lo = sem("sT_lo")
        rows_hi = sem("rows_hi")
        rows_lo = sem("rows_lo")
        rden_done = sem("rden_done")
        rw_ready = sem("rw_ready")
        y_done = sem("y_done")
        out_ready = sem("out_ready")
        pm_ready = sem("pm_ready")
        g_full = sem("g_full")
        xg_copied = sem("xg_copied")
        xt_full = sem("xt_full")
        xgt_hi = sem("xgt_hi")
        xgt_lo = sem("xgt_lo")
        sb_full = sem("sb_full")
        pmt_ready = sem("pmt_ready")
        f1_full = sem("f1_full")
        tanh2_done = sem("tanh2_done")
        gs2_done = sem("gs2_done")
        mid_ready = sem("mid_ready")
        mt_full = sem("mt_full")
        mt_hi = sem("mt_hi")
        mt_lo = sem("mt_lo")
        f2_full = sem("f2_full")
        eo_hi = sem("eo_hi")
        eo_lo = sem("eo_lo")
        sc_done = sem("sc_done")
        ew_loaded = [sem(f"ew_loaded{b}") for b in range(2)]
        ew_hi = sem("ew_hi")
        ew_lo = sem("ew_lo")
        wsc_ready = sem("wsc_ready")

        block = ctx.enter_context(nc.Block())

        def k_windows(t_out, src):
            a = src[:, 0:T]
            mid = bass.AP(a.tensor, a.offset + P - HALF, [list(a.ap[0]), [P, NT - 2], [1, WIN]])
            return [(t_out[:, 1:NT - 1, 0:WIN], mid),
                    (t_out[:, 0, HALF:WIN], src[:, 0:WIN - HALF]),
                    (t_out[:, NT - 1, 0:WIN - HALF], src[:, T - WIN + HALF:T]),
                    (t_out[:, :, WIN:KW], src[:, 0:GLOBALS].unsqueeze(1).broadcast_to([P, NT, GLOBALS]))]

        def stage_of(u):
            return stage[:, UNITS.index(u) % 2, :]

        def expert_pieces(b):
            gr_ = gu_raw[:].rearrange("p k (d s) -> p k s d", s=2)
            return [(guw[0][:, b, k], guw[1][:, b, k], gr_[:, k]) for k in range(KC)] + \
                   [(dnw[0][:, b], dnw[1][:, b], dn_raw[:])]

        qkv_pieces = [(qkvw[0][:, n], qkvw[1][:, n], qkv_raw[:, n]) for n in range(3)]
        wo_piece = (wow[0][:], wow[1][:], wo_raw[:])

        @block.sync
        def _(sp):
            for q in range(2):
                sp.dma_start(acc[:, 4 * q:4 * q + 4, :], x.rearrange("(t p) h -> p t h", p=P)[:, 4 * q:4 * q + 4, :])\
                    .then_inc(x_in[q], 16)
            sp.dma_start(rw_raw[:], rw).then_inc(small_in, 16)
            sp.dma_start(gub_raw[:], gub).then_inc(small_in, 16)
            sp.dma_start(dnb_sb[:], dnb).then_inc(small_in, 16)
            sp.dma_start(rb_bc[:], rb.rearrange("(a e) -> a e", a=1).broadcast_to([P, EXPERTS])).then_inc(small_in, 16)
            sp.wait_ge(bias_added, 2)
            with sp.Fori(0, PAIRS) as i:
                sp.wait_ge(stage_read_dve, read_dve(i - 1, "v3"))
                for n in range(2):
                    sp.dma_start(vb[n][0:WIN - P, :, :].bitcast(F32), vp[n][0:WIN - P, 1:VT, :].bitcast(F32))\
                        .then_inc(vb_ready, 16)
                    sp.dma_start(vb[n][WIN - P:KB, :, :].bitcast(F32),
                                 vp[n][HALF:HALF + GLOBALS, 0:1, :].bitcast(F32).broadcast_to([GLOBALS, NT, 2 * HD]))\
                        .then_inc(vb_ready, 16)
            sp.wait_ge(w_lo, after(PAIRS - 2, NW, 7))
            for n, w in enumerate((l1["Wk"], l1["Wv"], l1["Wr"])):
                sp.dma_start(kvr_raw[:, n, :, :], w.rearrange("(c p) d -> p c d", p=P)).then_inc(l1_early, 16)
            sp.dma_start(gw_raw[:], l1["gate_w"]).then_inc(l1_early, 16)
            sp.dma_start(td[:], l1["time_decay"].rearrange("(c p) -> p c", p=P),
                         allow_slow_non_contiguous=True).then_inc(l1_early, 16)
            sp.wait_ge(stage_read_dve, read_dve(PAIRS - 1, "wo1"))
            for n, w in enumerate((l1["sw_gate"], l1["sw_up"])):
                sp.dma_start(sgu_raw[:, n, :, :], w.rearrange("(k p) n -> p k n", p=P)).then_inc(l1_loaded, 16)
            sp.dma_start(sd_raw[:, 0:2, :], l1["sw_down"][0:2 * P, :].rearrange("(c p) n -> p c n", p=P))\
                .then_inc(l1_loaded, 16)
            sp.dma_start(sd_raw[0:SD - 2 * P, 2, :], l1["sw_down"][2 * P:SD, :]).then_inc(l1_loaded, 16)

            def load(e, b):
                for n, w in enumerate((l1["w_gate"], l1["w_up"])):
                    sp.dma_start(eg_raw[:, b, :, n, :], w[e].rearrange("(k p) n -> p k n", p=P)).then_inc(ew_loaded[b], 16)
                sp.dma_start(ed_raw[:, b, :, :], l1["w_down"][e].rearrange("(c p) n -> p c n", p=IC)).then_inc(ew_loaded[b], 16)

            with sp.Fori(0, EXPERTS // 2) as i:
                sp.wait_ge(ew_lo, i * 2 + 1)
                load(i * 2, 0)
                load(i * 2 + 1, 1)
            for q in range(4):
                sp.wait_ge(out_ready, q + 1)
                sp.dma_start(out.rearrange("(t p) h -> p t h", p=P)[:, 2 * q:2 * q + 2, :], acc[:, 2 * q:2 * q + 2, :])\
                    .then_inc(out_stored, 16)
            sp.wait_ge(out_stored, 64)

        @block.gpsimd
        def _(pool):
            seq = 0

            def step(ins):
                nonlocal seq
                ins.then_inc(pool_seq, 1)
                seq += 1
                pool.wait_ge(pool_seq, seq)

            step(nc.gpsimd.memset(ident[:], 0.0))
            step(nc.gpsimd.affine_select(out=ident[:], in_=ident[:], compare_op=ALU.not_equal, fill=1.0,
                                         base=0, pattern=[[-1, P]], channel_multiplier=1))
            nc.gpsimd.iota(iota16[:], pattern=[[1, EXPERTS]], base=0, channel_multiplier=0,
                           allow_small_or_imprecise_dtypes=True).then_inc(consts, 1)
            def load_expert(e):
                pool.dma_start(gu_raw[:], gup[e].rearrange("(k p) n -> p k n", p=P)).then_inc(ex_loaded, 16)
                pool.dma_start(dn_raw[:], dnp[e].rearrange("(c p) n -> p c n", p=P)).then_inc(ex_loaded, 16)

            def load_qkv(g):
                for n, w in enumerate((wq, wk, wv)):
                    pool.dma_start(qkv_raw[:, n, :, :], w.rearrange("(k p) (g n) -> g p k n", p=P, n=2 * HD)[g])\
                        .then_inc(qkv_loaded, 16)

            def load_wo(g):
                pool.dma_start(wo_raw[:], wo.rearrange("(g j d) n -> g d j n", j=2, d=HD)[g]).then_inc(wo_loaded, 16)

            load_qkv(0)
            step(nc.gpsimd.memset(og_sum[:], 0.0))
            for n in range(2):
                step(nc.gpsimd.affine_select(out=og_sum[:], in_=og_sum[:], compare_op=ALU.not_equal, fill=1.0,
                                             base=-GR * n, pattern=[[-HALF, 2], [-1, GLOBALS]],
                                             channel_multiplier=1))
            step(nc.gpsimd.memset(mask[:], 0.0))
            for m in range(3):
                win = mask[:, m, 0:WIN]
                step(nc.gpsimd.affine_select(out=win, in_=win, compare_op=ALU.is_ge, fill=OUTSIDE,
                                             base=-1, pattern=[[1, WIN]], channel_multiplier=-1))
                step(nc.gpsimd.affine_select(out=win, in_=win, compare_op=ALU.is_ge, fill=OUTSIDE,
                                             base=WINDOW - 1, pattern=[[-1, WIN]], channel_multiplier=1))
            win = mask[:, 0, 0:WIN]
            step(nc.gpsimd.affine_select(out=win, in_=win, compare_op=ALU.is_ge, fill=OUTSIDE,
                                         base=-HALF - GLOBALS, pattern=[[1, WIN]], channel_multiplier=0))
            win = mask[:, 2, 0:WIN]
            nc.gpsimd.affine_select(out=win, in_=win, compare_op=ALU.is_ge, fill=OUTSIDE,
                                    base=P + HALF - 1, pattern=[[-1, WIN]], channel_multiplier=0).then_inc(consts, 1)

            def lows(i, n0, pieces):
                for n, piece in enumerate(pieces):
                    pool.wait_ge(w_hi, after(i, NW, n0 + n + 1))
                    nc.gpsimd.tensor_tensor(piece[1], piece[2], piece[0].bitcast(F32), ALU.subtract).then_inc(w_lo, 1)
                pool.wait_ge(w_lo, after(i, NW, n0 + len(pieces)))

            for s_, per in ((w_lo, 4), (h0_lo, 2)):
                pool.sem_inc(s_, per)
            load_expert(0)
            load_wo(0)
            lows(-1, 4, qkv_pieces)
            load_qkv(1)
            lows(-1, 7, expert_pieces(0))
            load_expert(1)

            def hidden_lo(i, j):
                pool.wait_ge(h_hi, after(i, 6, 3 * j + 1))
                nc.gpsimd.tensor_tensor(hh[1][:, 0], ff[:, 2], hh[0][:, 0].bitcast(F32), ALU.subtract)\
                    .then_inc(h0_lo, 1)

            def body(i, left):
                lows(i, 0, expert_pieces(1))
                if left:
                    load_expert(i * 2 + 2)
                hidden_lo(i, 0)
                lows(i, 3, [wo_piece])
                if left:
                    load_wo(i + 1)
                    lows(i, 4, qkv_pieces)
                hidden_lo(i, 1)
                if left > 1:
                    load_qkv(i + 2)
                if left:
                    lows(i, 7, expert_pieces(0))
                    load_expert(i * 2 + 3)

            with pool.Fori(0, PAIRS - 2) as i:
                body(i, 2)
            body(PAIRS - 2, 1)
            body(PAIRS - 1, 0)

            pool.wait_ge(stage_read_dve, read_dve(PAIRS - 1, "wo1"))
            step(nc.gpsimd.memset(before[:], 1.0))
            step(nc.gpsimd.affine_select(out=before[:], in_=before[:], compare_op=ALU.is_gt, fill=0.0,
                                         base=0, pattern=[[1, P]], channel_multiplier=-1))
            nc.gpsimd.memset(ones_b[:], 1.0)
            nc.gpsimd.iota(iota_c[:], pattern=[[1, P]], base=0, channel_multiplier=0,
                           allow_small_or_imprecise_dtypes=True)
            nc.gpsimd.iota(iota_p[:], pattern=[[1, 1]], base=0, channel_multiplier=1,
                           allow_small_or_imprecise_dtypes=True)
            nc.gpsimd.memset(slotT[:], 0.0)
            step(nc.gpsimd.memset(sel[:], 0.0))
            nc.gpsimd.affine_select(out=sel[:], in_=sel[:], compare_op=ALU.not_equal, fill=1.0, base=0,
                                    pattern=[[-1, EXPERTS], [0, P]], channel_multiplier=1).then_inc(l1_consts, 1)
            pool.sem_inc(ew_lo, 1)

            def weights_lo(i, b):
                pool.wait_ge(ew_hi, after(i, 2, b + 1))
                nc.gpsimd.tensor_tensor(egw[1][:, b], eg_raw[:, b], egw[0][:, b].bitcast(F32), ALU.subtract)
                nc.gpsimd.tensor_tensor(edw[1][:, b], ed_raw[:, b], edw[0][:, b].bitcast(F32), ALU.subtract)\
                    .then_inc(ew_lo, 1)

            with pool.Fori(0, EXPERTS // 2) as i:
                weights_lo(i, 0)
                weights_lo(i, 1)

        @block.scalar
        def _(act):
            for s_, per in ((qkv_hi, 8 - NEXT), (exp_done, NS), (stage_read_act, NA), (pt_hi, NP), (tanh_done, 4),
                            (h_hi, 6), (out_hi, 3), (w_hi, 4)):
                act.sem_inc(s_, per)
            act.wait_ge(sqrt_done, 1)
            nc.scalar.activation(sd[:, 1], sd[:, 0], ACT.Sqrt).then_inc(sqrt_done, 1)

            for k in range(KC):
                act.wait_ge(xnT_full, k + 1)
                nc.scalar.activation(xT[0][:, k, HALF:HALF + T], stage[:, k, :], ACT.Copy).then_inc(xT_hi, 1)
            act.wait_ge(small_T, 1)
            nc.scalar.activation(rwT[0][:], ps_s[:, 0:KC * EXPERTS].rearrange("p (k e) -> p k e", k=KC),
                                 ACT.Copy).then_inc(small_hi, 1)

            def split_hi(i, n, piece):
                nc.scalar.activation(piece[0], piece[2], ACT.Copy).then_inc(w_hi, 1)

            def even_expert(i, n):
                if n == 0:
                    act.wait_ge(ex_loaded, i * 64 + 96)
                    act.wait_ge(stage_full, full(i, "down10"))
                split_hi(i, n, expert_pieces(0)[n])

            def next_qkv(i, n):
                if n == 0:
                    act.wait_ge(qkv_loaded, i * 48 + 96)
                    act.wait_ge(stage_full, full(i, "k1"))
                split_hi(i, n, qkv_pieces[n])

            def q_hi(i, j):
                act.wait_ge(stage_full, full(i, f"q{j}"))
                act.wait_ge(scores_full, after(i, NS, NT * (2 - j)))
                nc.scalar.activation(qT[0][:, HALF:HALF + T], stage_of(f"q{j}"), ACT.Copy, scale=-SCALE)\
                    .then_inc(qkv_hi, 1)

            def k_hi(i, j):
                act.wait_ge(stage_full, full(i, f"k{j}"))
                for dst, src in k_windows(kw[0], stage_of(f"k{j}")):
                    ins = nc.scalar.activation(dst, src, ACT.Copy)
                ins.then_inc(qkv_hi, 1)

            def v_hi(i, v):
                a, b = V_TILES[v]
                act.wait_ge(stage_full, full(i, f"v{v}"))
                if v == 0:
                    act.wait_ge(pv_done, after(i, NP, NP))
                src = stage_of(f"v{v}")[:, 0:(b - a) * 2 * HD].rearrange("p (t n) -> p t n", n=2 * HD)
                nc.scalar.activation(vp[0][:, a:b, :], src, ACT.Copy).then_inc(qkv_hi, 1)

            for n in range(3):
                next_qkv(-1, n)
            act.wait_ge(lgT_full, 1)
            nc.scalar.activation(scT, ps_o[0:EXPERTS, :], ACT.Copy).then_inc(lgT_copied, 1)
            for n in range(3):
                even_expert(-1, n)
            act.wait_ge(top_sub, 1)
            nc.scalar.activation(topw[:], topw[:], ACT.Exp).then_inc(top_exp, 1)
            act.wait_ge(zeroed, 1)
            q_hi(-1, 0)
            k_hi(-1, 0)
            act.wait_ge(scT_full, 1)
            nc.scalar.activation(scT, ps_o[0:EXPERTS, :], ACT.Copy).then_inc(scT_ready, 1)
            for v in range(4):
                v_hi(-1, v)

            def body(i, more):
                def up_bias(c, j):
                    return ebias[:, 1, c, bass.ds(i * 2 + j, 1)]

                def exps(j, s):
                    n = NT * j + s
                    act.wait_ge(smax_done, after(i, NS, n + 1))
                    act.wait_ge(pt_full, after(i, NP, n - 1))
                    nc.scalar.activation(pr[:, n % 2, 0:KW], sm[:, n % 2, :], ACT.Exp, bias=nm[:, n % 2:n % 2 + 1],
                                         scale=-1.0, accum_out=rs[:, n % 2:n % 2 + 1]).then_inc(exp_done, 1)

                def global_exps(j):
                    rows = slice(HALF * j, HALF * j + GLOBALS)
                    act.wait_ge(gmin_done, after(i, 2, j + 1))
                    act.wait_ge(pt_full, after(i, NP, 0))
                    nc.scalar.activation(pg[rows, HALF:HALF + T], stage_of(f"sg{j}")[rows, :], ACT.Exp,
                                         bias=gm[rows, 0:1], scale=-1.0, accum_out=gs[rows, 0:1])\
                        .then_inc(stage_read_act, 1)

                def tanh(j, c):
                    act.wait_ge(stage_read_dve, read_dve(i, f"gate{c}{j}"))
                    act.wait_ge(h_ready, after(i, 8, 4 * j + 2 * c))
                    nc.scalar.activation(ff[:, 1], ff[:, 0], ACT.Tanh, scale=ALPHA / 2).then_inc(tanh_done, 1)

                def up(j, c):
                    act.wait_ge(stage_full, full(i, f"up{c}{j}"))
                    act.wait_ge(*((h0_lo, after(i, 2, j + 1)) if c else (h1_lo, after(i, 4, 2 * j))))
                    nc.scalar.activation(ff[:, 2], stage_of(f"up{c}{j}"), ACT.Identity,
                                         bias=up_bias(c, j), scale=0.5).then_inc(stage_read_act, 1)

                def hidden_hi(j, c):
                    for h in range(1 + c):
                        act.wait_ge(h_ready, after(i, 8, 4 * j + 2 * c + (h + 1 if c else 2)))
                        if c == 0:
                            act.wait_ge(stage_full, full(i - 1, "down11") if j == 0 else full(i, "down10"))
                        cols = half(h) if c else slice(0, T)
                        nc.scalar.activation(hh[0][:, c, cols], ff[:, 2, cols], ACT.Copy).then_inc(h_hi, 1)

                def probs_hi(n):
                    act.wait_ge(pt_full, after(i, NP, n + 1))
                    act.wait_ge(pv_done, after(i, NP, n - 1))
                    nc.scalar.activation(pT[0][:, n % 2, :], ps_t[:, 0:2 * P], ACT.Copy).then_inc(pt_hi, 1)

                def head(j):
                    for s in range(NT):
                        if s == 1:
                            global_exps(j)
                        exps(j, s)
                        if s == 3:
                            tanh(j, 0)
                        if s == 4:
                            up(j, 0)
                        if s == 6:
                            hidden_hi(j, 0)
                        if s:
                            probs_hi(NT * j + s - 1)
                        if s == 6:
                            tanh(j, 1)
                        if s == 7:
                            up(j, 1)
                        if j == 0:
                            if s < 3:
                                if s == 0:
                                    act.wait_ge(ex_loaded, i * 64 + 64)
                                    act.wait_ge(stage_full, full(i - 1, "down11"))
                                split_hi(i, s, expert_pieces(1)[s])
                            if s == 5:
                                act.wait_ge(wo_loaded, i * 16 + 16)
                                act.wait_ge(stage_full, after(i, NU, 0))
                                split_hi(i, 3, wo_piece)
                        elif more:
                            if s < 3:
                                next_qkv(i, s)
                            elif s in (4, 5, 7):
                                even_expert(i, {4: 0, 5: 1, 7: 2}[s])
                    probs_hi(NT * j + NT - 1)
                    if j == 0 or more:
                        q_hi(i, 1 - j)
                    if j == 1:
                        act.wait_ge(pt_full, after(i, NP, NP))
                        nc.scalar.activation(pgT[:, :, 0, :], ps_t[:, 0:VT * GR].rearrange("p (t g) -> p t g", t=VT),
                                             ACT.Copy).then_inc(pt_hi, 1)
                    hidden_hi(j, 1)
                    if j == 0 or more:
                        k_hi(i, 1 - j)
                    act.wait_ge(pv_done, after(i, NP, NT * (j + 1)))
                    if j == 0:
                        act.wait_ge(stage_full, after(i, NU, 0))
                    nc.scalar.activation(oT[0][:, j, GLOBALS:T], ps_o[:, GLOBALS:T], ACT.Copy).then_inc(out_hi, 1)

                def global_outputs():
                    act.wait_ge(pv_done, after(i, NP, NP))
                    nc.scalar.activation(og[:], ps_s[0:2 * GR, 0:2 * HD], ACT.Copy).then_inc(og_copied, 1)
                    if more:
                        v_hi(i, 0)
                    act.wait_ge(gcols_full, i + 1)
                    nc.scalar.activation(oT[0][:, :, 0:GLOBALS],
                                         ps_t[:, 0:2 * GLOBALS].rearrange("p (j c) -> p j c", j=2), ACT.Copy)\
                        .then_inc(out_hi, 1)
                    if more:
                        for v in range(1, 4):
                            v_hi(i, v)

                head(0)
                head(1)
                global_outputs()

            with act.Fori(0, PAIRS - 1) as i:
                body(i, True)
            body(PAIRS - 1, False)

            for s_ in (tanh2_done, mt_hi, eo_hi, ew_hi):
                act.sem_inc(s_, 2)

            def ring_hi_of(u, dst, src):
                act.wait_ge(ring_full, RNAMES.index(u) + 1)
                nc.scalar.activation(dst, src, ACT.Copy).then_inc(ring_hi, 1)

            nc.scalar.activation(warm[:], ident[:, 0:1], ACT.Sqrt)
            act.wait_ge(sqrt_done, 3)
            nc.scalar.activation(sd[:, 1], sd[:, 0], ACT.Sqrt).then_inc(sqrt_done, 1)
            for n, u in enumerate(("wkT", "wvT", "wrT")):
                ring_hi_of(u, kvrT[0][:, n], ring_of(u).rearrange("p (k e) -> p k e", k=KC))
            ring_hi_of("gwT", gwT[0][:], ring_of("gwT")[:, 0:KC * EXPERTS].rearrange("p (k e) -> p k e", k=KC))
            act.wait_ge(l1_early, 5 * 16)
            nc.scalar.activation(decay[:], td[:], ACT.Exp).then_inc(decay_exp, 1)
            act.wait_ge(decay_exp, 1)
            nc.scalar.activation(decay[:], decay[:], ACT.Exp, scale=-1.0).then_inc(decay_ready, 1)
            for h in range(2):
                for k in range(KC):
                    u = f"xT{k}{h}"
                    ring_hi_of(u, x2T[0][:, k, 1 + h * 512:1 + (h + 1) * 512], ring_of(u))
            for h in range(2):
                nc.scalar.activation(xr[0][:, 4 * h:4 * h + 4, 0:H], xn2[:, 4 * h:4 * h + 4, :], ACT.Copy)\
                    .then_inc(rows_hi, 1)
            for h in range(2):
                act.wait_ge(ring_full, RNAMES.index(f"lgT{h}") + 1)
                nc.scalar.activation(lgT2[:, h * 512:(h + 1) * 512], ring_of(f"lgT{h}")[0:EXPERTS, :], ACT.Copy)\
                    .then_inc(ring_act, 1)
            act.wait_ge(l1_loaded, 4 * 16)
            for g in range(2):
                nc.scalar.activation(sgu[0][:, g], sgu_raw[:, g], ACT.Copy).then_inc(l1_w_hi, 1)
            for c in range(KC):
                for u, func, dst in (("k", ACT.Exp, ek), ("v", ACT.Copy, av), ("r", ACT.Copy, rT)):
                    for h in range(2):
                        act.wait_ge(ring_full, RNAMES.index(f"{u}{c}{h}") + 1)
                        if u == "k" and c == 0 and h == 0:
                            act.wait_ge(rows_lo, 2)
                        nc.scalar.activation(dst[:, c, h * 512:(h + 1) * 512], ring_of(f"{u}{c}{h}"), func)\
                            .then_inc(ring_act, 1)
                    if u == "k" and c == 0:
                        act.wait_ge(l1_sub, 1)
                        nc.scalar.activation(topw[:], topw[:], ACT.Exp)
                        nc.scalar.activation(alls[:], alls[:], ACT.Exp).then_inc(l1_exp, 1)
            nc.scalar.activation(sdw[0][:, 0:2], sd_raw[:, 0:2], ACT.Copy)
            nc.scalar.activation(sdw[0][0:SD - 2 * P, 2], sd_raw[0:SD - 2 * P, 2], ACT.Copy).then_inc(l1_w_hi, 1)

            def expert_hi(i, b):
                act.wait_ge(ew_loaded[b], i * 48 + 48)
                act.wait_ge(f2_full, after(i, 2, b - 1))
                nc.scalar.activation(egw[0][:, b], eg_raw[:, b], ACT.Copy)
                nc.scalar.activation(edw[0][:, b], ed_raw[:, b], ACT.Copy).then_inc(ew_hi, 1)

            for n in range(7):
                c, h = n // 2, n % 2
                if n < 6:
                    w = S_CHUNKS[c][1] - S_CHUNKS[c][0]
                    act.wait_ge(ring_full, RNAMES.index(f"sg{c}{h}") + 1)
                    if n >= 2:
                        act.wait_ge(sT_lo, n - 1)
                    nc.scalar.activation(st[0:w, n % 2], ring_of(f"sg{c}{h}")[0:w, :], ACT.Tanh, scale=0.5)\
                        .then_inc(st_tanh, 1)
                if n >= 1:
                    c, h = (n - 1) // 2, (n - 1) % 2
                    w = S_CHUNKS[c][1] - S_CHUNKS[c][0]
                    act.wait_ge(smid_done, n)
                    nc.scalar.activation(sT[0][0:w, c, h * 512:(h + 1) * 512], st[0:w, (n - 1) % 2], ACT.Copy)\
                        .then_inc(sT_hi, 1)
                if n == 1:
                    expert_hi(0, 0)

            def rows_copy(count):
                act.wait_ge(g_full, count)
                nc.scalar.activation(xg[:], ps_g[:, 0:GW], ACT.Copy).then_inc(xg_copied, 1)

            def rows_hi_parts(count):
                act.wait_ge(xt_full, count)
                nc.scalar.activation(xgT[0][:], ps_f[:, 0:H].rearrange("p (k c) -> p k c", k=KC), ACT.Copy)\
                    .then_inc(xgt_hi, 1)

            rows_copy(1)
            rows_hi_parts(1)

            def step2(i, b, last):
                n = b + 1
                act.wait_ge(f1_full, after(i, 2, n))
                act.wait_ge(gs2_done, after(i, 2, b))
                nc.scalar.activation(tt2[:], ps_f[:, 0:ID], ACT.Tanh, scale=0.5).then_inc(tanh2_done, 1)
                if not last:
                    if b == 0:
                        expert_hi(i, 1)
                    else:
                        act.wait_ge(ew_loaded[0], i * 48 + 96)
                        act.wait_ge(f2_full, after(i, 2, 1))
                        nc.scalar.activation(egw[0][:, 0], eg_raw[:, 0], ACT.Copy)
                        nc.scalar.activation(edw[0][:, 0], ed_raw[:, 0], ACT.Copy).then_inc(ew_hi, 1)
                    act.wait_ge(wsc_ready, i * 2 + n)
                    rows_copy(i * 2 + (n + 1))
                act.wait_ge(mt_full, after(i, 2, n))
                act.wait_ge(f2_full, after(i, 2, b))
                nc.scalar.activation(midT[0][:], ps_x[0:IC, 0:2 * CAP].rearrange("p (c t) -> p c t", c=2),
                                     ACT.Copy).then_inc(mt_hi, 1)
                if not last:
                    rows_hi_parts(i * 2 + (n + 1))
                act.wait_ge(f2_full, after(i, 2, n))
                act.wait_ge(sc_done, after(i, 2, n))
                nc.scalar.activation(eo[0][:], ps_g[:, 0:H], ACT.Copy).then_inc(eo_hi, 1)

            step2(0, 0, False)
            step2(0, 1, False)
            with act.Fori(1, EXPERTS // 2 - 1) as i:
                step2(i, 0, False)
                step2(i, 1, False)
            step2(EXPERTS // 2 - 1, 0, False)
            step2(EXPERTS // 2 - 1, 1, True)

        @block.tensor
        def _(pe):
            for s_, per in ((stage_full, NU - NEXT - LATE), (scores_full, NS), (pt_full, NP), (pv_done, NP)):
                pe.sem_inc(s_, per)

            def three(out_, a, b, start, stop):
                nc.tensor.matmul(out_, a[0], b[0], start=start, stop=False, skip_group_check=True)
                nc.tensor.matmul(out_, a[0], b[1], start=False, stop=False, skip_group_check=True)
                return nc.tensor.matmul(out_, a[1], b[0], start=False, stop=stop, skip_group_check=True)

            pe.wait_ge(consts, 1)
            for k in range(KC):
                for t in range(NT):
                    if k == 0:
                        pe.wait_ge(xn_ready, t + 1)
                    ins = nc.tensor.transpose(stage[:, k, t * P:(t + 1) * P], xn[:, t, k * P:(k + 1) * P], ident[:])
                ins.then_inc(xnT_full, 1)
            pe.wait_ge(small_in, 64)
            for k in range(KC):
                nc.tensor.transpose(ps_s[:, k * EXPERTS:(k + 1) * EXPERTS], rw_raw[:, k * P:(k + 1) * P],
                                    ident[0:EXPERTS, 0:EXPERTS])
            bias_src = gub_raw[:].rearrange("e (c d s) -> e s c d", s=2, d=P)
            for s in range(2):
                for c in range(2):
                    col = KC * EXPERTS + (2 * s + c) * EXPERTS
                    ins = nc.tensor.transpose(ps_s[:, col:col + EXPERTS], bias_src[:, s, c, :],
                                              ident[0:EXPERTS, 0:EXPERTS])
            ins.then_inc(small_T, 1)
            pe.wait_ge(xT_lo, KC)
            pe.wait_ge(rwT_ready, 1)
            for h in range(2):
                for k in range(KC):
                    ins = three(ps_o[0:EXPERTS, h * 512:(h + 1) * 512], [rwT[n][:, k, :] for n in range(2)],
                                [xT[n][:, k, HALF + h * 512:HALF + (h + 1) * 512] for n in range(2)],
                                k == 0, k == KC - 1)
            ins.then_inc(lgT_full, 1)
            pe.wait_ge(lgT_copied, 1)
            for t in range(NT):
                ins = nc.tensor.transpose(ps_t[:, t * EXPERTS:(t + 1) * EXPERTS], scT[:, t * P:(t + 1) * P],
                                          ident[0:EXPERTS, 0:EXPERTS])
            ins.then_inc(logits_full, 1)

            def stage_free(i, u):
                n = UNITS.index(u) - 2
                last, i_ = UNITS[n], (i if n >= 0 else i - 1)
                pe.wait_ge(*((stage_read_act, read_act(i_, last)) if last in BY_ACT
                             else (stage_read_dve, read_dve(i_, last))))

            def project(i, u, parts, n_half=(0, 1), absent=0):
                o = stage_of(u)
                if 0 in n_half:
                    stage_free(i, u)
                for h in n_half:
                    for k in range(KC):
                        b = [xT[n][:, k, HALF + h * 512:HALF + (h + 1) * 512] for n in range(2)]
                        ins = three(o[:, h * 512:(h + 1) * 512], parts(k), b, k == 0, k == KC - 1)
                if 1 in n_half:
                    ins.then_inc(stage_full, 1 + absent)

            def project_qk(i, n, j, n_half=(0, 1)):
                project(i, f"{'qk'[n]}{j}", lambda k: [qkvw[m][:, n, k, j * HD:(j + 1) * HD] for m in range(2)],
                        n_half)

            def project_v(i, v):
                a, b = V_TILES[v]
                u = f"v{v}"
                stage_free(i, u)
                for t in range(a, b):
                    o = stage_of(u)[:, (t - a) * 2 * HD:(t - a + 1) * 2 * HD]
                    for k in range(KC):
                        ins = three(o, [xT[n][:, k, t * P:(t + 1) * P] for n in range(2)],
                                    [qkvw[n][:, 2, k, :] for n in range(2)], k == 0, k == KC - 1)
                ins.then_inc(stage_full, 1 + LATE if v == 3 and isinstance(i, int) else 1)

            pe.wait_ge(w_lo, after(-1, NW, 7))
            for n in range(2):
                project_qk(-1, n, 0)
            pe.wait_ge(scores_ready, 1)
            for t in range(NT):
                ins = nc.tensor.transpose(ps_o[0:EXPERTS, t * P:(t + 1) * P], scores[:, :, t], ident[:])
            ins.then_inc(scT_full, 1)
            for v in range(4):
                project_v(-1, v)
                if v < 2:
                    pe.wait_ge(scT_ready, 1)
                    for t in range(4 * v, 4 * v + 4):
                        ins = nc.tensor.matmul(ring[t // 2][:, (t % 2) * H:(t % 2 + 1) * H],
                                               scT[:, t * P:(t + 1) * P], dnb_sb[:], start=True, stop=True)
                    ins.then_inc(bias_full, 1)
            pe.wait_ge(bias_added, 1)

            def body(i, more):
                def scores_of(j, s):
                    n = NT * j + s
                    pe.wait_ge(smax_done, after(i, NS, n))
                    three(ps_s[:, 0:KW], [qT[m][:, HALF + s * P:HALF + (s + 1) * P] for m in range(2)],
                          [kw[m][:, s, :] for m in range(2)], True, True).then_inc(scores_full, 1)

                def global_scores(j):
                    u = f"sg{j}"
                    stage_free(i, u)
                    for h in range(2):
                        ins = three(stage_of(u)[:, h * 512:(h + 1) * 512],
                                    [qT[n][:, HALF * (1 - j):HALF * (1 - j) + P] for n in range(2)],
                                    [kw[n][:, 4 * h:4 * h + 4, HALF:HALF + P] for n in range(2)], True, True)
                    ins.then_inc(stage_full, 1)

                def expert_piece(j, s):
                    u = ("gate0", "up0", "gate1", "up1")[s // 2]
                    g, c = (0 if u[0] == "g" else 1), int(u[-1])
                    if s == 0:
                        pe.wait_ge(w_lo, after(i, NW, 0 if j == 0 else 3))
                    project(i, f"{u}{j}", lambda k: [guw[n][:, j, k, g, c * P:(c + 1) * P] for n in range(2)],
                            (s % 2,), NEXT if j == 1 and s == NT - 1 and not more else 0)

                def down(j, q):
                    pe.wait_ge(h0_lo, after(i, 2, j + 1))
                    pe.wait_ge(h1_lo, after(i, 4, 2 * j + q + 1))
                    u = f"down{q}{j}"
                    stage_free(i, u)
                    for t in range(4):
                        tt = 4 * q + t
                        for c in range(2):
                            ins = three(stage_of(u)[:, t * H:(t + 1) * H],
                                        [hh[n][:, c, tt * P:(tt + 1) * P] for n in range(2)],
                                        [dnw[n][:, j, c, :] for n in range(2)], c == 0, c == 1)
                    ins.then_inc(stage_full, 1)

                def transposed(n):
                    pe.wait_ge(p_norm, after(i, NS, n + 1))
                    pe.wait_ge(pt_lo, after(i, NP, n))
                    for b in range(2):
                        ins = nc.tensor.transpose(ps_t[:, b * P:(b + 1) * P], pr[:, n % 2, b * P:(b + 1) * P],
                                                  ident[:])
                    ins.then_inc(pt_full, 1)

                def weighted_values(j, t):
                    n = NT * j + t
                    hs = slice(j * HD, (j + 1) * HD)
                    pe.wait_ge(pt_lo, after(i, NP, n + 1))
                    if t == 0:
                        pe.wait_ge(out_lo, after(i, 3, j))
                        if j == 0:
                            pe.wait_ge(vb_ready, i * 64 + 64)
                    o = ps_o[:, t * P:(t + 1) * P]
                    three(o, [vp[m][:, t, hs] for m in range(2)], [pT[m][:, n % 2, 0:P] for m in range(2)],
                          True, False)
                    three(o, [vb[m][0:KB, t, hs] for m in range(2)],
                          [pT[m][0:KB, n % 2, P:2 * P] for m in range(2)], False, True).then_inc(pv_done, 1)

                def head(j):
                    pe.wait_ge(stage_read_dve, read_dve(i, "k1") if j else read_dve(i - 1, "k0"))
                    for s in range(NT):
                        scores_of(j, s)
                        if s == 0:
                            if j == 1:
                                down(0, 1)
                            global_scores(j)
                        expert_piece(j, s)
                        if s >= 1:
                            transposed(NT * j + s - 1)
                        if s >= 2:
                            weighted_values(j, s - 2)
                    if j == 1 and more:
                        pe.wait_ge(w_lo, after(i, NW, 7))
                    if j == 0 or more:
                        project_qk(i, 0, 1 - j)
                    transposed(NT * j + NT - 1)
                    weighted_values(j, NT - 2)
                    if j == 0 or more:
                        project_qk(i, 1, 1 - j, (0,))
                    if j == 1:
                        pe.wait_ge(pt_lo, after(i, NP, NS))
                        pe.wait_ge(pg_ready, after(i, 2, 2))
                        pe.sem_inc(held, 1)
                        for t in range(VT):
                            ins = nc.tensor.transpose(ps_t[:, t * GR:(t + 1) * GR], pg[:, t * P:(t + 1) * P],
                                                      ident[0:GR, 0:GR])
                        ins.then_inc(pt_full, 1)
                    if j == 0 or more:
                        project_qk(i, 1, 1 - j, (1,))
                    weighted_values(j, NT - 1)

                def global_values():
                    pe.wait_ge(pt_lo, after(i, NP, NP))
                    for t in range(VT):
                        for n in range(2):
                            ins = nc.tensor.matmul(ps_s[0:2 * GR, 0:2 * HD],
                                                   pgT[:, t].rearrange("p n g -> p (n g)"), vp[n][:, t, :],
                                                   start=t == 0 and n == 0, stop=t == VT - 1 and n == 1,
                                                   skip_group_check=True)
                    ins.then_inc(pv_done, 1)

                def global_columns():
                    pe.wait_ge(og_copied, i + 1)
                    for j in range(2):
                        ins = nc.tensor.matmul(ps_t[:, j * GLOBALS:(j + 1) * GLOBALS], og[:, j * HD:(j + 1) * HD],
                                               og_sum[:, j, :], start=True, stop=True)
                    ins.then_inc(gcols_full, 1)

                head(0)
                down(0, 0)
                head(1)
                global_values()
                if more:
                    project_v(i, 0)
                global_columns()
                if more:
                    for v in range(1, 4):
                        project_v(i, v)
                down(1, 0)
                down(1, 1)
                pe.wait_ge(w_lo, after(i, NW, 4))
                pe.wait_ge(out_lo, after(i, 3, 3))
                for q in range(2):
                    u = f"wo{q}"
                    stage_free(i, u)
                    for t in range(4):
                        tt = 4 * q + t
                        for j in range(2):
                            ins = three(stage_of(u)[:, t * H:(t + 1) * H],
                                        [oT[n][:, j, tt * P:(tt + 1) * P] for n in range(2)],
                                        [wow[n][:, j, :] for n in range(2)], j == 0, j == 1)
                    ins.then_inc(stage_full, 1)

            with pe.Fori(0, PAIRS - 1) as i:
                body(i, True)
            body(PAIRS - 1, False)

            for s_, per in ((sb_full, 4), (f1_full, 2), (mt_full, 2), (f2_full, 2), (sc_done, 2)):
                pe.sem_inc(s_, per)

            def ring_free(u):
                n = RNAMES.index(u) - 4
                if n >= 0:
                    last, reader = RING[n]
                    pe.wait_ge(ring_act if reader == "act" else ring_dve, ring_reads(last, reader))

            pe.wait_ge(stage_read_dve, read_dve(PAIRS - 1, "wo1"))
            pe.wait_ge(l1_early, 5 * 16)
            for n, u in enumerate(("wkT", "wvT", "wrT")):
                for k in range(KC):
                    for c in range(KC):
                        ins = nc.tensor.transpose(ring_of(u)[:, k * H + c * P:k * H + (c + 1) * P],
                                                  kvr_raw[:, n, c, k * P:(k + 1) * P], ident[:])
                ins.then_inc(ring_full, 1)
            for k in range(KC):
                ins = nc.tensor.transpose(ring_of("gwT")[:, k * EXPERTS:(k + 1) * EXPERTS], gw_raw[:, k * P:(k + 1) * P],
                                          ident[0:EXPERTS, 0:EXPERTS])
            ins.then_inc(ring_full, 1)
            for h in range(2):
                for k in range(KC):
                    u = f"xT{k}{h}"
                    ring_free(u)
                    for t in range(4 * h, 4 * h + 4):
                        pe.wait_ge(xn_ready, NT + t + 1)
                        ins = nc.tensor.transpose(ring_of(u)[:, (t % 4) * P:(t % 4 + 1) * P],
                                                  xn2[:, t, k * P:(k + 1) * P], ident[:])
                    ins.then_inc(ring_full, 1)

            def ring_project(u, w, parts, shift, h):
                ring_free(u)
                for k in range(KC):
                    b = [x2T[n][:, k, shift + h * 512:shift + (h + 1) * 512] for n in range(2)]
                    ins = three(ring_of(u)[0:w, :], parts(k), b, k == 0, k == KC - 1)
                ins.then_inc(ring_full, 1)

            def project_kvr(n, c, h):
                ring_project(f"{'kvr'[n]}{c}{h}", P, lambda k: [kvrT[m][:, n, k, c * P:(c + 1) * P] for m in range(2)],
                             1 if n == 2 else 0, h)

            pe.wait_ge(zeros2, 1)
            for h in range(2):
                pe.wait_ge(ring_dve, ring_reads(f"xT1{h}", "dve"))
                ring_project(f"lgT{h}", EXPERTS, lambda k: [gwT[m][:, k, :] for m in range(2)], 1, h)
            for h in range(2):
                project_kvr(0, 0, h)
            ring_free("logits")
            pe.wait_ge(ring_act, ring_reads("lgT1", "act"))
            for t in range(NT):
                ins = nc.tensor.transpose(ring_of("logits")[:, t * EXPERTS:(t + 1) * EXPERTS],
                                          lgT2[:, t * P:(t + 1) * P], ident[0:EXPERTS, 0:EXPERTS])
            ins.then_inc(ring_full, 1)
            for c in range(KC):
                for n in range(3):
                    for h in range(2):
                        if (n, c) != (0, 0):
                            project_kvr(n, c, h)
            ring_free("pos")
            pe.wait_ge(chosen_ready, 1)
            pe.wait_ge(l1_consts, 1)
            pos = ring_of("pos")[:, 0:NT * EXPERTS].rearrange("p (t e) -> p t e", t=NT)
            nc.tensor.matmul(pos, before[:], chosen_b[:], start=True, stop=False, skip_group_check=True)
            for t in range(NT - 1):
                ins = nc.tensor.matmul(pos[:, t + 1:NT, :], ones_b[:],
                                       chosen_b[:, t:t + 1, :].broadcast_to([P, NT - 1 - t, EXPERTS]),
                                       start=False, stop=t == NT - 2, skip_group_check=True)
            ins.then_inc(ring_full, 1)

            def shared(c, h):
                lo, hi = S_CHUNKS[c]
                for g, u in enumerate(("sg", "su")):
                    ring_project(f"{u}{c}{h}", hi - lo, lambda k: [sgu[m][:, g, k, lo:hi] for m in range(2)], 1, h)

            pe.wait_ge(l1_w_lo, 2)
            for c in range(2):
                for h in range(2):
                    shared(c, h)
            pe.wait_ge(slots_ready, 1)
            for h in range(2):
                u = f"slots{h}"
                ring_free(u)
                for t in range(4 * h, 4 * h + 4):
                    ins = nc.tensor.transpose(ring_of(u)[0:EXPERTS, (t % 4) * P:(t % 4 + 1) * P], slot[:, :, t],
                                              ident[:])
                ins.then_inc(ring_full, 1)
            shared(2, 0)
            shared(2, 1)

            def gather(b, half):
                for t in range(4 * half, 4 * half + 4):
                    for n in range(2):
                        ins = nc.tensor.matmul(ps_g[:, 0:GW], pmat[:, b, t, :], xr[n][:, t, :],
                                               start=t == 0 and n == 0, stop=t == NT - 1 and n == 1,
                                               skip_group_check=True)
                return ins

            def scatter(b, tiles, last=False):
                for t in tiles:
                    for n in range(2):
                        ins = nc.tensor.matmul(y[:, t, :], pmT[:, b, t * P:(t + 1) * P], eo[n][:],
                                               start=False, stop=last and t % 2 == 1 and n == 1,
                                               skip_group_check=True)
                return ins

            def recurrence_rows(tiles):
                for t in tiles:
                    pe.wait_ge(rw_ready, 2 * t + 2)
                    for c in range(KC):
                        nc.tensor.matmul(y[:, t, c * P:(c + 1) * P], av[:, c, t * P:(t + 1) * P], ident[:],
                                         start=False, stop=False, skip_group_check=True)

            last_here = [u for n, u in enumerate(RNAMES) if n % 4 == 0][-1]
            pe.wait_ge(ring_dve, ring_reads(last_here, "dve"))
            pe.wait_ge(rows_lo, 3)

            def rows_transposed():
                for k in range(KC):
                    ins = nc.tensor.transpose(ps_f[:, k * P:(k + 1) * P], xg[:, k * P:(k + 1) * P], ident[:])
                return ins

            pe.wait_ge(pm_ready, 1)
            gather(0, 0)
            gather(0, 1).then_inc(g_full, 1)
            pe.wait_ge(sT_lo, 6)
            pe.wait_ge(l1_w_lo, 3)
            for t in range(NT):
                for c, (lo, hi) in enumerate(S_CHUNKS):
                    three(y[:, t, :], [sT[n][0:hi - lo, c, t * P:(t + 1) * P] for n in range(2)],
                          [sdw[n][0:hi - lo, c, :] for n in range(2)], c == 0 and t % 2 == 0, False)

            pe.wait_ge(ring_dve, ring_reads(RNAMES[-1], "dve"))
            pe.wait_ge(xg_copied, 1)
            rows_transposed().then_inc(xt_full, 1)

            def step2(i, b, first, last):
                n = b + 1

                def slots_row(h):
                    pe.wait_ge(pmt_ready, after(i, 4, 2 * b + h))
                    pe.sem_inc(held, 1)
                    nc.tensor.matmul(ps_b, sel[:, bass.ds(i * 2 + b, 1), :].rearrange("p a c -> p (a c)"),
                                     slotT[:, h * 512:(h + 1) * 512], start=True, stop=True).then_inc(sb_full, 1)

                pe.wait_ge(xgt_lo, i * 2 + n)
                pe.wait_ge(ew_lo, i * 2 + (b + 2))
                for k in range(KC):
                    ins = three(ps_f[:, 0:2 * ID], [xgT[m][:, k, :] for m in range(2)],
                                [egw[m][:, b, k].rearrange("p g n -> p (g n)") for m in range(2)], k == 0, k == KC - 1)
                ins.then_inc(f1_full, 1)
                slots_row(0)
                if last:
                    recurrence_rows(range(0, 3))
                pe.wait_ge(eo_lo, after(i, 2, b))
                if not last:
                    pe.wait_ge(pm_ready, i * 2 + (n + 1))
                    gather(1 - b, 0)
                    gather(1 - b, 1).then_inc(g_full, 1)
                if not first:
                    pe.wait_ge(pmt_ready, after(i, 4, 2 * b))
                    scatter(1 - b, range(0, 4))
                pe.wait_ge(mid_ready, after(i, 2, n))
                for c in range(2):
                    ins = nc.tensor.transpose(ps_x[0:IC, c * CAP:(c + 1) * CAP], mid[:, c * IC:(c + 1) * IC], ident[:])
                ins.then_inc(mt_full, 1)
                if not last:
                    pe.wait_ge(xg_copied, i * 2 + (n + 1))
                    rows_transposed().then_inc(xt_full, 1)
                slots_row(1)
                if not first:
                    scatter(1 - b, range(4, 8)).then_inc(sc_done, 1)
                else:
                    pe.sem_inc(sc_done, 1)
                if last:
                    recurrence_rows(range(3, 5))
                pe.wait_ge(mt_lo, after(i, 2, n))
                for c in range(2):
                    ins = three(ps_g[:, 0:H], [midT[m][:, c, :] for m in range(2)],
                                [edw[m][:, b, c, :] for m in range(2)], c == 0, c == 1)
                ins.then_inc(f2_full, 1)

            step2(0, 0, True, False)
            step2(0, 1, False, False)
            with pe.Fori(1, EXPERTS // 2 - 1) as i:
                step2(i, 0, False, False)
                step2(i, 1, False, False)
            step2(EXPERTS // 2 - 1, 0, False, False)
            step2(EXPERTS // 2 - 1, 1, False, True)
            recurrence_rows(range(5, NT))
            pe.wait_ge(eo_lo, after(EXPERTS // 2 - 1, 2, 2))
            pe.wait_ge(pmt_ready, after(EXPERTS // 2 - 1, 4, 4))
            for q in range(4):
                scatter(1, range(2 * q, 2 * q + 2), last=True).then_inc(y_done, 1)

        @block.vector
        def _(dve):
            for s_, per in ((stage_read_dve, ND - NEXT - LATE), (smax_done, NS), (p_norm, NS), (recip_done, NS),
                            (gmin_done, 2), (grecip_done, 2), (pg_ready, 2), (pt_lo, NP), (out_lo, 3), (clip_done, 4),
                            (glu_done, 4), (h_ready, 8), (h1_lo, 4)):
                dve.sem_inc(s_, per)
            seq = 0

            def step(ins):
                nonlocal seq
                ins.then_inc(vseq, 1)
                seq += 1
                dve.wait_ge(vseq, seq)

            V = nc.vector
            for n in range(2):
                for ap in (xT[n][:, :, 0:HALF], xT[n][:, :, HALF + T:TP], kw[n][:, 0, 0:HALF],
                           kw[n][:, NT - 1, WIN - HALF:WIN]):
                    V.memset(ap.bitcast(F32), 0.0)
                V.memset(qT[n][:, 0:HALF].bitcast(F32), 0.0)
            V.memset(pr[:, :, KW:2 * P], 0.0)
            step(V.memset(pg[:], 0.0))
            dve.sem_inc(zeroed, 1)

            def layer_norm(xn, sq):
                step(V.memset(small[:, 0:1], 0.0))
                for t in range(NT):
                    V.bn_aggr(mv[:, t, :], stats[:, t, :])
                step(V.memset(small[:, 0:1], 0.0))
                V.tensor_scalar(sd[:, 0], mv[:, :, 1], EPS, None, ALU.add).then_inc(sqrt_done, 1)
                dve.wait_ge(sqrt_done, sq)
                step(V.reciprocal(sd[:, 2], sd[:, 1]))
                step(V.tensor_tensor(sd[:, 3], sd[:, 0], sd[:, 2], ALU.mult))
                step(V.tensor_tensor(sd[:, 2], sd[:, 3], sd[:, 1], ALU.add))
                step(V.tensor_scalar(sd[:, 3], sd[:, 2], 0.5, None, ALU.mult))
                step(V.reciprocal(sd[:, 2], sd[:, 3]))
                for t in range(NT):
                    V.tensor_scalar(xn[:, t, :], acc[:, t, :], mv[:, t, 0:1], sd[:, 2, t:t + 1],
                                    ALU.subtract, ALU.mult).then_inc(xn_ready, 1)

            for t in range(NT):
                if t % 4 == 0:
                    dve.wait_ge(x_in[t // 4], 16)
                V.bn_stats(stats[:, t, :], acc[:, t, :])
            layer_norm(xn, 2)
            for k in range(KC):
                dve.wait_ge(xT_hi, k + 1)
                V.tensor_tensor(xT[1][:, k, HALF:HALF + T], stage[:, k, :],
                                xT[0][:, k, HALF:HALF + T].bitcast(F32), ALU.subtract).then_inc(xT_lo, 1)
            dve.wait_ge(small_hi, 1)
            V.tensor_tensor(rwT[1][:], ps_s[:, 0:KC * EXPERTS].rearrange("p (k e) -> p k e", k=KC),
                            rwT[0][:].bitcast(F32), ALU.subtract).then_inc(rwT_ready, 1)
            b0 = KC * EXPERTS
            V.tensor_copy(ebias[:, 0], ps_s[:, b0:b0 + 2 * EXPERTS].rearrange("p (c e) -> p c e", c=2))
            step(V.tensor_scalar(ebias[:, 1], ps_s[:, b0 + 2 * EXPERTS:b0 + 4 * EXPERTS].rearrange(
                "p (c e) -> p c e", c=2), 1.0, 0.5, ALU.add, ALU.mult))

            def q_lo(i, j):
                dve.wait_ge(qkv_hi, after(i, 8, 3 - 2 * j))
                V.scalar_tensor_tensor(qT[1][:, HALF:HALF + T], stage_of(f"q{j}"), -SCALE,
                                       qT[0][:, HALF:HALF + T].bitcast(F32), ALU.mult, ALU.subtract)\
                    .then_inc(stage_read_dve, 1)

            def k_lo(i, j):
                dve.wait_ge(qkv_hi, after(i, 8, 4 - 2 * j))
                for (hi, src), (lo, _) in zip(k_windows(kw[0], stage_of(f"k{j}")), k_windows(kw[1], stage_of(f"k{j}"))):
                    ins = V.tensor_tensor(lo, src, hi.bitcast(F32), ALU.subtract)
                ins.then_inc(stage_read_dve, 1)

            def v_lo(i, v):
                a, b = V_TILES[v]
                dve.wait_ge(qkv_hi, after(i, 8, 5 + v))
                src = stage_of(f"v{v}")[:, 0:(b - a) * 2 * HD].rearrange("p (t n) -> p t n", n=2 * HD)
                V.tensor_tensor(vp[1][:, a:b, :], src, vp[0][:, a:b, :].bitcast(F32), ALU.subtract)\
                    .then_inc(stage_read_dve, 1 + LATE if v == 3 and isinstance(i, int) else 1)

            dve.wait_ge(consts, 2)
            dve.wait_ge(logits_full, 1)
            step(V.tensor_tensor(lg[:], ps_t[:, 0:NT * EXPERTS].rearrange("p (t e) -> p t e", t=NT),
                                 rb_bc[:].unsqueeze(1).broadcast_to([P, NT, EXPERTS]), ALU.add))
            for t in range(NT):
                V.max(top8[:, t, :], lg[:, t, :])
            step(V.memset(small[:, 0:1], 0.0))
            for t in range(NT):
                V.max_index(topi[:, t, :], top8[:, t, :], lg[:, t, :])
            V.tensor_tensor(topw[:], top8[:, :, 0:TOPK], top8[:, :, 0:1].broadcast_to([P, NT, TOPK]),
                            ALU.subtract).then_inc(top_sub, 1)
            step(V.memset(small[:, 0:1], 0.0))
            step(V.tensor_copy(topif[:], topi[:, :, 0:TOPK]))
            dve.wait_ge(top_exp, 1)
            step(V.tensor_reduce(rsum[:], topw[:], AX_X, ALU.add))
            step(V.reciprocal(rsum[:], rsum[:]))
            step(V.tensor_tensor(topw[:], topw[:], rsum[:].unsqueeze(2).broadcast_to([P, NT, TOPK]), ALU.mult))
            sc_te = scores[:].rearrange("p e t -> p t e")
            for n in range(TOPK):
                dst = sc_te if n == 0 else onehot[:]
                step(V.tensor_tensor(dst, iota16[:].unsqueeze(1).broadcast_to([P, NT, EXPERTS]),
                                     topif[:, :, n:n + 1].broadcast_to([P, NT, EXPERTS]), ALU.is_equal))
                step(V.tensor_tensor(dst, dst, topw[:, :, n:n + 1].broadcast_to([P, NT, EXPERTS]), ALU.mult))
                if n:
                    step(V.tensor_tensor(sc_te, sc_te, onehot[:], ALU.add))
            V.memset(small[:, 0:1], 0.0).then_inc(scores_ready, 1)
            q_lo(-1, 0)
            k_lo(-1, 0)
            for v in range(4):
                v_lo(-1, v)
                if v in (1, 2):
                    q = v - 1
                    dve.wait_ge(bias_full, q + 1)
                    for n in range(2):
                        t = 4 * q + 2 * n
                        ins = V.tensor_tensor(acc[:, t:t + 2, :], acc[:, t:t + 2, :],
                                              ring[2 * q + n].rearrange("p (t h) -> p t h", h=H), ALU.add)
                    ins.then_inc(bias_added, 1)
            dve.wait_ge(bias_added, 2)

            def body(i, more):
                def smax(j, s):
                    n = NT * j + s
                    dve.wait_ge(scores_full, after(i, NS, n + 1))
                    dve.wait_ge(exp_done, after(i, NS, n - 1))
                    dve.sem_inc(held, 1)
                    V.tensor_tensor_reduce(sm[:, n % 2, :], ps_s[:, 0:KW],
                                           mask[:, 0 if s == 0 else 2 if s == NT - 1 else 1, :],
                                           1.0, 3e38, ALU.add, ALU.min, nm[:, n % 2:n % 2 + 1]).then_inc(smax_done, 1)

                def normalise(n):
                    dve.wait_ge(exp_done, after(i, NS, n + 1))
                    V.reciprocal(rr[:, n % 2:n % 2 + 1], rs[:, n % 2:n % 2 + 1]).then_inc(recip_done, 1)
                    dve.wait_ge(recip_done, after(i, NS, n + 1))
                    V.tensor_scalar(pr[:, n % 2, 0:KW], pr[:, n % 2, 0:KW], rr[:, n % 2:n % 2 + 1], None,
                                    ALU.mult).then_inc(p_norm, 1)

                def probs_lo(n):
                    dve.wait_ge(pt_hi, after(i, NP, n + 1))
                    V.tensor_tensor(pT[1][:, n % 2, :], ps_t[:, 0:2 * P], pT[0][:, n % 2, :].bitcast(F32),
                                    ALU.subtract).then_inc(pt_lo, 1)

                def global_min(j):
                    rows = slice(HALF * j, HALF * j + GLOBALS)
                    dve.wait_ge(stage_full, full(i, f"sg{j}"))
                    V.tensor_reduce(gm[rows, 0:1], stage_of(f"sg{j}")[rows, :], AX_X, ALU.min).then_inc(gmin_done, 1)

                def global_normalise(j):
                    rows = slice(HALF * j, HALF * j + GLOBALS)
                    dve.wait_ge(stage_read_act, read_act(i, f"sg{j}"))
                    V.reciprocal(gr[rows, 0:1], gs[rows, 0:1]).then_inc(grecip_done, 1)
                    dve.wait_ge(grecip_done, after(i, 2, j + 1))
                    V.tensor_scalar(pg[rows, HALF:HALF + T], pg[rows, HALF:HALF + T], gr[rows, 0:1], None,
                                    ALU.mult).then_inc(pg_ready, 1)

                def gate(j, c, halves=(0, 1)):
                    if 0 in halves:
                        dve.wait_ge(stage_full, full(i, f"gate{c}{j}"))
                        dve.sem_inc(held, 1)
                    for h in halves:
                        ins = V.tensor_scalar(ff[:, 0, half(h)], stage_of(f"gate{c}{j}")[:, half(h)],
                                              ebias[:, 0, c, bass.ds(i * 2 + j, 1)], LIMIT, ALU.add, ALU.min)
                    if 1 in halves:
                        ins.then_inc(stage_read_dve, 1 + NEXT if j == 1 and c == 1 and not more else 1)

                def glu(j, c, halves=(0, 1)):
                    if 0 in halves:
                        dve.wait_ge(tanh_done, after(i, 4, 2 * j + c + 1))
                    for h in halves:
                        ins = V.scalar_tensor_tensor(ff[:, 1, half(h)], ff[:, 1, half(h)], 1.0, ff[:, 0, half(h)],
                                                     ALU.add, ALU.mult)
                    if 1 in halves:
                        ins.then_inc(glu_done, 1)

                def clip(j, c):
                    dve.wait_ge(stage_read_act, read_act(i, f"up{c}{j}"))
                    V.tensor_scalar(ff[:, 2], ff[:, 2], (LIMIT + 1) / 2, (1 - LIMIT) / 2, ALU.min, ALU.max)\
                        .then_inc(clip_done, 1)

                def hidden(j, c, h):
                    if h == 0:
                        dve.wait_ge(glu_done, after(i, 4, 2 * j + c + 1))
                        dve.wait_ge(clip_done, after(i, 4, 2 * j + c + 1))
                    V.tensor_tensor(ff[:, 2, half(h)], ff[:, 2, half(h)], ff[:, 1, half(h)], ALU.mult)\
                        .then_inc(h_ready, 1)

                def hidden_lo(j, h):
                    dve.wait_ge(h_hi, after(i, 6, 3 * j + 2 + h))
                    V.tensor_tensor(hh[1][:, 1, half(h)], ff[:, 2, half(h)], hh[0][:, 1, half(h)].bitcast(F32),
                                    ALU.subtract).then_inc(h1_lo, 1)

                def out_lo_of(j):
                    dve.wait_ge(out_hi, after(i, 3, j + 1))
                    V.tensor_tensor(oT[1][:, j, GLOBALS:T], ps_o[:, GLOBALS:T], oT[0][:, j, GLOBALS:T].bitcast(F32),
                                    ALU.subtract).then_inc(out_lo, 1)

                def down(j, q):
                    dve.wait_ge(stage_full, full(i, f"down{q}{j}"))
                    dve.wait_ge(stage_read_dve, after(i, ND, 0) if j == 0 else read_dve(i, "down10"))
                    for t in range(4):
                        tt = 4 * q + t
                        ins = V.scalar_tensor_tensor(acc[:, tt, :], stage_of(f"down{q}{j}")[:, t * H:(t + 1) * H],
                                                     scores[:, bass.ds(i * 2 + j, 1), tt], acc[:, tt, :],
                                                     ALU.mult, ALU.add)
                    ins.then_inc(stage_read_dve, 1)

                def head(j):
                    for s in range(NT):
                        smax(j, s)
                        if s == 0 and j == 1:
                            down(0, 1)
                        if s == 1 and j == 1:
                            out_lo_of(0)
                        if s == 7:
                            global_normalise(j)
                        for h in range(2):
                            if s in (2, 6):
                                gate(j, s // 4, (h,))
                            if s in (3, 7) and h == 1:
                                glu(j, s // 4, (0,))
                            if s == 4 and h == 0:
                                glu(j, 0, (1,))
                            if s == 5:
                                hidden(j, 0, h)
                            if h == 0:
                                normalise(NT * j + s)
                        if s == 0:
                            global_min(j)
                        if s == 4:
                            clip(j, 0)
                        if s:
                            probs_lo(NT * j + s - 1)
                    glu(j, 1, (1,))
                    clip(j, 1)
                    probs_lo(NT * j + NT - 1)
                    for h in range(2):
                        hidden(j, 1, h)
                    if j == 0 or more:
                        q_lo(i, 1 - j)
                    if j == 1:
                        dve.wait_ge(pt_hi, after(i, NP, NP))
                        V.tensor_tensor(pgT[:, :, 1, :], ps_t[:, 0:VT * GR].rearrange("p (t g) -> p t g", t=VT),
                                        pgT[:, :, 0, :].bitcast(F32), ALU.subtract).then_inc(pt_lo, 1)
                    for h in range(2):
                        hidden_lo(j, h)
                    if j == 0 or more:
                        k_lo(i, 1 - j)
                    if j == 1:
                        out_lo_of(1)

                head(0)
                down(0, 0)
                head(1)
                if more:
                    v_lo(i, 0)
                dve.wait_ge(out_hi, after(i, 3, 3))
                V.tensor_tensor(oT[1][:, :, 0:GLOBALS], ps_t[:, 0:2 * GLOBALS].rearrange("p (j c) -> p j c", j=2),
                                oT[0][:, :, 0:GLOBALS].bitcast(F32), ALU.subtract).then_inc(out_lo, 1)
                if more:
                    for v in range(1, 4):
                        v_lo(i, v)
                down(1, 0)
                down(1, 1)
                dve.wait_ge(stage_read_dve, read_dve(i, "down11"))
                for q in range(2):
                    dve.wait_ge(stage_full, full(i, f"wo{q}"))
                    V.tensor_tensor(acc[:, 4 * q:4 * q + 4, :], acc[:, 4 * q:4 * q + 4, :],
                                    stage_of(f"wo{q}").rearrange("p (t h) -> p t h", h=H), ALU.add)\
                        .then_inc(stage_read_dve, 1)
                    if not more:
                        dve.wait_ge(stage_read_dve, read_dve(i, f"wo{q}"))
                        for t in range(4 * q, 4 * q + 4):
                            V.bn_stats(stats[:, t, :], acc[:, t, :])

            with dve.Fori(0, PAIRS - 1) as i:
                body(i, True)
            body(PAIRS - 1, False)

            for s_, per in ((pmt_ready, 4), (gs2_done, 2), (mid_ready, 2), (mt_lo, 2), (eo_lo, 2)):
                dve.sem_inc(s_, per)
            dve.wait_ge(stage_read_dve, read_dve(PAIRS - 1, "wo1"))
            layer_norm(xn2, 4)
            V.memset(x2T[0][:, :, 0:1].bitcast(F32), 0.0)
            V.memset(x2T[1][:, :, 0:1].bitcast(F32), 0.0).then_inc(zeros2, 1)

            def ring_lo(u, dst, src, hi):
                dve.wait_ge(ring_hi, [v for v, r in RING if r == "dve"].index(u) + 1)
                V.tensor_tensor(dst, src, hi.bitcast(F32), ALU.subtract).then_inc(ring_dve, 1)

            for n, u in enumerate(("wkT", "wvT", "wrT")):
                ring_lo(u, kvrT[1][:, n], ring_of(u).rearrange("p (k e) -> p k e", k=KC), kvrT[0][:, n])
            ring_lo("gwT", gwT[1][:], ring_of("gwT")[:, 0:KC * EXPERTS].rearrange("p (k e) -> p k e", k=KC), gwT[0][:])
            for h in range(2):
                for k in range(KC):
                    cols = slice(1 + h * 512, 1 + (h + 1) * 512)
                    ring_lo(f"xT{k}{h}", x2T[1][:, k, cols], ring_of(f"xT{k}{h}"), x2T[0][:, k, cols])

            for h in range(2):
                dve.wait_ge(rows_hi, h + 1)
                V.tensor_tensor(xr[1][:, 4 * h:4 * h + 4, 0:H], xn2[:, 4 * h:4 * h + 4, :],
                                xr[0][:, 4 * h:4 * h + 4, 0:H].bitcast(F32), ALU.subtract).then_inc(rows_lo, 1)
            for g in range(2):
                dve.wait_ge(l1_w_hi, g + 1)
                V.tensor_tensor(sgu[1][:, g], sgu_raw[:, g], sgu[0][:, g].bitcast(F32), ALU.subtract).then_inc(l1_w_lo, 1)
            dve.wait_ge(ring_full, RNAMES.index("logits") + 1)
            V.tensor_copy(lg[:], ring_of("logits")[:, 0:NT * EXPERTS].rearrange("p (t e) -> p t e", t=NT))\
                .then_inc(ring_dve, 1)
            dve.wait_ge(ring_dve, ring_reads("logits", "dve"))
            for t in range(NT):
                V.max(top8[:, t, :], lg[:, t, :])
            step(V.memset(small[:, 0:1], 0.0))
            V.tensor_tensor(topw[:], top8[:, :, 0:TOPK], top8[:, :, 0:1].broadcast_to([P, NT, TOPK]), ALU.subtract)
            V.tensor_tensor(alls[:], lg[:], top8[:, :, 0:1].broadcast_to([P, NT, EXPERTS]),
                            ALU.subtract).then_inc(l1_sub, 1)
            for t in range(NT):
                V.max_index(topi[:, t, :], top8[:, t, :], lg[:, t, :])
            step(V.memset(small[:, 0:1], 0.0))
            step(V.tensor_copy(topif[:], topi[:, :, 0:TOPK]))
            dve.wait_ge(l1_exp, 1)
            step(V.tensor_reduce(rsum[:], alls[:], AX_X, ALU.add))
            step(V.reciprocal(rsum[:], rsum[:]))
            step(V.tensor_tensor(topw[:], topw[:], rsum[:].unsqueeze(2).broadcast_to([P, NT, TOPK]), ALU.mult))
            step(V.tensor_reduce(rsum[:], topw[:], AX_X, ALU.add))
            step(V.tensor_scalar(rsum[:], rsum[:], 1e-20, None, ALU.add))
            step(V.reciprocal(rsum[:], rsum[:]))
            step(V.tensor_tensor(topw[:], topw[:], rsum[:].unsqueeze(2).broadcast_to([P, NT, TOPK]), ALU.mult))
            for n in range(TOPK):
                one, weighted = (chosen, w16) if n == 0 else (onehot, alls)
                step(V.tensor_tensor(one[:], iota16[:].unsqueeze(1).broadcast_to([P, NT, EXPERTS]),
                                     topif[:, :, n:n + 1].broadcast_to([P, NT, EXPERTS]), ALU.is_equal))
                step(V.tensor_tensor(weighted[:], one[:], topw[:, :, n:n + 1].broadcast_to([P, NT, EXPERTS]), ALU.mult))
                if n:
                    V.tensor_tensor(chosen[:], chosen[:], onehot[:], ALU.add)
                    step(V.tensor_tensor(w16[:], w16[:], alls[:], ALU.add))
            V.tensor_copy(chosen_b[:], chosen[:]).then_inc(chosen_ready, 1)
            step(V.tensor_copy(xr[0][:, :, H:GW], w16[:]))
            V.tensor_tensor(xr[1][:, :, H:GW], w16[:], xr[0][:, :, H:GW].bitcast(F32), ALU.subtract)\
                .then_inc(rows_lo, 1)
            def recurrence(c):
                dve.wait_ge(ring_act, ring_reads(f"r{c}1", "act"))
                w = decay[:, c:c + 1].broadcast_to([P, T])
                V.tensor_tensor_scan(den[:, c], w, ek[:, c], 0.0, ALU.mult, ALU.add)
                step(V.tensor_tensor(av[:, c], av[:, c], ek[:, c], ALU.mult))
                step(V.tensor_tensor_scan(ek[:, c], w, av[:, c], 0.0, ALU.mult, ALU.add))
                V.tensor_scalar(den[:, c], den[:, c], 1e-8, None, ALU.add)
                step(V.tensor_tensor(ek[:, c], ek[:, c], rT[:, c], ALU.mult))

            dve.wait_ge(decay_ready, 1)
            recurrence(0)
            dve.wait_ge(ring_full, RNAMES.index("pos") + 1)
            slot_te = slot[:].rearrange("p e t -> p t e")
            V.scalar_tensor_tensor(slot_te, ring_of("pos")[:, 0:NT * EXPERTS].rearrange("p (t e) -> p t e", t=NT),
                                   -NONE, chosen[:], ALU.add, ALU.mult).then_inc(ring_dve, 1)
            dve.wait_ge(ring_dve, ring_reads("pos", "dve"))
            V.tensor_scalar(slot[:], slot[:], NONE, None, ALU.add).then_inc(slots_ready, 1)

            def shared_lo(n):
                c, h = n // 2, n % 2
                w = S_CHUNKS[c][1] - S_CHUNKS[c][0]
                dve.wait_ge(sT_hi, n + 1)
                hi = sT[0][0:w, c, h * 512:(h + 1) * 512]
                V.tensor_tensor(sT[1][0:w, c, h * 512:(h + 1) * 512], st[0:w, n % 2], hi.bitcast(F32), ALU.subtract)\
                    .then_inc(sT_lo, 1)

            def shared_unit(n):
                c, h = n // 2, n % 2
                w = S_CHUNKS[c][1] - S_CHUNKS[c][0]
                dve.wait_ge(st_tanh, n + 1)
                V.scalar_tensor_tensor(st[0:w, n % 2], st[0:w, n % 2], 1.0, ring_of(f"sg{c}{h}")[0:w, :],
                                       ALU.add, ALU.mult).then_inc(ring_dve, 1)
                dve.wait_ge(ring_dve, ring_reads(f"sg{c}{h}", "dve"))
                dve.wait_ge(ring_full, RNAMES.index(f"su{c}{h}") + 1)
                V.scalar_tensor_tensor(st[0:w, n % 2], st[0:w, n % 2], 0.5, ring_of(f"su{c}{h}")[0:w, :],
                                       ALU.mult, ALU.mult).then_inc(ring_dve, 1)
                dve.wait_ge(ring_dve, ring_reads(f"su{c}{h}", "dve"))
                V.memset(small[:, 1:2], 0.0).then_inc(smid_done, 1)

            for n in range(4):
                shared_unit(n)
                if n:
                    shared_lo(n - 1)
            dve.wait_ge(l1_w_hi, 3)
            V.tensor_tensor(sdw[1][:, 0:2], sd_raw[:, 0:2], sdw[0][:, 0:2].bitcast(F32), ALU.subtract)
            V.tensor_tensor(sdw[1][0:SD - 2 * P, 2], sd_raw[0:SD - 2 * P, 2], sdw[0][0:SD - 2 * P, 2].bitcast(F32),
                            ALU.subtract).then_inc(l1_w_lo, 1)
            dve.wait_ge(l1_consts, 1)
            for h in range(2):
                dve.wait_ge(ring_full, RNAMES.index(f"slots{h}") + 1)
                V.tensor_copy(slotT[0:EXPERTS, h * 512:(h + 1) * 512], ring_of(f"slots{h}")[0:EXPERTS, :])\
                    .then_inc(ring_dve, 1)
            shared_lo(3)

            def slot_matrix(e, b):
                row = slot[:, e, :] if isinstance(e, int) else slot[:, bass.ds(e, 1), :].rearrange("p a t -> p (a t)")
                V.tensor_tensor(pmat[:, b], iota_c[:].unsqueeze(1).broadcast_to([P, NT, CAP]),
                                row.unsqueeze(2).broadcast_to([P, NT, CAP]), ALU.is_equal).then_inc(pm_ready, 1)

            dve.wait_ge(slots_ready, 1)
            slot_matrix(0, 0)
            for n in (4, 5):
                shared_unit(n)
                if n == 5:
                    shared_lo(4)
            shared_lo(5)

            recurrence(1)
            slot_matrix(1, 1)

            def slot_weights(col, count):
                dve.wait_ge(xg_copied, count)
                V.tensor_scalar(wsc[:], xg[:, col], 0.5, None, ALU.mult).then_inc(wsc_ready, 1)

            def rows_lo_parts(count):
                dve.wait_ge(xgt_hi, count)
                V.tensor_tensor(xgT[1][:], ps_f[:, 0:H].rearrange("p (k c) -> p k c", k=KC),
                                xgT[0][:].bitcast(F32), ALU.subtract).then_inc(xgt_lo, 1)

            slot_weights(slice(H, H + 1), 1)
            rows_lo_parts(1)

            def step2(i, b, more, last):
                n = b + 1

                def transposed(h):
                    dve.wait_ge(sb_full, after(i, 4, 2 * b + h + 1))
                    dve.wait_ge(sc_done, after(i, 2, b))
                    V.tensor_scalar(pmT[:, b, h * 512:(h + 1) * 512], ps_b, iota_p[:, 0:1], None, ALU.is_equal)\
                        .then_inc(pmt_ready, 1)

                transposed(0)
                dve.wait_ge(tanh2_done, after(i, 2, n))
                V.scalar_tensor_tensor(gs2[:], tt2[:], 1.0, ps_f[:, 0:ID], ALU.add, ALU.mult).then_inc(gs2_done, 1)
                dve.wait_ge(gs2_done, after(i, 2, n))
                dve.wait_ge(wsc_ready, i * 2 + n)
                dve.wait_ge(mt_full, after(i, 2, b))
                V.scalar_tensor_tensor(mid[:], gs2[:], wsc[:, 0:1], ps_f[:, ID:2 * ID], ALU.mult, ALU.mult)\
                    .then_inc(mid_ready, 1)
                if more:
                    dve.wait_ge(g_full, i * 2 + n)
                    slot_matrix(i * 2 + (b + 2), b)
                if not last:
                    dve.wait_ge(mid_ready, after(i, 2, n))
                    slot_weights(bass.ds(i * 2 + (H + b + 1), 1), i * 2 + (n + 1))
                dve.wait_ge(mt_hi, after(i, 2, n))
                V.tensor_tensor(midT[1][:], ps_x[0:IC, 0:2 * CAP].rearrange("p (c t) -> p c t", c=2),
                                midT[0][:].bitcast(F32), ALU.subtract).then_inc(mt_lo, 1)
                if not last:
                    rows_lo_parts(i * 2 + (n + 1))
                transposed(1)
                cols = bass.ds(i * P, P)
                V.reciprocal(den[:, b, cols], den[:, b, cols]).then_inc(rden_done, 1)
                dve.wait_ge(eo_hi, after(i, 2, n))
                V.tensor_tensor(eo[1][:], ps_g[:, 0:H], eo[0][:].bitcast(F32), ALU.subtract).then_inc(eo_lo, 1)
                dve.wait_ge(rden_done, i * 2 + n)
                V.tensor_tensor(av[:, b, cols], ek[:, b, cols], den[:, b, cols], ALU.mult).then_inc(rw_ready, 1)

            with dve.Fori(0, EXPERTS // 2 - 1) as i:
                step2(i, 0, True, False)
                step2(i, 1, True, False)
            step2(EXPERTS // 2 - 1, 0, False, False)
            step2(EXPERTS // 2 - 1, 1, False, True)
            for q in range(4):
                dve.wait_ge(y_done, q + 1)
                V.tensor_tensor(acc[:, 2 * q:2 * q + 2, :], acc[:, 2 * q:2 * q + 2, :], y[:, 2 * q:2 * q + 2, :],
                                ALU.add).then_inc(out_ready, 1)


_INS = ['L0_attn_hidden_states', 'L0_attn_Wq', 'L0_attn_Wk', 'L0_attn_Wv', 'L0_attn_Wo', 'L0_ffn_router_weight',
        'L0_ffn_router_bias', 'L0_ffn_gate_up_proj', 'L0_ffn_gate_up_proj_bias', 'L0_ffn_down_proj',
        'L0_ffn_down_proj_bias']
_L1 = ['L1_attn_Wk', 'L1_attn_Wv', 'L1_attn_Wr', 'L1_attn_time_decay', 'L1_ffn_gate_w', 'L1_ffn_w_gate',
       'L1_ffn_w_up', 'L1_ffn_w_down', 'L1_ffn_sw_gate', 'L1_ffn_sw_up', 'L1_ffn_sw_down']


def kernel(**inputs):
    import numpy as np
    import concourse.bacc as bacc
    from concourse.bass_utils import run_bass_kernel_spmd as run

    nc = bacc.Bacc("TRN2", target_bir_lowering=False, num_devices=1)
    arrays, aps = {}, {}
    for name in _INS + _L1:
        a = np.ascontiguousarray(inputs[name])
        arrays[f"in_{name}"] = a
        aps[name] = nc.dram_tensor(f"in_{name}", a.shape, mybir.dt.from_np(a.dtype), kind="ExternalInput").ap()
    out = nc.dram_tensor("out_x", (1, T, H), F32, kind="ExternalOutput").ap()
    build(nc, aps[_INS[0]][0], *[aps[n] for n in _INS[1:]], {n.split('_', 2)[2]: aps[n] for n in _L1}, out[0])
    r = run(nc, [arrays], core_ids=[0])
    return r.results[0]["out_x"]
```
